# Optimizing a Trainium2 kernel written in Bass

```python
import numpy as np
import jax
import jax.numpy as jnp

def _softmax(x, axis=-1):
    return jax.nn.softmax(x, axis=axis)

def _gelu(x):
    return jax.nn.gelu(x, approximate=True)

def _silu(x):
    return jax.nn.silu(x)

def _sigmoid(x):
    return jax.nn.sigmoid(x)

def _layernorm(x, axis=-1, eps=1e-05):
    m = jnp.mean(x, axis=axis, keepdims=True)
    v = jnp.var(x, axis=axis, keepdims=True)
    return (x - m) / jnp.sqrt(v + eps)

def _scatter_add(tgt, idx, src, axis=0):
    return tgt.at[idx].add(src)

def _segment_sum(src, seg, n):
    return jax.ops.segment_sum(src, seg, n)
kernel_name = 'mk_prb_d1_jaxref_r4_2c641e'

def setup_inputs(seed: int=0):
    np.random.seed(seed)
    _w = jnp.asarray

    def _L0_attn_setup():
        import jax, jax.numpy as jnp
        import numpy as np
        D_MODEL = 256
        N_HEADS = 16
        D_K = D_MODEL // N_HEADS
        BASE = 10000.0

        def _rope(x):
            S = x.shape[1]
            freqs = BASE ** (-(jnp.arange(0, D_K, 2, dtype=jnp.float32) / D_MODEL))
            angles = jnp.arange(S, dtype=jnp.float32)[:, None] * freqs[None, :]
            cos = jnp.cos(angles)[None, :, None, :]
            sin = jnp.sin(angles)[None, :, None, :]
            xe, xo = (x[..., 0::2], x[..., 1::2])
            x1 = xe * cos - xo * sin
            x2 = xe * sin + xo * cos
            return jnp.stack([x1, x2], axis=-1).reshape(x.shape)
        key = jax.random.key(seed)
        ks = jax.random.split(key, 7)
        B, S = (4, 1024)
        scale = 1.0 / np.sqrt(D_MODEL)
        return {'x': jax.random.normal(ks[0], (B, S, D_MODEL), jnp.float32), 'Wq': jax.random.normal(ks[1], (D_MODEL, D_MODEL), jnp.float32) * scale, 'bq': jnp.zeros((D_MODEL,), jnp.float32), 'Wk': jax.random.normal(ks[2], (D_MODEL, D_MODEL), jnp.float32) * scale, 'bk': jnp.zeros((D_MODEL,), jnp.float32), 'Wv': jax.random.normal(ks[3], (D_MODEL, D_MODEL), jnp.float32) * scale, 'bv': jnp.zeros((D_MODEL,), jnp.float32)}
    _L0_attn_in = _L0_attn_setup()

    def _L0_ffn_setup():
        import jax, jax.numpy as jnp
        import numpy as np
        EMB = 256
        HEADS = 16
        SEQ = 512
        LATENT = 128
        N_EXP = 8
        TOP_K = 2
        EXP_DIM = 512
        BATCH = 2
        EPS = 1e-06

        def _rmsnorm(x, g):
            return x * jax.lax.rsqrt(jnp.mean(x * x, axis=-1, keepdims=True) + EPS) * g

        def _mla(h, Wq, Wdkv, Wuk, Wuv, Wo):
            B, S, D = h.shape
            hd = D // HEADS
            q = (h @ Wq).reshape(B, S, HEADS, hd)
            c = h @ Wdkv
            k = (c @ Wuk).reshape(B, S, HEADS, hd)
            v = (c @ Wuv).reshape(B, S, HEADS, hd)
            scores = jnp.einsum('bqhd,bkhd->bhqk', q, k) / jnp.sqrt(jnp.asarray(hd, h.dtype))
            causal = jnp.tril(jnp.ones((S, S), bool))
            scores = jnp.where(causal, scores, jnp.asarray(-1000000000.0, h.dtype))
            a = jax.nn.softmax(scores, axis=-1)
            out = jnp.einsum('bhqk,bkhd->bqhd', a, v).reshape(B, S, D)
            return out @ Wo

        def _moe(h, gate_w, w1, w2):
            B, S, D = h.shape
            t = h.reshape(B * S, D)
            logits = t @ gate_w
            top_v, top_i = jax.lax.top_k(logits, TOP_K)
            gates = jax.nn.softmax(top_v, axis=-1)
            T = t.shape[0]
            combine = jnp.zeros((T, N_EXP), t.dtype).at[jnp.arange(T)[:, None], top_i].add(gates)
            hid = jax.nn.silu(jnp.einsum('td,edh->teh', t, w1))
            ye = jnp.einsum('teh,ehd->ted', hid, w2)
            out = jnp.einsum('te,ted->td', combine, ye)
            return out.reshape(B, S, D)
        key = jax.random.key(seed)
        ks = jax.random.split(key, 12)
        s = 0.02
        return {'x': jax.random.normal(ks[0], (BATCH, SEQ, EMB), jnp.float32), 'g1': jnp.ones((EMB,), jnp.float32), 'Wq': jax.random.normal(ks[1], (EMB, EMB), jnp.float32) * s, 'Wdkv': jax.random.normal(ks[2], (EMB, LATENT), jnp.float32) * s, 'Wuk': jax.random.normal(ks[3], (LATENT, EMB), jnp.float32) * s, 'Wuv': jax.random.normal(ks[4], (LATENT, EMB), jnp.float32) * s, 'Wo': jax.random.normal(ks[5], (EMB, EMB), jnp.float32) * s, 'g2': jnp.ones((EMB,), jnp.float32), 'gate_w': jax.random.normal(ks[6], (EMB, N_EXP), jnp.float32) * s, 'w1': jax.random.normal(ks[7], (N_EXP, EMB, EXP_DIM), jnp.float32) * s, 'w2': jax.random.normal(ks[8], (N_EXP, EXP_DIM, EMB), jnp.float32) * s}
    _L0_ffn_in = _L0_ffn_setup()
    _d = {'L0_attn_x': _L0_attn_in['x'], 'L0_attn_Wq': _L0_attn_in['Wq'], 'L0_attn_bq': _L0_attn_in['bq'], 'L0_attn_Wk': _L0_attn_in['Wk'], 'L0_attn_bk': _L0_attn_in['bk'], 'L0_attn_Wv': _L0_attn_in['Wv'], 'L0_attn_bv': _L0_attn_in['bv'], 'L0_ffn_g1': _L0_ffn_in['g1'], 'L0_ffn_Wq': _L0_ffn_in['Wq'], 'L0_ffn_Wdkv': _L0_ffn_in['Wdkv'], 'L0_ffn_Wuk': _L0_ffn_in['Wuk'], 'L0_ffn_Wuv': _L0_ffn_in['Wuv'], 'L0_ffn_Wo': _L0_ffn_in['Wo'], 'L0_ffn_g2': _L0_ffn_in['g2'], 'L0_ffn_gate_w': _L0_ffn_in['gate_w'], 'L0_ffn_w1': _L0_ffn_in['w1'], 'L0_ffn_w2': _L0_ffn_in['w2']}
    _x0 = _d['L0_attn_x']
    _d['L0_attn_x'] = jax.random.normal(jax.random.fold_in(jax.random.key(seed), 1), (4, 2048, 256), dtype=_x0.dtype)
    del _x0
    return _d

def reference(L0_attn_x, L0_attn_Wq, L0_attn_bq, L0_attn_Wk, L0_attn_bk, L0_attn_Wv, L0_attn_bv, L0_ffn_g1, L0_ffn_Wq, L0_ffn_Wdkv, L0_ffn_Wuk, L0_ffn_Wuv, L0_ffn_Wo, L0_ffn_g2, L0_ffn_gate_w, L0_ffn_w1, L0_ffn_w2):

    def _L0_attn_ref(x, Wq, bq, Wk, bk, Wv, bv):
        import jax, jax.numpy as jnp
        import numpy as np
        D_MODEL = 256
        N_HEADS = 16
        D_K = D_MODEL // N_HEADS
        BASE = 10000.0

        def _rope(x):
            S = x.shape[1]
            freqs = BASE ** (-(jnp.arange(0, D_K, 2, dtype=jnp.float32) / D_MODEL))
            angles = jnp.arange(S, dtype=jnp.float32)[:, None] * freqs[None, :]
            cos = jnp.cos(angles)[None, :, None, :]
            sin = jnp.sin(angles)[None, :, None, :]
            xe, xo = (x[..., 0::2], x[..., 1::2])
            x1 = xe * cos - xo * sin
            x2 = xe * sin + xo * cos
            return jnp.stack([x1, x2], axis=-1).reshape(x.shape)
        B, S, D = x.shape
        Q = (x @ Wq + bq).reshape(B, S, N_HEADS, D_K)
        K = (x @ Wk + bk).reshape(B, S, N_HEADS, D_K)
        V = (x @ Wv + bv).reshape(B, S, N_HEADS, D_K)
        Q = _rope(Q)
        K = _rope(K)
        score = jnp.einsum('bsid,bsjd->bsij', Q, K) / jnp.sqrt(jnp.float32(D_K))
        attn = jax.nn.softmax(score, axis=-1)
        out = jnp.einsum('bsij,bsjd->bsid', attn, V)
        return out.reshape(B, S, D)

    def _L0_ffn_ref(x, g1, Wq, Wdkv, Wuk, Wuv, Wo, g2, gate_w, w1, w2):
        import jax, jax.numpy as jnp
        import numpy as np
        EMB = 256
        HEADS = 16
        SEQ = 512
        LATENT = 128
        N_EXP = 8
        TOP_K = 2
        EXP_DIM = 512
        BATCH = 2
        EPS = 1e-06

        def _rmsnorm(x, g):
            return x * jax.lax.rsqrt(jnp.mean(x * x, axis=-1, keepdims=True) + EPS) * g

        def _mla(h, Wq, Wdkv, Wuk, Wuv, Wo):
            B, S, D = h.shape
            hd = D // HEADS
            q = (h @ Wq).reshape(B, S, HEADS, hd)
            c = h @ Wdkv
            k = (c @ Wuk).reshape(B, S, HEADS, hd)
            v = (c @ Wuv).reshape(B, S, HEADS, hd)
            scores = jnp.einsum('bqhd,bkhd->bhqk', q, k) / jnp.sqrt(jnp.asarray(hd, h.dtype))
            causal = jnp.tril(jnp.ones((S, S), bool))
            scores = jnp.where(causal, scores, jnp.asarray(-1000000000.0, h.dtype))
            a = jax.nn.softmax(scores, axis=-1)
            out = jnp.einsum('bhqk,bkhd->bqhd', a, v).reshape(B, S, D)
            return out @ Wo

        def _moe(h, gate_w, w1, w2):
            B, S, D = h.shape
            t = h.reshape(B * S, D)
            logits = t @ gate_w
            top_v, top_i = jax.lax.top_k(logits, TOP_K)
            gates = jax.nn.softmax(top_v, axis=-1)
            T = t.shape[0]
            combine = jnp.zeros((T, N_EXP), t.dtype).at[jnp.arange(T)[:, None], top_i].add(gates)
            hid = jax.nn.silu(jnp.einsum('td,edh->teh', t, w1))
            ye = jnp.einsum('teh,ehd->ted', hid, w2)
            out = jnp.einsum('te,ted->td', combine, ye)
            return out.reshape(B, S, D)
        x = x + _mla(_rmsnorm(x, g1), Wq, Wdkv, Wuk, Wuv, Wo)
        x = x + _moe(_rmsnorm(x, g2), gate_w, w1, w2)
        return x
    x = L0_attn_x
    xn = _layernorm(x, axis=-1)
    x = x + _L0_attn_ref(xn, L0_attn_Wq, L0_attn_bq, L0_attn_Wk, L0_attn_bk, L0_attn_Wv, L0_attn_bv) + _L0_ffn_ref(xn, L0_ffn_g1, L0_ffn_Wq, L0_ffn_Wdkv, L0_ffn_Wuk, L0_ffn_Wuv, L0_ffn_Wo, L0_ffn_g2, L0_ffn_gate_w, L0_ffn_w1, L0_ffn_w2)
    return x

_drawn_inputs = setup_inputs


def setup_inputs(seed=0):
    import zlib

    import numpy as np

    out = dict(_drawn_inputs(seed))
    spreads = {'L0_attn_bq': (0.0, 2.0),
     'L0_attn_bk': (0.0, 2.0),
     'L0_attn_bv': (0.0, 2.0),
     'L0_ffn_g1': (1.0, 0.6),
     'L0_ffn_g2': (1.0, 0.6)}
    factors = {'L0_ffn_Wq': 8.0,
     'L0_ffn_Wdkv': 8.0,
     'L0_ffn_Wuk': 8.0,
     'L0_ffn_Wuv': 8.0,
     'L0_ffn_Wo': 8.0,
     'L0_attn_Wq': 2.96,
     'L0_attn_Wk': 2.903,
     'L0_ffn_gate_w': 8.0,
     'L0_ffn_w1': 8.0,
     'L0_ffn_w2': 8.0}
    for name, (base, spread) in spreads.items():
        noise = np.random.default_rng([zlib.crc32(name.encode()), seed]).standard_normal(out[name].shape)
        drawn = base * np.exp(spread * noise) if base else spread * noise
        out[name] = jnp.asarray(drawn.astype(out[name].dtype))
    for name, factor in factors.items():
        out[name] = (out[name] * factor).astype(out[name].dtype)
    return out
```

```python
from contextlib import ExitStack

import concourse.bass as bass
from concourse import mybir

F32 = mybir.dt.float32
BF16 = mybir.dt.bfloat16
U32 = mybir.dt.uint32
ALU = mybir.AluOpType
ACT = mybir.ActivationFunctionType
AX_X = mybir.AxisListType.X

P = 128
B, S, D = 4, 2048, 256
T = B * S
H, DH = 16, 16
L = 128
E, F = 8, 512
KD = D // P
CT = 512
TT = CT // P
NC = S // CT
HG = 4
NG = H // HG
VW = 32
EPS_LN, EPS_RMS = 1e-5, 1e-6
BIG = 1e30
Q_PART = (0, 0, 1, 1, 0, 2)
K_PART = (0, 1, 0, 1, 2, 0)
SPLIT = DH * len(Q_PART)
ROWS = SPLIT + 2
UNITS_16 = 16


def wait_apart(eng, sem, value, apart):
    eng.wait_ge(sem, value)
    eng.sem_inc(apart, 1)


def phase1_project(nc, x_v, w, xn_v, qk_parts, v_dram):
    with ExitStack() as ctx:
        sb = lambda name, shape, dt=F32: ctx.enter_context(nc.sbuf_tensor(name, shape, dt))
        sem = lambda name: ctx.enter_context(nc.semaphore(name))
        bank = lambda name: ctx.enter_context(nc.psum_tensor(name, [P, CT], F32))

        ident = sb("p1_ident", [P, P])
        wq = sb("p1_wq", [P, KD, D])
        wdkv = sb("p1_wdkv", [P, KD, L])
        wuk = sb("p1_wuk", [P, D])
        wuv = sb("p1_wuv", [P, D])
        g1 = sb("p1_g1", [P, KD])
        half = sb("p1_minus_half", [P, TT])
        x = sb("p1_x", [P, 2, TT, D])
        xn = sb("p1_xn", [P, 2, TT, D])
        h = sb("p1_h", [P, TT, D])
        hT = sb("p1_hT", [P, KD, CT])
        cT = sb("p1_cT", [P, CT])
        stats = sb("p1_stats", [P, TT, 6])
        mv = sb("p1_mv", [P, TT, 2])
        rstd = sb("p1_rstd", [P, TT])
        sq = sb("p1_sq", [P, TT, D])
        ss = sb("p1_ss", [P, TT])
        rrms = sb("p1_rrms", [P, TT])
        parts = sb("p1_parts", [P, 2, 4, 3, CT], BF16)
        rest = sb("p1_rest", [P, 4, CT])
        vx = sb("p1_vx", [P, 2, TT, H, VW])

        t_ps = [bank(f"p1_t{k}") for k in range(KD)]
        qk_ps = [bank(f"p1_qk{j}") for j in range(4)]
        c_ps = bank("p1_c")
        v_ps = bank("p1_v")

        w_loaded = sem("p1_w_loaded")
        consts = sem("p1_consts")
        w_scaled = sem("p1_w_scaled")
        x_loaded = [sem(f"p1_x_loaded{s}") for s in range(2)]
        stats_done = sem("p1_stats_done")
        mv_done = sem("p1_mv_done")
        eps_added = sem("p1_eps_added")
        rstd_done = sem("p1_rstd_done")
        xn_done = sem("p1_xn_done")
        ss_done = sem("p1_ss_done")
        mean_done = sem("p1_mean_done")
        rrms_done = sem("p1_rrms_done")
        h_done = sem("p1_h_done")
        t_done = sem("p1_t_done")
        hT_done = sem("p1_hT_done")
        qk_done = sem("p1_qk_done")
        part0_done = sem("p1_part0_done")
        rest_done = sem("p1_rest_done")
        part1_done = sem("p1_part1_done")
        part2_done = sem("p1_part2_done")
        c_done = sem("p1_c_done")
        cT_done = sem("p1_cT_done")
        v_done = sem("p1_v_done")
        vx_done = sem("p1_vx_done")
        xn_stored = [sem(f"p1_xn_stored{s}") for s in range(2)]
        parts_stored = [sem(f"p1_parts_stored{s}") for s in range(2)]
        vx_stored = [sem(f"p1_vx_stored{s}") for s in range(2)]
        apart = sem("p1_apart")
        block = ctx.enter_context(nc.Block())
        N_W = 6

        def chunks(eng, body):
            with eng.Fori(0, B - 1) as b:
                for c in range(NC):
                    body(b, c, NC * b + c, True)
            for c in range(NC):
                body(B - 1, c, NC * (B - 1) + c, c < NC - 1)

        def uses(b, c):
            return (NC // 2) * b + c // 2

        @block.sync
        def _(sp):
            sp.dma_start(wq[:, :, :], w["ffn_Wq"].rearrange("(k p) n -> p k n", p=P)).then_inc(w_loaded, 16)
            sp.dma_start(wdkv[:, :, :], w["ffn_Wdkv"].rearrange("(k p) n -> p k n", p=P)).then_inc(w_loaded, 16)
            sp.dma_start(wuk[:, :], w["ffn_Wuk"]).then_inc(w_loaded, 16)
            sp.dma_start(wuv[:, :], w["ffn_Wuv"]).then_inc(w_loaded, 16)
            with nc.allow_non_contiguous_dma(reason="256 gains, once"):
                sp.dma_start(g1[:, :], w["ffn_g1"].rearrange("(k p) -> p k", p=P)).then_inc(w_loaded, 16)
            sp.dma_start(x[:, 0, :, :], x_v[0, 0]).then_inc(x_loaded[0], 16)

            def body(b, c, n, follows):
                s, s1 = c % 2, (c + 1) % 2
                if follows:
                    b1, c1 = (b, c + 1) if c + 1 < NC else (b + 1, 0)
                    wait_apart(sp, xn_done, n, apart)
                    sp.dma_start(x[:, s1, :, :], x_v[b1, c1]).then_inc(x_loaded[s1], 16)
                wait_apart(sp, xn_done, n + 1, apart)
                sp.dma_start(xn_v[b, c], xn[:, s, :, :]).then_inc(xn_stored[s], 16)
                for j in range(4):
                    wait_apart(sp, part2_done, 4 * n + j + 1, apart)
                    sp.dma_start(qk_parts[j // 2, :, b, (j % 2) * P:(j % 2 + 1) * P, c * CT:(c + 1) * CT]
                                 .rearrange("a p t -> p a t"), parts[:, s, j, :, :]).then_inc(parts_stored[s], 16)
                wait_apart(sp, vx_done, 2 * n + 2, apart)
                for g in range(NG):
                    sp.dma_start(v_dram[b, g, c * CT:(c + 1) * CT, :].rearrange("(t p) v -> p t v", p=P),
                                 vx[:, s, :, g * HG:(g + 1) * HG, :].rearrange("p t h v -> p t (h v)")
                                 ).then_inc(vx_stored[s], 16)
            chunks(sp, body)
            for s in range(2):
                wait_apart(sp, xn_stored[s], 16 * B * NC // 2, apart)
                wait_apart(sp, parts_stored[s], 16 * 4 * B * NC // 2, apart)
                wait_apart(sp, vx_stored[s], 16 * NG * B * NC // 2, apart)

        @block.gpsimd
        def _(pool):
            nc.gpsimd.memset(ident[:, :], 0.0).then_inc(consts, 1)
            nc.gpsimd.memset(half[:, :], -0.5).then_inc(consts, 1)
            nc.gpsimd.memset(vx[:, :, :, :, :], 0.0).then_inc(consts, 1)
            wait_apart(pool, consts, 3, apart)
            nc.gpsimd.affine_select(out=ident[:, :], in_=ident[:, :], compare_op=ALU.not_equal, fill=1.0,
                                    base=0, pattern=[[-1, P]], channel_multiplier=1).then_inc(consts, 1)
            nc.gpsimd.memset(vx[:, :, :, :, DH:DH + 1], 1.0).then_inc(consts, 1)

            def inverse_std(n):
                wait_apart(pool, mv_done, n + 1, apart)
                nc.gpsimd.tensor_scalar(rstd[:, :], mv[:, :, 1], EPS_LN, None, ALU.add).then_inc(eps_added, 1)
                wait_apart(pool, eps_added, n + 1, apart)
                nc.gpsimd.tensor_tensor(rstd[:, :], rstd[:, :], half[:, :], ALU.pow).then_inc(rstd_done, 1)

            def inverse_rms(n):
                wait_apart(pool, ss_done, n + 1, apart)
                nc.gpsimd.tensor_scalar(rrms[:, :], ss[:, :], 1.0 / D, EPS_RMS, ALU.mult, ALU.add).then_inc(mean_done, 1)
                wait_apart(pool, mean_done, n + 1, apart)
                nc.gpsimd.tensor_tensor(rrms[:, :], rrms[:, :], half[:, :], ALU.pow).then_inc(rrms_done, 1)

            def lower_parts(n, s, j):
                wait_apart(pool, rest_done, 4 * n + j + 1, apart)
                nc.gpsimd.tensor_copy(parts[:, s, j, 1, :], rest[:, j, :]).then_inc(part1_done, 1)
                wait_apart(pool, part1_done, 4 * n + j + 1, apart)
                nc.gpsimd.tensor_tensor(parts[:, s, j, 2, :], rest[:, j, :], parts[:, s, j, 1, :],
                                        ALU.subtract).then_inc(part2_done, 1)

            inverse_std(0)
            inverse_rms(0)

            def body(b, c, n, follows):
                if follows:
                    inverse_std(n + 1)
                lower_parts(n, c % 2, 0)
                lower_parts(n, c % 2, 1)
                if follows:
                    inverse_rms(n + 1)
                lower_parts(n, c % 2, 2)
                lower_parts(n, c % 2, 3)
            chunks(pool, body)

        @block.vector
        def _(dve):
            dve.wait_ge(w_loaded, 16 * 5)
            for k in range(KD):
                nc.vector.tensor_scalar(wq[:, k, :], wq[:, k, :], g1[:, k:k + 1], DH ** -0.5, ALU.mult, ALU.mult)
                last = nc.vector.tensor_scalar(wdkv[:, k, :], wdkv[:, k, :], g1[:, k:k + 1], None, ALU.mult)
            last.then_inc(w_scaled, 1)

            def moments(n, s, u):
                dve.wait_ge(x_loaded[s], 16 * (u + 1))
                for t in range(TT):
                    last = nc.vector.bn_stats(stats[:, t, :], x[:, s, t, :])
                last.then_inc(stats_done, 1)
                wait_apart(dve, stats_done, n + 1, apart)
                for t in range(TT):
                    last = nc.vector.bn_aggr(mv[:, t, :], stats[:, t, :])
                last.then_inc(mv_done, 1)

            def normalise(n, s, u):
                dve.wait_ge(rstd_done, n + 1)
                dve.wait_ge(xn_stored[s], 16 * u)
                for t in range(TT):
                    last = nc.vector.tensor_scalar(xn[:, s, t, :], x[:, s, t, :], mv[:, t, 0:1], rstd[:, t:t + 1],
                                                   ALU.subtract, ALU.mult)
                last.then_inc(xn_done, 1)

            def scale_rms(n, s):
                dve.wait_ge(rrms_done, n + 1)
                dve.wait_ge(t_done, KD * n)
                for t in range(TT):
                    last = nc.vector.tensor_scalar(h[:, t, :], xn[:, s, t, :], rrms[:, t:t + 1], None, ALU.mult)
                last.then_inc(h_done, 1)

            def subtract_part0(n, s, j):
                dve.wait_ge(part0_done, 4 * n + j + 1)
                dve.wait_ge(part2_done, 4 * n)
                nc.vector.tensor_tensor(rest[:, j, :], qk_ps[j][:, :], parts[:, s, j, 0, :],
                                        ALU.subtract).then_inc(rest_done, 1)

            moments(0, 0, 0)
            normalise(0, 0, 0)
            scale_rms(0, 0)

            def body(b, c, n, follows):
                s, s1 = c % 2, (c + 1) % 2
                u1 = uses(b, c + 1)
                if follows:
                    moments(n + 1, s1, u1)
                subtract_part0(n, s, 0)
                subtract_part0(n, s, 1)
                if follows:
                    normalise(n + 1, s1, u1)
                subtract_part0(n, s, 2)
                subtract_part0(n, s, 3)
                if follows:
                    scale_rms(n + 1, s1)
            chunks(dve, body)

        @block.scalar
        def _(act):
            def squares(n, s):
                act.wait_ge(xn_done, n + 1)
                act.wait_ge(mean_done, n)
                for t in range(TT):
                    last = nc.scalar.activation(sq[:, t, :], xn[:, s, t, :], ACT.Square, accum_out=ss[:, t:t + 1])
                last.then_inc(ss_done, 1)

            def part0(b, c, n, s, j):
                act.wait_ge(qk_done, 4 * n + j + 1)
                act.wait_ge(parts_stored[s], 64 * uses(b, c))
                nc.scalar.copy(parts[:, s, j, 0, :], qk_ps[j][:, :]).then_inc(part0_done, 1)

            act.wait_ge(consts, 5)
            squares(0, 0)

            def body(b, c, n, follows):
                s = c % 2
                for k in range(KD):
                    act.wait_ge(t_done, KD * n + k + 1)
                    act.wait_ge(c_done, n)
                    nc.scalar.copy(hT[:, k, :], t_ps[k][:, :]).then_inc(hT_done, 1)
                part0(b, c, n, s, 0)
                part0(b, c, n, s, 1)
                act.wait_ge(c_done, n + 1)
                act.wait_ge(v_done, 2 * n)
                nc.scalar.copy(cT[:, :], c_ps[:, :]).then_inc(cT_done, 1)
                if follows:
                    squares(n + 1, (c + 1) % 2)
                part0(b, c, n, s, 2)
                part0(b, c, n, s, 3)
                act.wait_ge(vx_stored[s], 16 * NG * uses(b, c))
                for i in range(2):
                    act.wait_ge(v_done, 2 * n + i + 1)
                    nc.scalar.copy(vx[:, s, 2 * i:2 * i + 2, :, 0:DH],
                                   v_ps[:, :].rearrange("p (t h d) -> p t h d", t=2, h=H)).then_inc(vx_done, 1)
            chunks(act, body)

        @block.tensor
        def _(pe):
            pe.wait_ge(w_scaled, 1)
            pe.wait_ge(consts, 5)

            def body(b, c, n, follows):
                pe.wait_ge(h_done, n + 1)
                pe.wait_ge(hT_done, KD * n)
                for k in range(KD):
                    for t in range(TT):
                        last = nc.tensor.transpose(t_ps[k][:, t * P:(t + 1) * P], h[:, t, k * P:(k + 1) * P], ident[:, :])
                    last.then_inc(t_done, 1)
                pe.wait_ge(hT_done, KD * n + KD)
                pe.wait_ge(rest_done, 4 * n)
                for m in range(2):
                    for k in range(KD):
                        last = nc.tensor.matmul(qk_ps[m][:, :], wq[:, k, m * P:(m + 1) * P], hT[:, k, :],
                                                start=k == 0, stop=k == KD - 1)
                    last.then_inc(qk_done, 1)
                pe.wait_ge(cT_done, n)
                for k in range(KD):
                    last = nc.tensor.matmul(c_ps[:, :], wdkv[:, k, :], hT[:, k, :], start=k == 0, stop=k == KD - 1)
                last.then_inc(c_done, 1)
                pe.wait_ge(cT_done, n + 1)
                for m in range(2):
                    nc.tensor.matmul(qk_ps[2 + m][:, :], wuk[:, m * P:(m + 1) * P], cT[:, :],
                                     start=True, stop=True).then_inc(qk_done, 1)
                for i in range(2):
                    pe.wait_ge(vx_done, 2 * n + i)
                    for t in range(2):
                        tok = (2 * i + t) * P
                        last = nc.tensor.matmul(v_ps[:, t * D:(t + 1) * D], cT[:, tok:tok + P], wuv[:, :],
                                                start=True, stop=True)
                    last.then_inc(v_done, 1)
            chunks(pe, body)


def phase2_attend(nc, qk_heads, v_dram, o_dram):
    UNITS = B * NG
    KT = S // P
    STEPS = [(c, kt) for c in range(NC) for kt in range(TT * (c + 1))]
    N_STEP = len(STEPS)
    LAST = [max(i for i, (c, _) in enumerate(STEPS) if c == cc) for cc in range(NC)]
    PIECES = [(hh, i, pc, min(CT, (i + 1) * P - pc * CT))
              for hh in range(HG) for i in range(KT) for pc in range(i // TT + 1)]
    N_PIECE = len(PIECES)
    SLOTS = 3

    with ExitStack() as ctx:
        sb = lambda name, shape, dt=F32: ctx.enter_context(nc.sbuf_tensor(name, shape, dt))
        sem = lambda name: ctx.enter_context(nc.semaphore(name))

        ident = sb("p2_ident", [P, P])
        ident_b = sb("p2_ident_b", [P, P], BF16)
        mask_q = sb("p2_mask_q", [P, P], BF16)
        mask_k = sb("p2_mask_k", [P, P], BF16)
        q6 = [sb(f"p2_q6_{s}", [ROWS, HG, S], BF16) for s in range(SLOTS)]
        k6 = [sb(f"p2_k6_{s}", [ROWS, HG, S], BF16) for s in range(SLOTS)]
        vg = [sb(f"p2_vg_{s}", [P, KT, HG * VW]) for s in range(SLOTS)]
        probs = sb("p2_probs", [P, 4, 2, CT])
        piece_max = sb("p2_piece_max", [P, HG * KT, NC])
        neg_max = sb("p2_neg_max", [P, P])
        neg_hi = sb("p2_neg_hi", [HG * KT, P], BF16)
        neg_lo = sb("p2_neg_lo", [HG * KT, P], BF16)
        pv_sb = sb("p2_pv_sb", [P, CT])
        inv = sb("p2_inv", [P, TT * HG])
        o_sb = sb("p2_o", [P, 2, TT, HG * DH])

        row_ps = [ctx.enter_context(nc.psum_tensor(f"p2_row{i}", [P, CT], F32)) for i in range(2)]
        st_ps = [ctx.enter_context(nc.psum_tensor(f"p2_st{i}", [P, 2, CT], F32)) for i in range(2)]
        pv_ps = ctx.enter_context(nc.psum_tensor("p2_pv", [P, CT], F32))
        tr_ps = ctx.enter_context(nc.psum_tensor("p2_tr", [P, CT], F32))

        consts = sem("p2_consts")
        loaded = [sem(f"p2_loaded{s}") for s in range(SLOTS)]
        row_scored = sem("p2_row_scored")
        row_free = sem("p2_row_free")
        neg_max_done = sem("p2_neg_max_done")
        neg_hi_done = sem("p2_neg_hi_done")
        neg_rows_done = sem("p2_neg_rows_done")
        neg_stored = sem("p2_neg_stored")
        st_scored = sem("p2_st_scored")
        probs_done = sem("p2_probs_done")
        pv_done = sem("p2_pv_done")
        pv_copied = sem("p2_pv_copied")
        tr_done = sem("p2_tr_done")
        inv_done = sem("p2_inv_done")
        tr_free = sem("p2_tr_free")
        o_stored = [sem(f"p2_o_stored{s}") for s in range(2)]
        apart = sem("p2_apart")
        block = ctx.enter_context(nc.Block())

        N_LOAD = 16 * (2 * len(Q_PART) + 2)

        def turns(n):
            return 1 + (NC + 1) * n

        def units(eng, body):
            with eng.Fori(0, (UNITS - 1) // SLOTS) as j:
                for s in range(SLOTS):
                    body(SLOTS * j + s, s, True, j)
            body(UNITS - 1, (UNITS - 1) % SLOTS, False, (UNITS - 1) // SLOTS)

        def next_round(j, s):
            return j + (s + 1) // SLOTS

        def load(sp, n, s):
            for g, (a, k) in enumerate(zip(Q_PART, K_PART)):
                sp.dma_start(q6[s][g * DH:(g + 1) * DH, :, :],
                             qk_heads[0, a, bass.ds(n * HG, HG), :, :].rearrange("h d t -> d h t")).then_inc(loaded[s], 16)
                sp.dma_start(k6[s][g * DH:(g + 1) * DH, :, :],
                             qk_heads[1, k, bass.ds(n * HG, HG), :, :].rearrange("h d t -> d h t")).then_inc(loaded[s], 16)
            for i in range(2):
                half = slice(i * S // 2, (i + 1) * S // 2)
                sp.dma_start(vg[s][:, i * KT // 2:(i + 1) * KT // 2, :],
                             v_dram[bass.ds(n, 1), half, :].rearrange("a (k p) v -> p (a k) v", p=P)).then_inc(loaded[s], 16)

        @block.sync
        def _(sp):
            def store_neg_rows(n, s):
                wait_apart(sp, neg_rows_done, n + 1, apart)
                for r, part in enumerate((neg_hi, neg_lo)):
                    sp.dma_start(q6[s][SPLIT + r:SPLIT + r + 1, :, :].rearrange("a h (i p) -> a (h i) p", p=P),
                                 part[:, :]).then_inc(neg_stored, 16)

            def store_o(n, c, turn):
                wait_apart(sp, tr_free, 1 + turn + 1, apart)
                sp.dma_start(o_dram[bass.ds(n, 1), c * CT:(c + 1) * CT, :].rearrange("a (t p) d -> p (a t) d", p=P),
                             o_sb[:, c % 2, :, :]).then_inc(o_stored[c % 2], 16)

            load(sp, 0, 0)
            load(sp, 1, 1)
            store_neg_rows(0, 0)

            def body(n, s, loads, has_next):
                if loads:
                    wait_apart(sp, pv_done, 2 + N_STEP * n, apart)
                    load(sp, n + 2, (s + 2) % SLOTS)
                for c in range(NC - 1):
                    store_o(n, c, turns(n) + c)
                if has_next:
                    store_neg_rows(n + 1, (s + 1) % SLOTS)
                store_o(n, NC - 1, turns(n) + NC - (0 if has_next else 1))
            rounds = (UNITS - 2) // SLOTS
            with sp.Fori(0, rounds) as j:
                for s in range(SLOTS):
                    body(SLOTS * j + s, s, True, True)
            for n in range(SLOTS * rounds, UNITS):
                body(n, n % SLOTS, n + 2 < UNITS, n + 1 < UNITS)
            for s in range(2):
                wait_apart(sp, o_stored[s], 16 * UNITS * NC // 2, apart)

        @block.gpsimd
        def _(pool):
            nc.gpsimd.memset(ident[:, :], 0.0)
            nc.gpsimd.memset(ident_b[:, :], 0.0)
            nc.gpsimd.memset(mask_q[:, :], 0.0)
            nc.gpsimd.memset(mask_k[:, :], 0.0)
            nc.gpsimd.memset(neg_max[:, :], 0.0)
            nc.gpsimd.memset(piece_max[:, :, :], -3e38).then_inc(consts, 1)
            wait_apart(pool, consts, 1, apart)
            for m in (ident, ident_b):
                nc.gpsimd.affine_select(out=m[:, :], in_=m[:, :], compare_op=ALU.not_equal, fill=1.0,
                                        base=0, pattern=[[-1, P]], channel_multiplier=1)
            nc.gpsimd.affine_select(out=mask_q[:, :], in_=mask_q[:, :], compare_op=ALU.is_ge, fill=-BIG,
                                    base=0, pattern=[[-1, P]], channel_multiplier=1)
            nc.gpsimd.affine_select(out=mask_k[:, :], in_=mask_k[:, :], compare_op=ALU.is_ge, fill=-BIG,
                                    base=0, pattern=[[1, P]], channel_multiplier=-1).then_inc(consts, 1)
            for s in range(SLOTS):
                wait_apart(pool, consts, 2 + s, apart)
                nc.gpsimd.memset(k6[s][SPLIT:ROWS, :, :], 1.0).then_inc(consts, 1)

        @block.vector
        def _(dve):
            dve.sem_inc(row_free, 2)
            dve.sem_inc(tr_free, 1)
            dve.wait_ge(consts, 2)

            def reduce_piece(n, m):
                hh, i, pc, width = PIECES[m]
                dve.wait_ge(row_scored, N_PIECE * n + m + 1)
                nc.vector.tensor_reduce(piece_max[:, hh * KT + i, pc:pc + 1], row_ps[m % 2][:, 0:width], AX_X,
                                        ALU.max).then_inc(row_free, 1)

            def negate_max(n, turn):
                dve.wait_ge(row_free, 2 + N_PIECE * (n + 1))
                nc.vector.tensor_reduce(neg_max[:, 0:HG * KT], piece_max[:, :, :], AX_X, ALU.max, negate=True
                                        ).then_inc(neg_max_done, 1)
                dve.wait_ge(tr_done, turn + 1)
                dve.wait_ge(neg_stored, 32 * n)
                nc.vector.tensor_copy(neg_hi[:, :], tr_ps[0:HG * KT, 0:P]).then_inc(neg_hi_done, 1)
                dve.wait_ge(neg_hi_done, n + 1)
                nc.vector.tensor_tensor(neg_lo[:, :], tr_ps[0:HG * KT, 0:P], neg_hi[:, :], ALU.subtract
                                        ).then_inc(neg_rows_done, 1)
                dve.wait_ge(neg_rows_done, n + 1)
                dve.sem_inc(tr_free, 1)

            def normalise(n, c, turn):
                dve.wait_ge(tr_done, turn + 1)
                tr = tr_ps[:, :].rearrange("p (g v) -> p g v", v=VW)
                nc.vector.reciprocal(inv[:, :], tr[:, :, DH]).then_inc(inv_done, 1)
                dve.wait_ge(inv_done, NC * n + c + 1)
                dve.wait_ge(o_stored[c % 2], 16 * (NC // 2 * n + c // 2))
                nc.vector.tensor_tensor(o_sb[:, c % 2, :, :].rearrange("p t (h d) -> p (t h) d", d=DH), tr[:, :, 0:DH],
                                        inv[:, :].unsqueeze(2).to_broadcast([P, TT * HG, DH]), ALU.mult
                                        ).then_inc(tr_free, 1)

            for m in range(N_PIECE):
                reduce_piece(0, m)
            negate_max(0, 0)

            def body(n, s, has_next, j):
                done = 0
                for i in range(N_STEP):
                    upto = min(N_PIECE, (i + 1) * N_PIECE // N_STEP) if has_next else 0
                    for m in range(done, upto):
                        reduce_piece(n + 1, m)
                    done = upto
                    for c in range(NC - 1):
                        if i == LAST[c] + 3:
                            normalise(n, c, turns(n) + c)
                if has_next:
                    negate_max(n + 1, turns(n) + NC - 1)
                normalise(n, NC - 1, turns(n) + NC - (0 if has_next else 1))
            units(dve, body)

        @block.scalar
        def _(act):
            act.sem_inc(pv_done, 2)
            act.sem_inc(probs_done, 2)

            def exps(n, i, u):
                c, kt = STEPS[i]
                width = CT - max(0, kt - TT * c) * P
                act.wait_ge(st_scored, 2 * (N_STEP * n + i) + u + 1)
                act.wait_ge(pv_done, N_STEP * n + i + 1)
                nc.scalar.activation(probs[:, (2 * i + u) % 4, :, 0:width], st_ps[u][:, :, 0:width], ACT.Exp
                                     ).then_inc(probs_done, 1)

            def copy_pv(n, c, has_next):
                act.wait_ge(pv_done, 2 + N_STEP * n + LAST[c] + 1)
                act.wait_ge(tr_done, turns(n) + c)
                nc.scalar.copy(pv_sb[:, :], pv_ps[:, :]).then_inc(pv_copied, 1)

            def body(n, s, has_next, j):
                for i in range(N_STEP):
                    exps(n, i, 0)
                    exps(n, i, 1)
                    for c in range(NC - 1):
                        if i == LAST[c] + 1:
                            copy_pv(n, c, has_next)
                copy_pv(n, NC - 1, has_next)
            units(act, body)

        @block.tensor
        def _(pe):
            def row_scores(n, s, m, rnd):
                hh, i, pc, width = PIECES[m]
                if m == 0:
                    pe.wait_ge(loaded[s], N_LOAD * (rnd + 1))
                pe.wait_ge(row_free, N_PIECE * n + m + 1)
                diagonal = pc == i // TT
                out = row_ps[m % 2]
                last = nc.tensor.matmul(out[:, 0:width], q6[s][0:SPLIT, hh, i * P:(i + 1) * P],
                                        k6[s][0:SPLIT, hh, pc * CT:pc * CT + width], start=True, stop=not diagonal)
                if diagonal:
                    last = nc.tensor.matmul(out[:, width - P:width], ident_b[:, :], mask_q[:, :], start=False, stop=True)
                last.then_inc(row_scored, 1)

            def transpose_max(n, turn):
                pe.wait_ge(neg_max_done, n + 1)
                pe.wait_ge(tr_free, turn + 1)
                nc.tensor.transpose(tr_ps[:, 0:P], neg_max[:, :], ident[:, :]).then_inc(tr_done, 1)

            def scores(n, s, i, u):
                c, kt = STEPS[i]
                skip = max(0, kt - TT * c) * P
                width = CT - skip
                if i == 0 and u == 0:
                    pe.wait_ge(neg_stored, 32 * (n + 1))
                    pe.wait_ge(consts, 2 + SLOTS)
                pe.wait_ge(probs_done, 2 * (N_STEP * n + i) + u + 1)
                diagonal = kt >= TT * c
                for j in range(2):
                    hh = 2 * u + j
                    last = nc.tensor.matmul(st_ps[u][:, j, 0:width], k6[s][:, hh, kt * P:(kt + 1) * P],
                                            q6[s][:, hh, c * CT + skip:(c + 1) * CT], start=True, stop=not diagonal)
                    if diagonal:
                        last = nc.tensor.matmul(st_ps[u][:, j, 0:P], ident_b[:, :], mask_k[:, :], start=False, stop=True)
                last.then_inc(st_scored, 1)

            def values(n, s, i):
                c, kt = STEPS[i]
                skip = max(0, kt - TT * c) * P
                if kt == 0:
                    pe.wait_ge(pv_copied, NC * n + c)
                pe.wait_ge(probs_done, 2 + 2 * (N_STEP * n + i) + 2)
                for hh in range(HG):
                    last = nc.tensor.matmul(pv_ps[hh * VW:(hh + 1) * VW, skip:CT], vg[s][:, kt, hh * VW:(hh + 1) * VW],
                                            probs[:, (2 * i + hh // 2) % 4, hh % 2, 0:CT - skip],
                                            start=kt == 0, stop=kt == TT * (c + 1) - 1, skip_group_check=True)
                last.then_inc(pv_done, 1)

            def transpose_o(n, c, turn):
                pe.wait_ge(pv_copied, NC * n + c + 1)
                pe.wait_ge(tr_free, turn + 1)
                for t in range(TT):
                    last = nc.tensor.transpose(tr_ps[:, t * P:(t + 1) * P], pv_sb[:, t * P:(t + 1) * P], ident[:, :])
                last.then_inc(tr_done, 1)

            pe.wait_ge(consts, 2)

            def maxima(n1, s, first, end, j):
                for m in range(first, end):
                    row_scores(n1, (s + 1) % SLOTS, m, next_round(j, s))

            for m in range(N_PIECE):
                row_scores(0, 0, m, 0)
            transpose_max(0, 0)

            def body(n, s, has_next, j):
                done = 0
                for i in range(N_STEP):
                    upto = min(N_PIECE, (i + 1) * N_PIECE // N_STEP) if has_next else 0
                    cut = [done + k * (upto - done) // 4 for k in range(5)]
                    done = upto
                    maxima(n + 1, s, cut[0], cut[1], j)
                    scores(n, s, i, 0)
                    maxima(n + 1, s, cut[1], cut[2], j)
                    scores(n, s, i, 1)
                    maxima(n + 1, s, cut[2], cut[3], j)
                    if i:
                        values(n, s, i - 1)
                    maxima(n + 1, s, cut[3], cut[4], j)
                    for c in range(NC - 1):
                        if i == LAST[c] + 2:
                            transpose_o(n, c, turns(n) + c)
                values(n, s, N_STEP - 1)
                if has_next:
                    transpose_max(n + 1, turns(n) + NC - 1)
                transpose_o(n, NC - 1, turns(n) + NC - (0 if has_next else 1))
            units(pe, body)


ROW_TILE = 256
CAP = T + ROW_TILE
N_TILE = T * 2 // ROW_TILE + E
SORTED = E * CAP + E * ROW_TILE


def phase3_route(nc, x_v, xn_v, o_v, w, sorted_rows, res_v, pos_v, gates_v, table):
    with ExitStack() as ctx:
        sb = lambda name, shape, dt=F32: ctx.enter_context(nc.sbuf_tensor(name, shape, dt))
        sem = lambda name: ctx.enter_context(nc.semaphore(name))
        bank = lambda name: ctx.enter_context(nc.psum_tensor(name, [P, CT], F32))

        ident = sb("p3_ident", [P, P])
        before = sb("p3_before", [P, P], BF16)
        ones = sb("p3_ones", [P, P], BF16)
        iota_e = sb("p3_iota_e", [P, E])
        iota_tile = sb("p3_iota_tile", [P, N_TILE])
        half = sb("p3_minus_half", [P, TT])
        zeros = sb("p3_zeros", [P, D])
        wo = sb("p3_wo", [P, KD, D])
        gate_w = sb("p3_gate_w", [P, KD, E])
        g2 = sb("p3_g2", [P, D])
        x = sb("p3_x", [P, 2, TT, D])
        xn = sb("p3_xn", [P, 2, TT, D])
        o = sb("p3_o", [P, 2, TT, NG, HG * DH])
        oT = sb("p3_oT", [P, KD, CT])
        x2 = sb("p3_x2", [P, TT, D])
        sq = sb("p3_sq", [P, TT, D])
        ss = sb("p3_ss", [P, TT])
        rrms = sb("p3_rrms", [P, TT])
        res = sb("p3_res", [P, 2, TT, D])
        th = sb("p3_th", [P, 2, TT, D])
        tT = sb("p3_tT", [P, KD, CT])
        logits = sb("p3_logits", [P, TT, E])
        top = sb("p3_top", [P, TT, E])
        top_i = sb("p3_top_i", [P, TT, E], U32)
        top_f = sb("p3_top_f", [P, TT, 2])
        chosen = sb("p3_chosen", [P, TT, 2, E])
        either = sb("p3_either", [P, TT, E], BF16)
        diff = sb("p3_diff", [P, TT])
        ediff = sb("p3_ediff", [P, TT])
        denom = sb("p3_denom", [P, TT])
        gates = sb("p3_gates", [P, 2, TT, 2])
        base = sb("p3_base", [P, E])
        place = sb("p3_place", [P, TT, E])
        picked = sb("p3_picked", [P, TT, 2, E])
        pos_f = sb("p3_pos_f", [P, TT, 2])
        pos_all = sb("p3_pos_all", [P, B * NC * TT * 2])
        pos_sum = sb("p3_pos_sum", [P, B * NC * TT * 2])
        behind = sb("p3_behind", [P, 2, B * NC * TT * 2])
        pos_out = sb("p3_pos_out", [P, B * NC * TT * 2], U32)
        pos = sb("p3_pos", [P, 2, TT, 2], U32)
        region = sb("p3_region", [P, E])
        tail_f = sb("p3_tail_f", [P, E, 2])
        tail = sb("p3_tail", [P, E, 2], U32)
        iota_p = sb("p3_iota_p", [P, 2])
        count = sb("p3_count", [P, E])
        count_i = sb("p3_count_i", [P, E], mybir.dt.int32)
        tiles = sb("p3_tiles", [P, E])
        ends = sb("p3_ends", [P, E])
        ones_e = sb("p3_ones_e", [P, E])
        jump = sb("p3_jump", [P, E])
        past = sb("p3_past", [P, N_TILE, E])
        past_j = sb("p3_past_j", [P, N_TILE, E])
        table_f = sb("p3_table_f", [P, 2, N_TILE])
        table_i = sb("p3_table_i", [P, 2, N_TILE], mybir.dt.int32)

        oT_ps = [bank(f"p3_oT{k}_ps") for k in range(KD)]
        mla_ps = [bank(f"p3_mla{i}_ps") for i in range(2)]
        tT_ps = [bank(f"p3_tT{k}_ps") for k in range(KD)]
        small_ps = bank("p3_small_ps")
        logit_ps = small_ps[:, 0:TT * E].rearrange("p (t e) -> p t e", e=E)
        rank_ps = small_ps[:, TT * E:2 * TT * E].rearrange("p (t e) -> p t e", e=E)
        total_ps = small_ps[:, 2 * TT * E:2 * TT * E + E]

        w_loaded = sem("p3_w_loaded")
        consts = sem("p3_consts")
        zeroed = sem("p3_zeroed")
        loaded = [sem(f"p3_loaded{s}") for s in range(2)]
        oT_done = sem("p3_oT_done")
        oT_copied = sem("p3_oT_copied")
        mla_done = sem("p3_mla_done")
        x2_done = sem("p3_x2_done")
        ss_done = sem("p3_ss_done")
        mean_done = sem("p3_mean_done")
        rrms_done = sem("p3_rrms_done")
        res_done = sem("p3_res_done")
        th_done = sem("p3_th_done")
        tT_done = sem("p3_tT_done")
        tT_copied = sem("p3_tT_copied")
        logit_done = sem("p3_logit_done")
        chain = sem("p3_chain")
        diff_done = sem("p3_diff_done")
        ediff_done = sem("p3_ediff_done")
        either_done = sem("p3_either_done")
        rank_done = sem("p3_rank_done")
        place_done = sem("p3_place_done")
        gates_done = sem("p3_gates_done")
        pos_done = sem("p3_pos_done")
        scattered = [sem(f"p3_scattered{s}") for s in range(2)]
        tail_done = sem("p3_tail_done")
        tail_stored = sem("p3_tail_stored")
        res_stored = [sem(f"p3_res_stored{s}") for s in range(2)]
        place_stored = [sem(f"p3_place_stored{s}") for s in range(2)]
        table_done = sem("p3_table_done")
        table_stored = sem("p3_table_stored")
        apart = sem("p3_apart")
        block = ctx.enter_context(nc.Block())
        ALL = B * NC
        N_LOAD = 16 * (NG + 2)

        def chunks(eng, body):
            with eng.Fori(0, B - 1) as b:
                for c in range(NC):
                    body(b, c, NC * b + c, True)
            for c in range(NC):
                body(B - 1, c, NC * (B - 1) + c, c < NC - 1)

        def uses(b, c):
            return (NC // 2) * b + c // 2

        @block.sync
        def _(sp):
            sp.dma_start(wo[:, :, :], w["ffn_Wo"].rearrange("(k p) n -> p k n", p=P)).then_inc(w_loaded, 16)
            sp.dma_start(gate_w[:, :, :], w["ffn_gate_w"].rearrange("(k p) n -> p k n", p=P)).then_inc(w_loaded, 16)
            sp.dma_start(g2[:, :], w["ffn_g2"].partition_broadcast(P)).then_inc(w_loaded, 16)

            def load(b, c):
                s = c % 2
                for g in range(NG):
                    sp.dma_start(o[:, s, :, g, :], o_v[b, c][:, :, g, :]).then_inc(loaded[s], 16)
                sp.dma_start(xn[:, s, :, :], xn_v[b, c]).then_inc(loaded[s], 16)
                sp.dma_start(x[:, s, :, :], x_v[b, c]).then_inc(loaded[s], 16)

            load(0, 0)
            load(0, 1)
            wait_apart(sp, consts, 1, apart)
            sp.dma_start(sorted_rows[E * CAP:SORTED, :].rearrange("(r p) d -> p r d", p=P),
                         zeros[:, :].unsqueeze(1).to_broadcast([P, E * ROW_TILE // P, D])).then_inc(zeroed, 16)

            def body(b, c, n, follows):
                s = c % 2
                wait_apart(sp, res_done, n + 1, apart)
                if follows and not (isinstance(b, int) and b == B - 1 and c + 2 >= NC):
                    load(b if c + 2 < NC else b + 1, (c + 2) % NC)
                sp.dma_start(res_v[b, c], res[:, s, :, :]).then_inc(res_stored[s], 16)
                wait_apart(sp, gates_done, n + 1, apart)
                sp.dma_start(gates_v[b, c], gates[:, s, :, :]).then_inc(place_stored[s], 16)
            chunks(sp, body)
            wait_apart(sp, table_done, 1, apart)
            sp.dma_start(table.rearrange("(a k) n -> a k n", a=1), table_i[0:1, :, :]).then_inc(table_stored, 16)
            sp.dma_start(pos_v, pos_out[:, :]).then_inc(table_stored, 16)
            wait_apart(sp, zeroed, 16, apart)
            wait_apart(sp, table_stored, 32, apart)
            for s in range(2):
                wait_apart(sp, res_stored[s], 16 * ALL // 2, apart)
                wait_apart(sp, place_stored[s], 16 * ALL // 2, apart)

        @block.gpsimd
        def _(pool):
            nc.gpsimd.memset(zeros[:, :], 0.0).then_inc(consts, 1)
            nc.gpsimd.memset(ident[:, :], 0.0)
            nc.gpsimd.memset(ones[:, :], 1.0)
            nc.gpsimd.memset(half[:, :], -0.5)
            nc.gpsimd.memset(ones_e[:, :], 1.0)
            exact = dict(allow_small_or_imprecise_dtypes=True)
            nc.gpsimd.iota(iota_e[:, :], [[1, E]], base=0, channel_multiplier=0, **exact)
            nc.gpsimd.iota(iota_tile[:, :], [[1, N_TILE]], base=0, channel_multiplier=0, **exact)
            nc.gpsimd.iota(iota_p[:, :], [[P, 2]], base=0, channel_multiplier=1, **exact)
            nc.gpsimd.iota(region[:, :], [[CAP, E]], base=0, channel_multiplier=0, **exact).then_inc(consts, 1)
            wait_apart(pool, consts, 2, apart)
            nc.gpsimd.affine_select(out=ident[:, :], in_=ident[:, :], compare_op=ALU.not_equal, fill=1.0,
                                    base=0, pattern=[[-1, P]], channel_multiplier=1)
            nc.gpsimd.affine_select(out=before[:, :], in_=ones[:, :], compare_op=ALU.is_gt, fill=0.0,
                                    base=0, pattern=[[1, P]], channel_multiplier=-1).then_inc(consts, 1)

            def stage_a(n, s, u):
                wait_apart(pool, ss_done, n + 1, apart)
                nc.gpsimd.tensor_scalar(rrms[:, :], ss[:, :], 1.0 / D, EPS_RMS, ALU.mult, ALU.add).then_inc(mean_done, 1)
                wait_apart(pool, mean_done, n + 1, apart)
                nc.gpsimd.tensor_tensor(rrms[:, :], rrms[:, :], half[:, :], ALU.pow).then_inc(rrms_done, 1)
                wait_apart(pool, res_stored[s], 16 * u, apart)
                nc.gpsimd.tensor_tensor(res[:, s, :, :], x[:, s, :, :], x2[:, :, :], ALU.add).then_inc(res_done, 1)

            stage_a(0, 0, 0)

            def body(b, c, n, follows):
                s = c % 2
                if follows:
                    stage_a(n + 1, (c + 1) % 2, uses(b, c + 1))
                wait_apart(pool, pos_done, n + 1, apart)
                for t in range(TT):
                    for k in range(2):
                        nc.gpsimd.indirect_dma_start(
                            sorted_rows, bass.IndirectOffsetOnAxis(pos[:, s, t, k:k + 1], 0), th[:, s, t, :], None
                        ).then_inc(scattered[s], 16)
            chunks(pool, body)
            wait_apart(pool, tail_done, 1, apart)
            for e in range(E):
                for i in range(2):
                    nc.gpsimd.indirect_dma_start(sorted_rows, bass.IndirectOffsetOnAxis(tail[:, e, i:i + 1], 0),
                                                 zeros[:, :], None).then_inc(tail_stored, 16)
            for s in range(2):
                wait_apart(pool, scattered[s], 16 * 2 * TT * ALL // 2, apart)
            wait_apart(pool, tail_stored, 16 * 2 * E, apart)

        @block.vector
        def _(dve):
            dve.wait_ge(consts, 3)
            nc.vector.tensor_copy(base[:, :], region[:, :]).then_inc(chain, 1)
            dve.wait_ge(chain, 1)
            dve.wait_ge(w_loaded, 48)
            LINKS = 10

            def add_attention(n, s, u):
                dve.wait_ge(loaded[s], N_LOAD * (u + 1))
                dve.wait_ge(res_done, n)
                dve.wait_ge(th_done, n)
                for i in range(2):
                    dve.wait_ge(mla_done, 2 * n + i + 1)
                    nc.vector.tensor_tensor(x2[:, 2 * i:2 * i + 2, :], mla_ps[i][:, :].rearrange("p (t d) -> p t d", d=D),
                                            xn[:, s, 2 * i:2 * i + 2, :], ALU.add).then_inc(x2_done, 1)

            def scale_rms(n, s, u):
                dve.wait_ge(rrms_done, n + 1)
                dve.wait_ge(scattered[s], 16 * 2 * TT * u)
                for t in range(TT):
                    last = nc.vector.scalar_tensor_tensor(th[:, s, t, :], x2[:, t, :], rrms[:, t:t + 1], g2[:, :],
                                                          ALU.mult, ALU.mult)
                last.then_inc(th_done, 1)

            add_attention(0, 0, 0)
            scale_rms(0, 0, 0)

            def body(b, c, n, follows):
                s, s1 = c % 2, (c + 1) % 2
                u1 = uses(b, c + 1)
                links = [0]

                def link(ins):
                    links[0] += 1
                    ins.then_inc(chain, 1)
                    wait_apart(dve, chain, 1 + LINKS * n + links[0], apart)

                if follows:
                    add_attention(n + 1, s1, u1)
                dve.wait_ge(logit_done, n + 1)
                link(nc.vector.tensor_copy(logits[:, :, :], logit_ps))
                for t in range(TT):
                    last = nc.vector.max(top[:, t, :], logits[:, t, :])
                link(last)
                for t in range(TT):
                    last = nc.vector.max_index(top_i[:, t, :], top[:, t, :], logits[:, t, :])
                link(last)
                nc.vector.tensor_tensor(diff[:, :], top[:, :, 1], top[:, :, 0], ALU.subtract).then_inc(diff_done, 1)
                link(nc.vector.tensor_copy(top_f[:, :, :], top_i[:, :, 0:2]))
                link(nc.vector.tensor_tensor(chosen[:, :, :, :].rearrange("p t k e -> p (t k) e"),
                                             iota_e[:, :].unsqueeze(1).to_broadcast([P, TT * 2, E]),
                                             top_f[:, :, :].rearrange("p t k -> p (t k)").unsqueeze(2)
                                             .to_broadcast([P, TT * 2, E]), ALU.is_equal))
                nc.vector.tensor_tensor(either[:, :, :], chosen[:, :, 0, :], chosen[:, :, 1, :], ALU.add
                                        ).then_inc(either_done, 1)
                dve.wait_ge(ediff_done, n + 1)
                link(nc.vector.tensor_scalar(denom[:, :], ediff[:, :], 1.0, None, ALU.add))
                dve.wait_ge(place_stored[s], 16 * uses(b, c))
                link(nc.vector.reciprocal(gates[:, s, :, 0], denom[:, :]))
                nc.vector.tensor_tensor(gates[:, s, :, 1], ediff[:, :], gates[:, s, :, 0], ALU.mult).then_inc(gates_done, 1)
                if follows:
                    scale_rms(n + 1, s1, u1)
                dve.wait_ge(rank_done, n + 1)
                dve.wait_ge(place_done, n)
                link(nc.vector.tensor_tensor(place[:, :, :], rank_ps, base[:, :].unsqueeze(1).to_broadcast([P, TT, E]),
                                             ALU.add))
                nc.vector.tensor_tensor(base[:, :], total_ps, base[:, :], ALU.add).then_inc(place_done, 1)
                for k in range(2):
                    last = nc.vector.tensor_tensor(picked[:, :, k, :], chosen[:, :, k, :], place[:, :, :], ALU.mult)
                link(last)
                link(nc.vector.tensor_reduce(pos_f[:, :, :], picked[:, :, :, :], AX_X, ALU.add))
                nc.vector.tensor_copy(pos_all[:, bass.ds(n * TT * 2, TT * 2)], pos_f[:, :, :].rearrange("p t k -> p (t k)"))
                dve.wait_ge(scattered[s], 16 * 2 * TT * uses(b, c))
                nc.vector.tensor_copy(pos[:, s, :, :], pos_f[:, :, :]).then_inc(pos_done, 1)
                assert links[0] == LINKS
            chunks(dve, body)

            links = [0]

            def link(ins):
                links[0] += 1
                ins.then_inc(chain, 1)
                dve.wait_ge(chain, 1 + LINKS * ALL + links[0])

            dve.wait_ge(place_done, ALL)
            link(nc.vector.tensor_tensor(tail_f[:, :, :], base[:, :].unsqueeze(2).to_broadcast([P, E, 2]),
                                         iota_p[:, :].unsqueeze(1).to_broadcast([P, E, 2]), ALU.add))
            nc.vector.tensor_copy(tail[:, :, :], tail_f[:, :, :]).then_inc(tail_done, 1)
            link(nc.vector.tensor_tensor(count[:, :], base[:, :], region[:, :], ALU.subtract))
            link(nc.vector.tensor_scalar(count_i[:, :], count[:, :], float(ROW_TILE - 1), None, ALU.add))
            link(nc.vector.tensor_scalar(count_i[:, :], count_i[:, :], ROW_TILE.bit_length() - 1, None,
                                         ALU.arith_shift_right))
            link(nc.vector.tensor_copy(tiles[:, :], count_i[:, :]))
            link(nc.vector.tensor_tensor_scan(ends[:, :], ones_e[:, :], tiles[:, :], 0.0, ALU.mult, ALU.add))
            link(nc.vector.tensor_scalar(jump[:, :], tiles[:, :], -float(ROW_TILE), float(CAP), ALU.mult, ALU.add))
            link(nc.vector.tensor_tensor(past[:, :, :], iota_tile[:, :].unsqueeze(2).to_broadcast([P, N_TILE, E]),
                                         ends[:, :].unsqueeze(1).to_broadcast([P, N_TILE, E]), ALU.is_ge))
            link(nc.vector.tensor_reduce(table_f[:, 0, :], past[:, :, :], AX_X, ALU.add))
            link(nc.vector.tensor_tensor(past_j[:, :, :], past[:, :, :],
                                         jump[:, :].unsqueeze(1).to_broadcast([P, N_TILE, E]), ALU.mult))
            link(nc.vector.tensor_reduce(table_f[:, 1, :], past_j[:, :, :], AX_X, ALU.add))
            link(nc.vector.scalar_tensor_tensor(table_f[:, 1, :], iota_tile[:, :], float(ROW_TILE), table_f[:, 1, :],
                                                ALU.mult, ALU.add))
            link(nc.vector.tensor_scalar(table_f[:, 0, :], table_f[:, 0, :], float(E - 1), None, ALU.min))
            nc.vector.tensor_copy(table_i[:, :, :], table_f[:, :, :])
            for e in range(1, E):
                link(nc.vector.tensor_scalar(behind[:, e % 2, :], pos_all[:, :], region[:, e:e + 1], jump[:, e - 1:e],
                                             ALU.is_ge, ALU.mult))
                link(nc.vector.tensor_tensor(pos_sum[:, :], pos_sum[:, :] if e > 1 else pos_all[:, :], behind[:, e % 2, :],
                                             ALU.subtract))
            nc.vector.tensor_copy(pos_out[:, :], pos_sum[:, :]).then_inc(table_done, 1)

        @block.scalar
        def _(act):
            def copy_oT(n):
                for k in range(KD):
                    act.wait_ge(oT_done, KD * n + k + 1)
                    act.wait_ge(mla_done, 2 * n)
                    nc.scalar.copy(oT[:, k, :], oT_ps[k][:, :]).then_inc(oT_copied, 1)

            def squares(n):
                act.wait_ge(mean_done, n)
                act.wait_ge(x2_done, 2 * n + 2)
                for t in range(TT):
                    last = nc.scalar.activation(sq[:, t, :], x2[:, t, :], ACT.Square, accum_out=ss[:, t:t + 1])
                last.then_inc(ss_done, 1)

            copy_oT(0)
            squares(0)

            def body(b, c, n, follows):
                if follows:
                    copy_oT(n + 1)
                for k in range(KD):
                    act.wait_ge(tT_done, KD * n + k + 1)
                    act.wait_ge(logit_done, n)
                    nc.scalar.copy(tT[:, k, :], tT_ps[k][:, :]).then_inc(tT_copied, 1)
                if follows:
                    squares(n + 1)
                act.wait_ge(diff_done, n + 1)
                nc.scalar.activation(ediff[:, :], diff[:, :], ACT.Exp).then_inc(ediff_done, 1)
            chunks(act, body)

        @block.tensor
        def _(pe):
            pe.wait_ge(consts, 3)
            pe.wait_ge(w_loaded, 48)

            def transpose_o(n, s, u):
                pe.wait_ge(loaded[s], N_LOAD * (u + 1))
                pe.wait_ge(oT_copied, KD * n)
                for k in range(KD):
                    for t in range(TT):
                        last = nc.tensor.transpose(oT_ps[k][:, t * P:(t + 1) * P],
                                                   o[:, s, t, 2 * k:2 * k + 2, :].rearrange("p g d -> p (g d)"), ident[:, :])
                    last.then_inc(oT_done, 1)

            def project(n):
                pe.wait_ge(oT_copied, KD * n + KD)
                pe.wait_ge(x2_done, 2 * n)
                for i in range(2):
                    for t in range(2):
                        tok = (2 * i + t) * P
                        for k in range(KD):
                            last = nc.tensor.matmul(mla_ps[i][:, t * D:(t + 1) * D], oT[:, k, tok:tok + P], wo[:, k, :],
                                                    start=k == 0, stop=k == KD - 1)
                    last.then_inc(mla_done, 1)

            transpose_o(0, 0, 0)
            project(0)

            def body(b, c, n, follows):
                s = c % 2
                if follows:
                    transpose_o(n + 1, (c + 1) % 2, uses(b, c + 1))
                pe.wait_ge(th_done, n + 1)
                pe.wait_ge(tT_copied, KD * n)
                for k in range(KD):
                    for t in range(TT):
                        last = nc.tensor.transpose(tT_ps[k][:, t * P:(t + 1) * P], th[:, s, t, k * P:(k + 1) * P], ident[:, :])
                    last.then_inc(tT_done, 1)
                if follows:
                    project(n + 1)
                pe.wait_ge(tT_copied, KD * n + KD)
                pe.wait_ge(place_done, n)
                for t in range(TT):
                    for k in range(KD):
                        last = nc.tensor.matmul(logit_ps[:, t, :], tT[:, k, t * P:(t + 1) * P], gate_w[:, k, :],
                                                start=k == 0, stop=k == KD - 1)
                last.then_inc(logit_done, 1)
                pe.wait_ge(either_done, n + 1)
                for t in range(TT):
                    nc.tensor.matmul(rank_ps[:, t, :], before[:, :], either[:, t, :], start=True, stop=t == 0)
                    for t0 in range(t):
                        nc.tensor.matmul(rank_ps[:, t, :], ones[:, :], either[:, t0, :], start=False, stop=t0 == t - 1)
                for t in range(TT):
                    last = nc.tensor.matmul(total_ps, ones[:, :], either[:, t, :], start=t == 0, stop=t == TT - 1)
                last.then_inc(rank_done, 1)
            chunks(pe, body)


def phase4_experts(nc, x_n, w, sorted_rows, expert_rows, attn_rows, table):
    NB = T // P
    RT = ROW_TILE // P
    FB = F // P
    HH = H * H
    with ExitStack() as ctx:
        sb = lambda name, shape, dt=F32: ctx.enter_context(nc.sbuf_tensor(name, shape, dt))
        sem = lambda name: ctx.enter_context(nc.semaphore(name))
        bank = lambda name: ctx.enter_context(nc.psum_tensor(name, [P, CT], F32))

        ident = sb("p4_ident", [P, P])
        ones_rows = sb("p4_ones_rows", [3, P], BF16)
        bias = sb("p4_bias", [1, 3, D])
        bias_part = sb("p4_bias_part", [1, 3, 3, D], BF16)
        bias_rest = sb("p4_bias_rest", [1, 3, D])
        bias_rows = sb("p4_bias_rows", [3, 3, D], BF16)
        wqkv = sb("p4_wqkv", [P, KD, 3, D])
        table_sb = sb("p4_table", [1, 2, N_TILE], mybir.dt.int32)
        w1 = sb("p4_w1", [P, 2, KD, F])
        w2 = sb("p4_w2", [P, 2, FB, D])
        rows = sb("p4_rows", [P, 2, RT, D])
        rT = sb("p4_rT", [P, KD, ROW_TILE])
        hid = sb("p4_hid", [P, FB, ROW_TILE])
        y = sb("p4_y", [P, 2, RT, D])
        xn = sb("p4_xn", [P, 2, D])
        xT = sb("p4_xT", [P, 2, KD, P])
        kv = sb("p4_kv", [P, 2, 2, D])
        prod = sb("p4_prod", [P, H, H, DH])
        s = sb("p4_s", [P, H, H])
        smax = sb("p4_smax", [P, H])
        sm = sb("p4_sm", [P, H, H])
        pr = sb("p4_pr", [P, 2, H, H])
        psum = sb("p4_psum", [P, H])
        inv = sb("p4_inv", [P, 2, H])
        pv = sb("p4_pv", [P, 2, H, DH, H])
        oh = sb("p4_oh", [P, 2, H, DH])

        rT_ps = bank("p4_rT_ps")
        hid_ps = [bank(f"p4_hid{i}_ps") for i in range(2)]
        y_ps = bank("p4_y_ps")
        xT_ps = bank("p4_xT_ps")
        qk_ps = [bank(f"p4_qk{i}_ps") for i in range(2)]
        v_ps = bank("p4_v_ps")

        w_loaded = sem("p4_w_loaded")
        consts = sem("p4_consts")
        w_scaled = sem("p4_w_scaled")
        bias_split_step = sem("p4_bias_split_step")
        bias_split = sem("p4_bias_split")
        bias_loaded = sem("p4_bias_loaded")
        w1_loaded = [sem(f"p4_w1_loaded{i}") for i in range(2)]
        rows_loaded = [sem(f"p4_rows_loaded{i}") for i in range(2)]
        rT_done = sem("p4_rT_done")
        rT_copied = sem("p4_rT_copied")
        hid_done = sem("p4_hid_done")
        silu_done = sem("p4_silu_done")
        y_done = sem("p4_y_done")
        y_copied = sem("p4_y_copied")
        y_stored = [sem(f"p4_y_stored{i}") for i in range(2)]
        xn_loaded = [sem(f"p4_xn_loaded{i}") for i in range(2)]
        xT_done = sem("p4_xT_done")
        xT_copied = sem("p4_xT_copied")
        qkv_done = sem("p4_qkv_done")
        kv_copied = sem("p4_kv_copied")
        prod_done = sem("p4_prod_done")
        s_done = sem("p4_s_done")
        smax_done = sem("p4_smax_done")
        sm_done = sem("p4_sm_done")
        exp_done = sem("p4_exp_done")
        psum_done = sem("p4_psum_done")
        inv_done = sem("p4_inv_done")
        pv_done = sem("p4_pv_done")
        pv_added = sem("p4_pv_added")
        oh_done = sem("p4_oh_done")
        oh_stored = [sem(f"p4_oh_stored{i}") for i in range(2)]
        apart = sem("p4_apart")
        block = ctx.enter_context(nc.Block())

        def both(eng, body):
            pairs, all_pairs = NB // 2, N_TILE // 2

            def pair(j, has_block, ends=False):
                for u in range(2):
                    end = ends and u == 1
                    body(2 * j + u, u, j, has_block, has_block or not end, has_block and not end)
            pair(0, True)
            with eng.Fori(1, pairs - 1) as j:
                pair(j, True)
            pair(pairs - 1, True, True)
            pair(pairs, False)
            with eng.Fori(pairs + 1, all_pairs - 1) as j:
                pair(j, False)
            pair(all_pairs - 1, False, True)

        @block.sync
        def _(sp):
            for i, name in enumerate(("q", "k", "v")):
                sp.dma_start(wqkv[:, :, i, :], w[f"attn_W{name}"].rearrange("(k p) n -> p k n", p=P)).then_inc(w_loaded, 16)
                sp.dma_start(bias[:, i, :], w[f"attn_b{name}"].unsqueeze(0)).then_inc(w_loaded, 16)
            sp.dma_start(table_sb[:, :, :], table.unsqueeze(0)).then_inc(w_loaded, 16)
            wait_apart(sp, w_loaded, 16 * 7, apart)

            wait_apart(sp, bias_split, 1, apart)
            for a in range(3):
                sp.dma_start(bias_rows[a:a + 1, :, :], bias_part[:, a, :, :]).then_inc(bias_loaded, 16)

            def body(n, u, j, has_block, next_tile, next_block):
                e = sp.value_load(table_sb[0:1, 0, bass.ds(n, 1)], min_val=0, max_val=E - 1)
                row = sp.value_load(table_sb[0:1, 1, bass.ds(n, 1)], min_val=0, max_val=SORTED - ROW_TILE)
                if has_block:
                    wait_apart(sp, xT_done, n + 1, apart)
                    sp.dma_start(xn[:, u, :], x_n[bass.ds(n, 1), :, :].rearrange("a p d -> p (a d)")).then_inc(xn_loaded[u], 16)
                wait_apart(sp, rT_done, n + 1, apart)
                sp.dma_start(rows[:, u, :, :], sorted_rows[bass.ds(row, ROW_TILE), :].rearrange("(t p) d -> p t d", p=P)
                             ).then_inc(rows_loaded[u], 16)
                wait_apart(sp, y_done, n + 1, apart)
                sp.dma_start(w1[:, u, :, :], w["ffn_w1"][bass.ds(e, 1), :, :].rearrange("a (k p) f -> p (a k) f", p=P)
                             ).then_inc(w1_loaded[u], 16)
                sp.dma_start(w2[:, u, :, :], w["ffn_w2"][bass.ds(e, 1), :, :].rearrange("a (k p) f -> p (a k) f", p=P)
                             ).then_inc(w1_loaded[u], 16)
            both(sp, body)

        @block.gpsimd
        def _(pool):
            nc.gpsimd.memset(ident[:, :], 0.0)
            nc.gpsimd.memset(ones_rows[:, :], 1.0).then_inc(consts, 1)
            wait_apart(pool, consts, 1, apart)
            nc.gpsimd.affine_select(out=ident[:, :], in_=ident[:, :], compare_op=ALU.not_equal, fill=1.0,
                                    base=0, pattern=[[-1, P]], channel_multiplier=1).then_inc(consts, 1)

            def weigh_values(n, u):
                wait_apart(pool, exp_done, n + 1, apart)
                wait_apart(pool, pv_added, n + 1, apart)
                nc.gpsimd.tensor_tensor(
                    pv[:, u, :, :, :],
                    pr[:, u, :, :].unsqueeze(2).to_broadcast([P, H, DH, H]),
                    kv[:, u, 1, :].rearrange("p (j d) -> p d j", d=DH).unsqueeze(1).to_broadcast([P, H, DH, H]),
                    ALU.mult).then_inc(pv_done, 1)

            def store(n, u):
                wait_apart(pool, oh_done, n + 1, apart)
                nc.gpsimd.dma_start(attn_rows[bass.ds(n, 1), :, :].rearrange("a p d -> p (a d)"),
                                    oh[:, u, :, :].rearrange("p i d -> p (i d)")).then_inc(oh_stored[u], 16)

            weigh_values(0, 0)
            weigh_values(1, 1)
            with pool.Fori(1, NB // 2) as j:
                for u in range(2):
                    store(2 * j + u - 2, u)
                    weigh_values(2 * j + u, u)
            store(NB - 2, 0)
            store(NB - 1, 1)
            for u in range(2):
                wait_apart(pool, oh_stored[u], 16 * NB // 2, apart)

        @block.vector
        def _(dve):
            dve.sem_inc(xT_done, 2)
            dve.sem_inc(rT_done, 2)
            dve.sem_inc(y_done, 2)
            dve.sem_inc(pv_added, 2)
            dve.sem_inc(prod_done, 2)
            dve.sem_inc(psum_done, 2)
            dve.sem_inc(pv_done, 2)
            dve.wait_ge(w_loaded, 16 * 7)
            nc.vector.tensor_scalar(wqkv[:, :, 0, :], wqkv[:, :, 0, :], DH ** -0.5, None, ALU.mult)
            nc.vector.tensor_scalar(bias[:, 0, :], bias[:, 0, :], DH ** -0.5, None, ALU.mult).then_inc(w_scaled, 1)
            dve.wait_ge(w_scaled, 1)
            nc.vector.tensor_copy(bias_part[:, 0, :, :], bias[:, :, :]).then_inc(bias_split_step, 1)
            dve.wait_ge(bias_split_step, 1)
            nc.vector.tensor_tensor(bias_rest[:, :, :], bias[:, :, :], bias_part[:, 0, :, :], ALU.subtract
                                    ).then_inc(bias_split_step, 1)
            dve.wait_ge(bias_split_step, 2)
            nc.vector.tensor_copy(bias_part[:, 1, :, :], bias_rest[:, :, :]).then_inc(bias_split_step, 1)
            dve.wait_ge(bias_split_step, 3)
            nc.vector.tensor_tensor(bias_part[:, 2, :, :], bias_rest[:, :, :], bias_part[:, 1, :, :], ALU.subtract
                                    ).then_inc(bias_split, 1)

            def score(n, u):
                dve.wait_ge(kv_copied, n + 1)
                q = qk_ps[u][:, 0:D].rearrange("p (i d) -> p i d", d=DH)
                k = kv[:, u, 0, :].rearrange("p (j d) -> p j d", d=DH)
                nc.vector.tensor_tensor(prod[:, :, :, :], q.unsqueeze(2).to_broadcast([P, H, H, DH]),
                                        k.unsqueeze(1).to_broadcast([P, H, H, DH]), ALU.mult).then_inc(prod_done, 1)
                dve.wait_ge(prod_done, 2 + n + 1)
                nc.vector.tensor_reduce(s[:, :, :], prod[:, :, :, :], AX_X, ALU.add).then_inc(s_done, 1)
                dve.wait_ge(s_done, n + 1)
                nc.vector.tensor_reduce(smax[:, :], s[:, :, :], AX_X, ALU.max).then_inc(smax_done, 1)
                dve.wait_ge(smax_done, n + 1)
                dve.wait_ge(exp_done, n)
                nc.vector.tensor_tensor(sm[:, :, :], s[:, :, :], smax[:, :].unsqueeze(2).to_broadcast([P, H, H]),
                                        ALU.subtract).then_inc(sm_done, 1)

            def row_sums(n, u):
                dve.wait_ge(exp_done, n + 1)
                nc.vector.tensor_reduce(psum[:, :], pr[:, u, :, :], AX_X, ALU.add).then_inc(psum_done, 1)
                dve.wait_ge(psum_done, 2 + n + 1)
                nc.vector.reciprocal(inv[:, u, :], psum[:, :]).then_inc(inv_done, 1)

            def finish(n, u, j):
                dve.wait_ge(pv_done, 2 + n + 1)
                dve.wait_ge(oh_stored[u], 16 * j)
                nc.vector.tensor_reduce(oh[:, u, :, :], pv[:, u, :, :, :], AX_X, ALU.add).then_inc(pv_added, 1)
                dve.wait_ge(pv_added, 2 + n + 1)
                dve.wait_ge(inv_done, n + 1)
                nc.vector.tensor_tensor(oh[:, u, :, :], oh[:, u, :, :],
                                        inv[:, u, :].unsqueeze(2).to_broadcast([P, H, DH]), ALU.mult).then_inc(oh_done, 1)

            score(0, 0)
            score(1, 1)
            row_sums(0, 0)
            with dve.Fori(1, NB // 2) as j:
                for u in range(2):
                    score(2 * j + u, u)
                    row_sums(2 * j + u - 1, 1 - u)
                    finish(2 * j + u - 2, u, j - 1)
            row_sums(NB - 1, 1)
            finish(NB - 2, 0, NB // 2 - 1)
            finish(NB - 1, 1, NB // 2 - 1)

        @block.scalar
        def _(act):
            act.sem_inc(silu_done, 2)

            def copy_rows(n):
                act.wait_ge(rT_done, 2 + n + 1)
                act.wait_ge(hid_done, 2 * n)
                nc.scalar.copy(rT[:, :, :].rearrange("p k t -> p (k t)"), rT_ps[:, :]).then_inc(rT_copied, 1)

            def copy_block(n, u):
                act.wait_ge(xT_done, 2 + n + 1)
                nc.scalar.copy(xT[:, u, :, :].rearrange("p k t -> p (k t)"), xT_ps[:, 0:D]).then_inc(xT_copied, 1)

            def probabilities(n, u):
                act.wait_ge(sm_done, n + 1)
                act.wait_ge(psum_done, n + 1)
                act.wait_ge(pv_done, n + 1)
                nc.scalar.activation(pr[:, u, :, :], sm[:, :, :], ACT.Exp).then_inc(exp_done, 1)

            copy_rows(0)
            copy_block(0, 0)

            def body(n, u, j, has_block, next_tile, next_block):
                for i in range(2):
                    act.wait_ge(hid_done, 2 * n + i + 1)
                    act.wait_ge(y_done, 2 + n)
                    nc.scalar.activation(hid[:, 2 * i:2 * i + 2, :].rearrange("p k t -> p (k t)"), hid_ps[i][:, :],
                                         ACT.Silu).then_inc(silu_done, 1)
                if next_tile:
                    copy_rows(n + 1)
                if next_block:
                    copy_block(n + 1, 1 - u)
                if has_block:
                    act.wait_ge(qkv_done, n + 1)
                    act.wait_ge(prod_done, n + 1)
                    act.wait_ge(pv_done, n + 1)
                    nc.scalar.copy(kv[:, u, 0, :], qk_ps[u][:, D:2 * D])
                    nc.scalar.copy(kv[:, u, 1, :], v_ps[:, 0:D]).then_inc(kv_copied, 1)
                if has_block and not (isinstance(n, int) and n == 0):
                    probabilities(n - 1, 1 - u)
                elif isinstance(n, int) and n == NB:
                    probabilities(n - 1, 1 - u)
                act.wait_ge(y_done, 2 + n + 1)
                act.wait_ge(y_stored[u], 16 * j)
                nc.scalar.copy(y[:, u, :, :].rearrange("p t d -> p (t d)"), y_ps[:, :]).then_inc(y_copied, 1)
                act.wait_ge(y_copied, n + 1)
                act.dma_start(expert_rows[bass.ds(n, 1), :, :].rearrange("a (t p) d -> p (a t) d", p=P),
                              y[:, u, :, :]).then_inc(y_stored[u], 16)
            both(act, body)
            for u in range(2):
                act.wait_ge(y_stored[u], 16 * N_TILE // 2)

        @block.tensor
        def _(pe):
            pe.wait_ge(consts, 2)
            pe.wait_ge(w_scaled, 1)

            def transpose_rows(n, u, j):
                pe.wait_ge(rows_loaded[u], 16 * (j + 1))
                pe.wait_ge(rT_copied, n)
                for k in range(KD):
                    for t in range(RT):
                        last = nc.tensor.transpose(rT_ps[:, k * ROW_TILE + t * P:k * ROW_TILE + (t + 1) * P],
                                                   rows[:, u, t, k * P:(k + 1) * P], ident[:, :])
                last.then_inc(rT_done, 1)

            def transpose_block(n, u, j):
                pe.wait_ge(xn_loaded[u], 16 * (j + 1))
                pe.wait_ge(xT_copied, n)
                for k in range(KD):
                    last = nc.tensor.transpose(xT_ps[:, k * P:(k + 1) * P], xn[:, u, k * P:(k + 1) * P], ident[:, :])
                last.then_inc(xT_done, 1)

            def hidden(n, u, j):
                pe.wait_ge(rT_copied, n + 1)
                pe.wait_ge(w1_loaded[u], 32 * (j + 1))
                for i in range(2):
                    pe.wait_ge(silu_done, 2 * n + i + 1)
                    for f in range(2):
                        for k in range(KD):
                            last = nc.tensor.matmul(hid_ps[i][:, f * ROW_TILE:(f + 1) * ROW_TILE],
                                                    w1[:, u, k, (2 * i + f) * P:(2 * i + f + 1) * P], rT[:, k, :],
                                                    start=k == 0, stop=k == KD - 1)
                    last.then_inc(hid_done, 1)

            def project(n, u):
                pe.wait_ge(xT_copied, n + 1)
                pe.wait_ge(kv_copied, n)
                pe.wait_ge(prod_done, n + 1)
                for k in range(KD):
                    nc.tensor.matmul(qk_ps[u][:, :], xT[:, u, k, :], wqkv[:, k, 0:2, :].rearrange("p a d -> p (a d)"),
                                     start=k == 0, stop=False)
                nc.tensor.matmul(qk_ps[u][:, :], ones_rows[:, :], bias_rows[:, 0:2, :].rearrange("p a d -> p (a d)"),
                                 start=False, stop=True)
                for k in range(KD):
                    nc.tensor.matmul(v_ps[:, 0:D], xT[:, u, k, :], wqkv[:, k, 2, :], start=k == 0, stop=False)
                nc.tensor.matmul(v_ps[:, 0:D], ones_rows[:, :], bias_rows[:, 2, :], start=False, stop=True
                                 ).then_inc(qkv_done, 1)

            transpose_rows(0, 0, 0)
            transpose_block(0, 0, 0)
            pe.wait_ge(bias_loaded, 48)

            def body(n, u, j, has_block, next_tile, next_block):
                hidden(n, u, j)
                if next_tile:
                    transpose_rows(n + 1, 1 - u, j + u)
                if next_block:
                    transpose_block(n + 1, 1 - u, j + u)
                if has_block:
                    project(n, u)
                pe.wait_ge(silu_done, 2 + 2 * n + 2)
                pe.wait_ge(y_copied, n)
                for t in range(RT):
                    for f in range(FB):
                        last = nc.tensor.matmul(y_ps[:, t * D:(t + 1) * D], hid[:, f, t * P:(t + 1) * P], w2[:, u, f, :],
                                                start=f == 0, stop=f == FB - 1)
                last.then_inc(y_done, 1)
            both(pe, body)


def phase5_combine(nc, res_v, attn_v, pos_v, gates_v, expert_rows, out_v):
    with ExitStack() as ctx:
        sb = lambda name, shape, dt=F32: ctx.enter_context(nc.sbuf_tensor(name, shape, dt))
        sem = lambda name: ctx.enter_context(nc.semaphore(name))
        res = sb("p5_res", [P, 2, TT, D])
        attn = sb("p5_attn", [P, 2, TT, D])
        pos = sb("p5_pos", [P, 2, TT, 2], U32)
        gates = sb("p5_gates", [P, 2, TT, 2])
        ye = sb("p5_ye", [P, 2, TT, 2, D])
        acc = sb("p5_acc", [P, 2, TT, D])
        loaded = [sem(f"p5_loaded{i}") for i in range(2)]
        pos_loaded = [sem(f"p5_pos_loaded{i}") for i in range(2)]
        gathered = [sem(f"p5_gathered{i}") for i in range(2)]
        added = sem("p5_added")
        first_done = sem("p5_first_done")
        out_done = sem("p5_out_done")
        stored = [sem(f"p5_stored{i}") for i in range(2)]
        apart = sem("p5_apart")
        block = ctx.enter_context(nc.Block())

        def chunks(eng, body):
            with eng.Fori(0, B) as b:
                for c in range(NC):
                    body(b, c, NC * b + c, c % 2, NC // 2 * b + c // 2)

        @block.sync
        def _(sp):
            def body(b, c, n, s, u):
                wait_apart(sp, out_done, n + 1, apart)
                sp.dma_start(pos[:, s, :, :], pos_v[b, c]).then_inc(pos_loaded[s], 16)
                sp.dma_start(res[:, s, :, :], res_v[b, c]).then_inc(loaded[s], 16)
                sp.dma_start(attn[:, s, :, :], attn_v[b, c]).then_inc(loaded[s], 16)
                sp.dma_start(gates[:, s, :, :], gates_v[b, c]).then_inc(loaded[s], 16)
            chunks(sp, body)

        @block.gpsimd
        def _(pool):
            def body(b, c, n, s, u):
                wait_apart(pool, pos_loaded[s], 16 * (u + 1), apart)
                wait_apart(pool, out_done, n + 1, apart)
                for t in range(TT):
                    for k in range(2):
                        nc.gpsimd.indirect_dma_start(ye[:, s, t, k, :], None, expert_rows,
                                                     bass.IndirectOffsetOnAxis(pos[:, s, t, k:k + 1], 0)
                                                     ).then_inc(gathered[s], 16)
            chunks(pool, body)

        @block.vector
        def _(dve):
            dve.sem_inc(out_done, 2)

            def body(b, c, n, s, u):
                dve.wait_ge(loaded[s], 48 * (u + 1))
                dve.wait_ge(stored[s], 16 * u)
                nc.vector.tensor_tensor(acc[:, s, :, :], res[:, s, :, :], attn[:, s, :, :], ALU.add).then_inc(added, 1)
                dve.wait_ge(gathered[s], 16 * 2 * TT * (u + 1))
                dve.wait_ge(added, n + 1)
                for t in range(TT):
                    last = nc.vector.scalar_tensor_tensor(acc[:, s, t, :], ye[:, s, t, 0, :], gates[:, s, t, 0:1],
                                                          acc[:, s, t, :], ALU.mult, ALU.add)
                last.then_inc(first_done, 1)
                dve.wait_ge(first_done, n + 1)
                for t in range(TT):
                    last = nc.vector.scalar_tensor_tensor(acc[:, s, t, :], ye[:, s, t, 1, :], gates[:, s, t, 1:2],
                                                          acc[:, s, t, :], ALU.mult, ALU.add)
                last.then_inc(out_done, 1)
            chunks(dve, body)

        @block.scalar
        def _(act):
            def body(b, c, n, s, u):
                act.wait_ge(out_done, 2 + n + 1)
                act.dma_start(out_v[b, c], acc[:, s, :, :]).then_inc(stored[s], 16)
            chunks(act, body)
            for s in range(2):
                act.wait_ge(stored[s], 16 * B * NC // 2)


INPUTS = ["attn_x", "attn_Wq", "attn_bq", "attn_Wk", "attn_bk", "attn_Wv", "attn_bv", "ffn_g1", "ffn_Wq", "ffn_Wdkv",
          "ffn_Wuk", "ffn_Wuv", "ffn_Wo", "ffn_g2", "ffn_gate_w", "ffn_w1", "ffn_w2"]


def build(nc, w, out):
    dram = lambda name, shape, dt=F32: nc.dram_tensor(name, shape, dt, kind="Internal").ap()
    xn = dram("xn", [T, D])
    qk = dram("qk_parts", [2, 3, B, D, S], BF16)
    v = dram("v_padded", [B * NG, S, HG * VW])
    o = dram("o_heads", [B * NG, S, HG * DH])
    res = dram("res", [T, D])
    pos = dram("pos", [P, B * NC * TT * 2], U32)
    gates = dram("gates", [B, NC, P, TT * 2])
    table = dram("tile_table", [2, N_TILE], mybir.dt.int32)
    sorted_rows = dram("sorted_rows", [SORTED, D])
    expert_rows = dram("expert_rows", [N_TILE * ROW_TILE, D])
    attn = dram("attn_rows", [T, D])
    by_chunk = lambda a: a.rearrange("(b c t p) d -> b c p t d", b=B, c=NC, p=P)
    by_block = lambda a: a.rearrange("(n p) d -> n p d", p=P)
    x = w["attn_x"].rearrange("b s d -> (b s) d")
    pairs = lambda a: a.rearrange("b c p (t k) -> b c p t k", k=2)

    phase1_project(nc, by_chunk(x), w, by_chunk(xn), qk, v.rearrange("(b g) t v -> b g t v", b=B))
    phase2_attend(nc, qk.rearrange("a p b (h d) t -> a p (b h) d t", d=DH), v, o)
    phase3_route(nc, by_chunk(x), by_chunk(xn), o.rearrange("(b g) (c t p) d -> b c p t g d", b=B, c=NC, p=P), w,
                 sorted_rows, by_chunk(res), pos, pairs(gates), table)
    phase4_experts(nc, by_block(xn), w, sorted_rows, expert_rows.rearrange("(n r) d -> n r d", r=ROW_TILE),
                   by_block(attn), table)
    phase5_combine(nc, by_chunk(res), by_chunk(attn),
                   pos.rearrange("p (b c t k) -> b c p t k", b=B, c=NC, k=2), pairs(gates), expert_rows, by_chunk(out))


def kernel(**inputs):
    import numpy as np
    import concourse.bacc as bacc
    from concourse.bass_utils import run_bass_kernel_spmd

    nc = bacc.Bacc("TRN2", target_bir_lowering=False, num_devices=1)
    arrays, w = {}, {}
    for name in INPUTS:
        a = np.ascontiguousarray(inputs[f"L0_{name}"])
        arrays[name] = a
        w[name] = nc.dram_tensor(name, list(a.shape), mybir.dt.from_np(a.dtype), kind="ExternalInput").ap()
    out = nc.dram_tensor("out", [T, D], F32, kind="ExternalOutput").ap()
    build(nc, w, out)
    r = run_bass_kernel_spmd(nc, [arrays], core_ids=[0])
    return r.results[0]["out"].reshape(B, S, D)
```

```python
from contextlib import ExitStack

import concourse.bass as bass
from concourse import mybir

F32 = mybir.dt.float32
BF16 = mybir.dt.bfloat16
U32 = mybir.dt.uint32
ALU = mybir.AluOpType
ACT = mybir.ActivationFunctionType
AX_X = mybir.AxisListType.X

P = 128
B, S, D = 4, 2048, 256
T = B * S
H, DH = 16, 16
L = 128
E, F = 8, 512
KD = D // P
CT = 512
TT = CT // P
NC = S // CT
HG = 4
NG = H // HG
VW = 32
EPS_LN, EPS_RMS = 1e-5, 1e-6
BIG = 1e30
Q_PART = (0, 0, 1, 1, 0, 2)
K_PART = (0, 1, 0, 1, 2, 0)
SPLIT = DH * len(Q_PART)
ROWS = SPLIT + 2
HEAD_BLOCKS = 2 * B * NG


def wait_apart(eng, sem, value, apart):
    eng.wait_ge(sem, value)
    eng.sem_inc(apart, 1)


def phase1_project(nc, x_v, w, xn_v, qk_parts, v_dram, head_qkv):
    with ExitStack() as ctx:
        sb = lambda name, shape, dt=F32: ctx.enter_context(nc.sbuf_tensor(name, shape, dt))
        sem = lambda name: ctx.enter_context(nc.semaphore(name))
        bank = lambda name: ctx.enter_context(nc.psum_tensor(name, [P, CT], F32))

        ident = sb("p1_ident", [P, P])
        wq = sb("p1_wq", [P, KD, D])
        wdkv = sb("p1_wdkv", [P, KD, L])
        wuk = sb("p1_wuk", [P, D])
        wuv = sb("p1_wuv", [P, D])
        g1 = sb("p1_g1", [P, KD])
        half = sb("p1_minus_half", [P, TT])
        plus_half = sb("p1_plus_half", [P, TT])
        wh = sb("p1_wh", [P, KD, 3, D])
        bh = sb("p1_bh", [P, 3, D])
        heads = sb("p1_heads", [P, 2, TT, 3, D])
        meansq = sb("p1_meansq", [P, TT])
        rms = sb("p1_rms", [P, 2, TT])
        x = sb("p1_x", [P, 2, TT, D])
        xn = sb("p1_xn", [P, 2, TT, D])
        h = sb("p1_h", [P, TT, D])
        hT = sb("p1_hT", [P, 2, KD, CT])
        cT = sb("p1_cT", [P, CT])
        stats = sb("p1_stats", [P, TT, 6])
        mv = sb("p1_mv", [P, TT, 2])
        rstd = sb("p1_rstd", [P, TT])
        sq = sb("p1_sq", [P, TT, D])
        ss = sb("p1_ss", [P, TT])
        rrms = sb("p1_rrms", [P, TT])
        parts = sb("p1_parts", [P, 2, 4, 3, CT], BF16)
        rest = sb("p1_rest", [P, 4, CT])
        vx = sb("p1_vx", [P, 2, TT, H, VW])

        t_ps = [bank(f"p1_t{k}") for k in range(KD)]
        qk_ps = [bank(f"p1_qk{j}") for j in range(2)]
        heads_ps = ctx.enter_context(nc.psum_tensor("p1_heads_ps", [P, 2 * CT], F32))
        c_ps = bank("p1_c")
        v_ps = bank("p1_v")

        w_loaded = sem("p1_w_loaded")
        consts = sem("p1_consts")
        w_scaled = sem("p1_w_scaled")
        x_loaded = [sem(f"p1_x_loaded{s}") for s in range(2)]
        stats_done = sem("p1_stats_done")
        mv_done = sem("p1_mv_done")
        eps_added = sem("p1_eps_added")
        rstd_done = sem("p1_rstd_done")
        xn_done = sem("p1_xn_done")
        ss_done = sem("p1_ss_done")
        mean_done = sem("p1_mean_done")
        rrms_done = sem("p1_rrms_done")
        rms_done = sem("p1_rms_done")
        h_done = sem("p1_h_done")
        t_done = sem("p1_t_done")
        hT_done = sem("p1_hT_done")
        qk_done = sem("p1_qk_done")
        heads_done = sem("p1_heads_done")
        heads_taken = sem("p1_heads_taken")
        heads_stored = [sem(f"p1_heads_stored{s}") for s in range(2)]
        part0_done = sem("p1_part0_done")
        rest_done = sem("p1_rest_done")
        part1_done = sem("p1_part1_done")
        part2_done = sem("p1_part2_done")
        c_done = sem("p1_c_done")
        cT_done = sem("p1_cT_done")
        v_done = sem("p1_v_done")
        vx_done = sem("p1_vx_done")
        xn_stored = [sem(f"p1_xn_stored{s}") for s in range(2)]
        parts_stored = [sem(f"p1_parts_stored{s}") for s in range(2)]
        vx_stored = [sem(f"p1_vx_stored{s}") for s in range(2)]
        apart = sem("p1_apart")
        block = ctx.enter_context(nc.Block())
        N_W = 6

        def chunks(eng, body):
            with eng.Fori(0, B - 1) as b:
                for c in range(NC):
                    body(b, c, NC * b + c, True)
            for c in range(NC):
                body(B - 1, c, NC * (B - 1) + c, c < NC - 1)

        def uses(b, c):
            return (NC // 2) * b + c // 2

        @block.sync
        def _(sp):
            for c in range(2):
                sp.dma_start(x[:, c, :, :], x_v[0, c]).then_inc(x_loaded[c], 16)
            sp.dma_start(wq[:, :, :], w["ffn_Wq"].rearrange("(k p) n -> p k n", p=P)).then_inc(w_loaded, 16)
            sp.dma_start(wdkv[:, :, :], w["ffn_Wdkv"].rearrange("(k p) n -> p k n", p=P)).then_inc(w_loaded, 16)
            sp.dma_start(wuk[:, :], w["ffn_Wuk"]).then_inc(w_loaded, 16)
            sp.dma_start(wuv[:, :], w["ffn_Wuv"]).then_inc(w_loaded, 16)
            with nc.allow_non_contiguous_dma(reason="256 gains, once"):
                sp.dma_start(g1[:, :], w["ffn_g1"].rearrange("(k p) -> p k", p=P)).then_inc(w_loaded, 16)
            for i, name in enumerate(("q", "k", "v")):
                sp.dma_start(wh[:, :, i, :], w[f"attn_W{name}"].rearrange("(k p) n -> p k n", p=P)).then_inc(w_loaded, 16)
                sp.dma_start(bh[:, i, :], w[f"attn_b{name}"].partition_broadcast(P)).then_inc(w_loaded, 16)

            def store_xn(b, c, n):
                wait_apart(sp, xn_done, n + 1, apart)
                sp.dma_start(xn_v[b, c], xn[:, c % 2, :, :]).then_inc(xn_stored[c % 2], 16)

            def load_x(b, c):
                sp.dma_start(x[:, c % 2, :, :], x_v[b, c]).then_inc(x_loaded[c % 2], 16)

            def store_parts(b, c, n, j):
                wait_apart(sp, part2_done, 4 * n + j + 1, apart)
                sp.dma_start(qk_parts[j // 2, :, b, (j % 2) * P:(j % 2 + 1) * P, c * CT:(c + 1) * CT]
                             .rearrange("a p t -> p a t"), parts[:, c % 2, j, :, :]).then_inc(parts_stored[c % 2], 16)

            store_xn(0, 0, 0)
            load_x(0, 2)

            def body(b, c, n, follows):
                s = c % 2
                store_parts(b, c, n, 0)
                store_parts(b, c, n, 1)
                if follows:
                    store_xn(*((b, c + 1) if c + 1 < NC else (b + 1, 0)), n + 1)
                    if c + 3 < NC:
                        load_x(b, c + 3)
                    elif not isinstance(b, int):
                        load_x(b + 1, c + 3 - NC)
                store_parts(b, c, n, 2)
                store_parts(b, c, n, 3)
                wait_apart(sp, heads_taken, TT * n + TT, apart)
                sp.dma_start(head_qkv[b, c], heads[:, s, :, :, :].rearrange("p t i d -> p t (i d)")).then_inc(heads_stored[s], 16)
                wait_apart(sp, vx_done, 2 * n + 2, apart)
                for g in range(NG):
                    sp.dma_start(v_dram[b, g, c * CT:(c + 1) * CT, :].rearrange("(t p) v -> p t v", p=P),
                                 vx[:, s, :, g * HG:(g + 1) * HG, :].rearrange("p t h v -> p t (h v)")
                                 ).then_inc(vx_stored[s], 16)
            chunks(sp, body)
            for s in range(2):
                wait_apart(sp, xn_stored[s], 16 * B * NC // 2, apart)
                wait_apart(sp, parts_stored[s], 16 * 4 * B * NC // 2, apart)
                wait_apart(sp, vx_stored[s], 16 * NG * B * NC // 2, apart)
                wait_apart(sp, heads_stored[s], 16 * B * NC // 2, apart)

        @block.gpsimd
        def _(pool):
            nc.gpsimd.memset(ident[:, :], 0.0).then_inc(consts, 1)
            nc.gpsimd.memset(half[:, :], -0.5)
            nc.gpsimd.memset(plus_half[:, :], 0.5).then_inc(consts, 1)
            nc.gpsimd.memset(vx[:, :, :, :, :], 0.0).then_inc(consts, 1)
            wait_apart(pool, consts, 3, apart)
            nc.gpsimd.affine_select(out=ident[:, :], in_=ident[:, :], compare_op=ALU.not_equal, fill=1.0,
                                    base=0, pattern=[[-1, P]], channel_multiplier=1).then_inc(consts, 1)
            nc.gpsimd.memset(vx[:, :, :, :, DH:DH + 1], 1.0).then_inc(consts, 1)

            def inverse_std(n):
                wait_apart(pool, mv_done, n + 1, apart)
                nc.gpsimd.tensor_scalar(rstd[:, :], mv[:, :, 1], EPS_LN, None, ALU.add).then_inc(eps_added, 1)
                wait_apart(pool, eps_added, n + 1, apart)
                nc.gpsimd.tensor_tensor(rstd[:, :], rstd[:, :], half[:, :], ALU.pow).then_inc(rstd_done, 1)

            def inverse_rms(n, s):
                wait_apart(pool, ss_done, n + 1, apart)
                nc.gpsimd.tensor_scalar(meansq[:, :], ss[:, :], 1.0 / D, EPS_RMS, ALU.mult, ALU.add).then_inc(mean_done, 1)
                wait_apart(pool, mean_done, n + 1, apart)
                nc.gpsimd.tensor_tensor(rrms[:, :], meansq[:, :], half[:, :], ALU.pow).then_inc(rrms_done, 1)
                nc.gpsimd.tensor_tensor(rms[:, s, :], meansq[:, :], plus_half[:, :], ALU.pow).then_inc(rms_done, 1)

            def lower_parts(n, s, j):
                wait_apart(pool, rest_done, 2 + 4 * n + j + 1, apart)
                nc.gpsimd.tensor_copy(parts[:, s, j, 1, :], rest[:, j, :]).then_inc(part1_done, 1)
                wait_apart(pool, part1_done, 4 * n + j + 1, apart)
                nc.gpsimd.tensor_tensor(parts[:, s, j, 2, :], rest[:, j, :], parts[:, s, j, 1, :],
                                        ALU.subtract).then_inc(part2_done, 1)

            inverse_std(0)
            inverse_rms(0, 0)

            def body(b, c, n, follows):
                if follows:
                    inverse_std(n + 1)
                lower_parts(n, c % 2, 0)
                lower_parts(n, c % 2, 1)
                if follows:
                    inverse_rms(n + 1, (c + 1) % 2)
                lower_parts(n, c % 2, 2)
                lower_parts(n, c % 2, 3)
            chunks(pool, body)

        @block.vector
        def _(dve):
            dve.sem_inc(rest_done, 2)
            dve.wait_ge(w_loaded, 16 * 11)
            nc.vector.tensor_scalar(wh[:, :, 0, :], wh[:, :, 0, :], DH ** -0.5, None, ALU.mult)
            nc.vector.tensor_scalar(bh[:, 0, :], bh[:, 0, :], DH ** -0.5, None, ALU.mult)
            for k in range(KD):
                nc.vector.tensor_scalar(wq[:, k, :], wq[:, k, :], g1[:, k:k + 1], DH ** -0.5, ALU.mult, ALU.mult)
                last = nc.vector.tensor_scalar(wdkv[:, k, :], wdkv[:, k, :], g1[:, k:k + 1], None, ALU.mult)
            last.then_inc(w_scaled, 1)

            def moments(n, s, u):
                dve.wait_ge(x_loaded[s], 16 * (u + 1))
                for t in range(TT):
                    last = nc.vector.bn_stats(stats[:, t, :], x[:, s, t, :])
                last.then_inc(stats_done, 1)
                wait_apart(dve, stats_done, n + 1, apart)
                for t in range(TT):
                    last = nc.vector.bn_aggr(mv[:, t, :], stats[:, t, :])
                last.then_inc(mv_done, 1)

            def normalise(n, s, u):
                dve.wait_ge(rstd_done, n + 1)
                dve.wait_ge(xn_stored[s], 16 * u)
                for t in range(TT):
                    last = nc.vector.tensor_scalar(xn[:, s, t, :], x[:, s, t, :], mv[:, t, 0:1], rstd[:, t:t + 1],
                                                   ALU.subtract, ALU.mult)
                last.then_inc(xn_done, 1)

            def scale_rms(n, s):
                dve.wait_ge(rrms_done, n + 1)
                dve.wait_ge(t_done, KD * n)
                for t in range(TT):
                    last = nc.vector.tensor_scalar(h[:, t, :], xn[:, s, t, :], rrms[:, t:t + 1], None, ALU.mult)
                last.then_inc(h_done, 1)

            def subtract_part0(n, s, j):
                dve.wait_ge(part0_done, 4 * n + j + 1)
                dve.wait_ge(part2_done, 4 * n)
                nc.vector.tensor_tensor(rest[:, j, :], qk_ps[j % 2][:, :], parts[:, s, j, 0, :],
                                        ALU.subtract).then_inc(rest_done, 1)

            def take_heads(n, s, u, t):
                dve.wait_ge(heads_done, TT * n + t + 1)
                if t == 0:
                    dve.wait_ge(rms_done, n + 1)
                    dve.wait_ge(heads_stored[s], 16 * u)
                nc.vector.scalar_tensor_tensor(heads[:, s, t, :, :].rearrange("p i d -> p (i d)"), heads_ps[:, 0:3 * D],
                                               rms[:, s, t:t + 1], bh[:, :, :].rearrange("p i d -> p (i d)"),
                                               ALU.mult, ALU.add).then_inc(heads_taken, 1)

            moments(0, 0, 0)
            normalise(0, 0, 0)
            scale_rms(0, 0)
            dve.wait_ge(w_scaled, 1)

            def body(b, c, n, follows):
                s, s1 = c % 2, (c + 1) % 2
                u, u1 = uses(b, c), uses(b, c + 1)
                if follows:
                    moments(n + 1, s1, u1)
                subtract_part0(n, s, 0)
                take_heads(n, s, u, 0)
                if follows:
                    normalise(n + 1, s1, u1)
                subtract_part0(n, s, 1)
                take_heads(n, s, u, 1)
                take_heads(n, s, u, 2)
                if follows:
                    scale_rms(n + 1, s1)
                subtract_part0(n, s, 2)
                subtract_part0(n, s, 3)
                take_heads(n, s, u, 3)
            chunks(dve, body)

        @block.scalar
        def _(act):
            def squares(n, s):
                act.wait_ge(xn_done, n + 1)
                act.wait_ge(mean_done, n)
                for t in range(TT):
                    last = nc.scalar.activation(sq[:, t, :], xn[:, s, t, :], ACT.Square, accum_out=ss[:, t:t + 1])
                last.then_inc(ss_done, 1)

            def part0(b, c, n, s, j):
                act.wait_ge(qk_done, 4 * n + j + 1)
                act.wait_ge(parts_stored[s], 64 * uses(b, c))
                nc.scalar.copy(parts[:, s, j, 0, :], qk_ps[j % 2][:, :]).then_inc(part0_done, 1)

            def copy_hT(n, s):
                for k in range(KD):
                    act.wait_ge(t_done, KD * n + k + 1)
                    nc.scalar.copy(hT[:, s, k, :], t_ps[k][:, :]).then_inc(hT_done, 1)

            act.wait_ge(consts, 5)
            squares(0, 0)
            copy_hT(0, 0)

            def body(b, c, n, follows):
                s = c % 2
                part0(b, c, n, s, 0)
                if follows:
                    squares(n + 1, (c + 1) % 2)
                part0(b, c, n, s, 1)
                act.wait_ge(c_done, n + 1)
                act.wait_ge(v_done, 2 * n)
                nc.scalar.copy(cT[:, :], c_ps[:, :]).then_inc(cT_done, 1)
                part0(b, c, n, s, 2)
                part0(b, c, n, s, 3)
                if follows:
                    act.wait_ge(heads_done, TT * n)
                    copy_hT(n + 1, (c + 1) % 2)
                act.wait_ge(vx_stored[s], 16 * NG * uses(b, c))
                for i in range(2):
                    act.wait_ge(v_done, 2 * n + i + 1)
                    nc.scalar.copy(vx[:, s, 2 * i:2 * i + 2, :, 0:DH],
                                   v_ps[:, :].rearrange("p (t h d) -> p t h d", t=2, h=H)).then_inc(vx_done, 1)
            chunks(act, body)

        @block.tensor
        def _(pe):
            def transpose_h(n):
                pe.wait_ge(h_done, n + 1)
                pe.wait_ge(hT_done, KD * n)
                for k in range(KD):
                    for t in range(TT):
                        last = nc.tensor.transpose(t_ps[k][:, t * P:(t + 1) * P], h[:, t, k * P:(k + 1) * P], ident[:, :])
                    last.then_inc(t_done, 1)

            def queries(n, s, m):
                pe.wait_ge(rest_done, 4 * n + m + 1)
                for k in range(KD):
                    last = nc.tensor.matmul(qk_ps[m][:, :], wq[:, k, m * P:(m + 1) * P], hT[:, s, k, :],
                                            start=k == 0, stop=k == KD - 1)
                last.then_inc(qk_done, 1)

            def keys(n, m):
                pe.wait_ge(cT_done, n + 1)
                pe.wait_ge(rest_done, 4 * n + 2 + m + 1)
                nc.tensor.matmul(qk_ps[m][:, :], wuk[:, m * P:(m + 1) * P], cT[:, :],
                                 start=True, stop=True).then_inc(qk_done, 1)

            def head_rows(n, s, t):
                pe.wait_ge(heads_taken, TT * n + t)
                for k in range(KD):
                    nc.tensor.matmul(heads_ps[:, 0:2 * D], hT[:, s, k, t * P:(t + 1) * P],
                                     wh[:, k, 0:2, :].rearrange("p i d -> p (i d)"), start=k == 0, stop=k == KD - 1)
                for k in range(KD):
                    last = nc.tensor.matmul(heads_ps[:, 2 * D:3 * D], hT[:, s, k, t * P:(t + 1) * P], wh[:, k, 2, :],
                                            start=k == 0, stop=k == KD - 1)
                last.then_inc(heads_done, 1)

            pe.wait_ge(consts, 5)
            transpose_h(0)
            pe.wait_ge(w_scaled, 1)

            def body(b, c, n, follows):
                s = c % 2
                pe.wait_ge(hT_done, KD * n + KD)
                queries(n, s, 0)
                head_rows(n, s, 0)
                queries(n, s, 1)
                pe.wait_ge(cT_done, n)
                for k in range(KD):
                    last = nc.tensor.matmul(c_ps[:, :], wdkv[:, k, :], hT[:, s, k, :], start=k == 0, stop=k == KD - 1)
                last.then_inc(c_done, 1)
                head_rows(n, s, 1)
                keys(n, 0)
                head_rows(n, s, 2)
                keys(n, 1)
                if follows:
                    transpose_h(n + 1)
                head_rows(n, s, 3)
                for i in range(2):
                    pe.wait_ge(vx_done, 2 * n + i)
                    for t in range(2):
                        tok = (2 * i + t) * P
                        last = nc.tensor.matmul(v_ps[:, t * D:(t + 1) * D], cT[:, tok:tok + P], wuv[:, :],
                                                start=True, stop=True)
                    last.then_inc(v_done, 1)
            chunks(pe, body)


def phase2_attend(nc, qk_heads, v_dram, o_dram, head_qkv, attn_rows):
    UNITS = HEAD_BLOCKS // 2
    assert UNITS == B * NG
    KT = S // P
    STEPS = [(c, kt) for c in range(NC) for kt in range(TT * (c + 1))]
    N_STEP = len(STEPS)
    LAST = [max(i for i, (c, _) in enumerate(STEPS) if c == cc) for cc in range(NC)]
    PIECES = [(hh, i, pc, min(CT, (i + 1) * P - pc * CT))
              for hh in range(HG) for i in range(KT) for pc in range(i // TT + 1)]
    N_PIECE = len(PIECES)
    SLOTS = 3
    RING = 3
    LAG = 2
    AHEAD = 3
    skipped = lambda c, kt: max(0, kt - TT * c) * P
    step_cost = [CT // 8 + CT - skipped(c, kt) for c, kt in STEPS[:N_STEP - AHEAD]]
    piece_cost = [P + width for *_, width in PIECES]
    PIECES_BY = [sum(sum(piece_cost[:m + 1]) * sum(step_cost) <= sum(step_cost[:i + 1]) * sum(piece_cost)
                     for m in range(N_PIECE)) for i in range(N_STEP)]
    assert PIECES_BY[N_STEP - AHEAD - 1] == N_PIECE

    with ExitStack() as ctx:
        sb = lambda name, shape, dt=F32: ctx.enter_context(nc.sbuf_tensor(name, shape, dt))
        sem = lambda name: ctx.enter_context(nc.semaphore(name))

        ident = sb("p2_ident", [P, P])
        ident_b = sb("p2_ident_b", [P, P], BF16)
        mask_q = sb("p2_mask_q", [P, P], BF16)
        mask_k = sb("p2_mask_k", [P, P], BF16)
        q6 = [sb(f"p2_q6_{s}", [ROWS, HG, S], BF16) for s in range(SLOTS)]
        k6 = [sb(f"p2_k6_{s}", [ROWS, HG, S], BF16) for s in range(SLOTS)]
        vg = [sb(f"p2_vg_{s}", [P, KT, HG * VW]) for s in range(SLOTS)]
        probs = sb("p2_probs", [P, 2 * (LAG + 1), 2, CT])
        piece_max = sb("p2_piece_max", [P, HG * KT, NC])
        neg_max = sb("p2_neg_max", [P, P])
        neg_hi = sb("p2_neg_hi", [HG * KT, P], BF16)
        neg_lo = sb("p2_neg_lo", [HG * KT, P], BF16)
        pv_sb = sb("p2_pv_sb", [P, CT])
        inv = sb("p2_inv", [P, TT * HG])
        o_sb = sb("p2_o", [P, 2, TT, HG * DH])

        head_in = sb("p2_head_in", [P, 2, 3, H, DH])
        terms = sb("p2_terms", [P, H, H, DH])
        head_s = sb("p2_head_s", [P, 2, H, H])
        head_max = sb("p2_head_max", [P, H])
        head_p = sb("p2_head_p", [P, 2, H, H])
        head_sum = sb("p2_head_sum", [P, H, H // 2])
        head_inv = sb("p2_head_inv", [P, H])
        minus_one = sb("p2_minus_one", [P, H])
        head_o = sb("p2_head_o", [P, 2, H, DH])

        ring_ps = [ctx.enter_context(nc.psum_tensor(f"p2_ring{i}", [P, CT], F32)) for i in range(RING)]
        st_ps = [ctx.enter_context(nc.psum_tensor(f"p2_st{i}", [P, 2, CT], F32)) for i in range(2)]
        pv_ps = ctx.enter_context(nc.psum_tensor("p2_pv", [P, CT], F32))

        consts = sem("p2_consts")
        loaded = [sem(f"p2_loaded{s}") for s in range(SLOTS)]
        ring_filled = sem("p2_ring_filled")
        ring_free = sem("p2_ring_free")
        neg_max_done = sem("p2_neg_max_done")
        neg_hi_done = sem("p2_neg_hi_done")
        neg_rows_done = sem("p2_neg_rows_done")
        neg_stored = sem("p2_neg_stored")
        st_scored = sem("p2_st_scored")
        probs_done = sem("p2_probs_done")
        pv_done = sem("p2_pv_done")
        pv_copied = sem("p2_pv_copied")
        inv_done = sem("p2_inv_done")
        o_done = sem("p2_o_done")
        head_loaded = [sem(f"p2_head_loaded{s}") for s in range(2)]
        head_steps = sem("p2_head_steps")
        head_scored = sem("p2_head_scored")
        head_max_done = sem("p2_head_max_done")
        head_shifted = sem("p2_head_shifted")
        head_probs_done = sem("p2_head_probs_done")
        head_done = sem("p2_head_done")
        head_stored = [sem(f"p2_head_stored{s}") for s in range(2)]
        o_stored = [sem(f"p2_o_stored{s}") for s in range(2)]
        apart = sem("p2_apart")
        block = ctx.enter_context(nc.Block())

        N_LOAD = 16 * (2 * len(Q_PART) + 2)
        SHIFT_AT = (1, 8)

        def turn_of(s, i):
            return (N_STEP * s + i) % (LAG + 1)
        assert SLOTS * N_STEP % (LAG + 1) == 0

        unit_items = []
        for i in range(N_STEP):
            unit_items += [("piece", m) for m in range(PIECES_BY[i - 1] if i else 0, PIECES_BY[i])]
            unit_items += [("o", c) for c in range(NC - 1) if i == LAST[c] + LAG + 1]
            unit_items += [("maxima", 0)] if i == N_STEP - AHEAD + 1 else []
        unit_items.append(("o", NC - 1))
        last_items = [item for item in unit_items if item[0] == "o"]
        FIRST = N_PIECE + 1
        assert len(unit_items) % RING == 0

        def ring_item(n, has_next, what, k):
            r = (unit_items if has_next else last_items).index((what, k))
            return FIRST + len(unit_items) * n + r, (FIRST + r) % RING

        def units(eng, body):
            with eng.Fori(0, (UNITS - 1) // SLOTS) as j:
                for s in range(SLOTS):
                    body(SLOTS * j + s, s, True, j)
            body(UNITS - 1, (UNITS - 1) % SLOTS, False, (UNITS - 1) // SLOTS)

        def next_round(j, s):
            return j + (s + 1) // SLOTS

        def load(sp, n, s):
            for g, (a, k) in enumerate(zip(Q_PART, K_PART)):
                sp.dma_start(q6[s][g * DH:(g + 1) * DH, :, :],
                             qk_heads[0, a, bass.ds(n * HG, HG), :, :].rearrange("h d t -> d h t")).then_inc(loaded[s], 16)
                sp.dma_start(k6[s][g * DH:(g + 1) * DH, :, :],
                             qk_heads[1, k, bass.ds(n * HG, HG), :, :].rearrange("h d t -> d h t")).then_inc(loaded[s], 16)
            for i in range(2):
                half = slice(i * S // 2, (i + 1) * S // 2)
                sp.dma_start(vg[s][:, i * KT // 2:(i + 1) * KT // 2, :],
                             v_dram[bass.ds(n, 1), half, :].rearrange("a (k p) v -> p (a k) v", p=P)).then_inc(loaded[s], 16)

        @block.sync
        def _(sp):
            def store_neg_rows(n, s):
                wait_apart(sp, neg_rows_done, n + 1, apart)
                for r, part in enumerate((neg_hi, neg_lo)):
                    sp.dma_start(q6[s][SPLIT + r:SPLIT + r + 1, :, :].rearrange("a h (i p) -> a (h i) p", p=P),
                                 part[:, :]).then_inc(neg_stored, 16)

            def store_o(n, c):
                wait_apart(sp, o_done, NC * n + c + 1, apart)
                sp.dma_start(o_dram[bass.ds(n, 1), c * CT:(c + 1) * CT, :].rearrange("a (t p) d -> p (a t) d", p=P),
                             o_sb[:, c % 2, :, :]).then_inc(o_stored[c % 2], 16)

            load(sp, 0, 0)
            load(sp, 1, 1)
            store_neg_rows(0, 0)

            def body(n, s, loads, has_next):
                if loads:
                    wait_apart(sp, pv_done, LAG + 1 + N_STEP * n, apart)
                    load(sp, n + 2, (s + 2) % SLOTS)
                for c in range(NC - 1):
                    store_o(n, c)
                if has_next:
                    store_neg_rows(n + 1, (s + 1) % SLOTS)
                store_o(n, NC - 1)
            rounds = (UNITS - 2) // SLOTS
            with sp.Fori(0, rounds) as j:
                for s in range(SLOTS):
                    body(SLOTS * j + s, s, True, True)
            for n in range(SLOTS * rounds, UNITS):
                body(n, n % SLOTS, n + 2 < UNITS, n + 1 < UNITS)
            for s in range(2):
                wait_apart(sp, o_stored[s], 16 * UNITS * NC // 2, apart)

        @block.gpsimd
        def _(pool):
            nc.gpsimd.memset(ident[:, :], 0.0)
            nc.gpsimd.memset(ident_b[:, :], 0.0)
            nc.gpsimd.memset(mask_q[:, :], 0.0)
            nc.gpsimd.memset(mask_k[:, :], 0.0)
            nc.gpsimd.memset(neg_max[:, :], 0.0)
            nc.gpsimd.memset(piece_max[:, :, :], -3e38).then_inc(consts, 1)
            wait_apart(pool, consts, 1, apart)
            for m in (ident, ident_b):
                nc.gpsimd.affine_select(out=m[:, :], in_=m[:, :], compare_op=ALU.not_equal, fill=1.0,
                                        base=0, pattern=[[-1, P]], channel_multiplier=1)
            nc.gpsimd.affine_select(out=mask_q[:, :], in_=mask_q[:, :], compare_op=ALU.is_ge, fill=-BIG,
                                    base=0, pattern=[[-1, P]], channel_multiplier=1)
            nc.gpsimd.affine_select(out=mask_k[:, :], in_=mask_k[:, :], compare_op=ALU.is_ge, fill=-BIG,
                                    base=0, pattern=[[1, P]], channel_multiplier=-1).then_inc(consts, 1)
            for s in range(SLOTS):
                wait_apart(pool, consts, 2 + s, apart)
                nc.gpsimd.memset(k6[s][SPLIT:ROWS, :, :], 1.0).then_inc(consts, 1)

            wait_apart(pool, consts, 2 + SLOTS, apart)
            nc.gpsimd.memset(minus_one[:, :], -1.0).then_inc(head_steps, 1)
            STEPS_A, STEPS_B = 4, 10

            def steps(scored, weighed):
                return 1 + STEPS_A * scored + STEPS_B * weighed

            def load_heads(m, u):
                pool.dma_start(head_in[:, u, :, :, :].rearrange("p i h d -> p (i h d)"),
                               head_qkv[bass.ds(m, 1), :, :].rearrange("a p d -> p (a d)")).then_inc(head_loaded[u], 16)

            def step(ins, count):
                ins.then_inc(head_steps, 1)
                wait_apart(pool, head_steps, count, apart)

            def score_heads(m, u, loads, before):
                wait_apart(pool, head_loaded[u], 16 * loads, apart)
                step(nc.gpsimd.tensor_tensor(
                    terms[:, :, :, :], head_in[:, u, 0, :, :].unsqueeze(2).to_broadcast([P, H, H, DH]),
                    head_in[:, u, 1, :, :].unsqueeze(1).to_broadcast([P, H, H, DH]), ALU.mult), before + 1)
                width = DH // 2
                for k in range(STEPS_A - 1):
                    step(nc.gpsimd.tensor_tensor(terms[:, :, :, 0:width], terms[:, :, :, 0:width],
                                                 terms[:, :, :, width:2 * width], ALU.add), before + 2 + k)
                    width //= 2
                nc.gpsimd.tensor_tensor(head_s[:, u, :, :], terms[:, :, :, 0], terms[:, :, :, 1], ALU.add
                                        ).then_inc(head_scored, 1)
                wait_apart(pool, head_scored, m + 1, apart)

            def weigh_heads(m, u, stores, before):
                wait_apart(pool, head_probs_done, m + 1, apart)
                step(nc.gpsimd.tensor_tensor(
                    terms[:, :, :, :], head_p[:, u, :, :].unsqueeze(2).to_broadcast([P, H, DH, H]),
                    head_in[:, u, 2, :, :].rearrange("p j d -> p d j").unsqueeze(1).to_broadcast([P, H, DH, H]),
                    ALU.mult), before + 1)
                width = H // 2
                for k in range(3):
                    step(nc.gpsimd.tensor_tensor(terms[:, :, :, 0:width], terms[:, :, :, 0:width],
                                                 terms[:, :, :, width:2 * width], ALU.add), before + 2 + k)
                    width //= 2
                src, width = head_p[:, u, :, :], H // 2
                for k in range(4):
                    step(nc.gpsimd.tensor_tensor(head_sum[:, :, 0:width], src[:, :, 0:width],
                                                 src[:, :, width:2 * width], ALU.add), before + 5 + k)
                    src, width = head_sum[:, :, :], width // 2
                step(nc.gpsimd.tensor_tensor(head_inv[:, :], head_sum[:, :, 0], minus_one[:, :], ALU.pow), before + 9)
                wait_apart(pool, head_stored[u], 16 * stores, apart)
                step(nc.gpsimd.tensor_tensor(head_o[:, u, :, :], terms[:, :, :, 0], terms[:, :, :, 1], ALU.add), before + 10)
                nc.gpsimd.tensor_tensor(head_o[:, u, :, :], head_o[:, u, :, :],
                                        head_inv[:, :].unsqueeze(2).to_broadcast([P, H, DH]), ALU.mult).then_inc(head_done, 1)
                wait_apart(pool, head_done, 2 + m + 1, apart)
                pool.dma_start(attn_rows[bass.ds(m, 1), :, :].rearrange("a p d -> p (a d)"),
                               head_o[:, u, :, :].rearrange("p h d -> p (h d)")).then_inc(head_stored[u], 16)

            wait_apart(pool, head_steps, 1, apart)
            load_heads(0, 0)
            load_heads(1, 1)
            for u in range(2):
                score_heads(u, u, 1, steps(u, 0))
            with pool.Fori(0, UNITS - 1) as n:
                for u in range(2):
                    weigh_heads(2 * n + u, u, n, steps(2 * n + 2, 2 * n + u))
                    load_heads(2 * n + 2 + u, u)
                for u in range(2):
                    score_heads(2 * n + 2 + u, u, n + 2, steps(2 * n + 2 + u, 2 * n + 2))
            for u in range(2):
                weigh_heads(2 * (UNITS - 1) + u, u, UNITS - 1, steps(2 * UNITS, 2 * (UNITS - 1) + u))
            for u in range(2):
                wait_apart(pool, head_stored[u], 16 * UNITS, apart)

        @block.vector
        def _(dve):
            dve.sem_inc(ring_free, RING)
            dve.sem_inc(head_done, 2)
            dve.wait_ge(consts, 2)

            def reduce_piece(m, g, bank):
                hh, i, pc, width = PIECES[m]
                dve.wait_ge(ring_filled, g + 1)
                nc.vector.tensor_reduce(piece_max[:, hh * KT + i, pc:pc + 1], ring_ps[bank][:, 0:width], AX_X,
                                        ALU.max).then_inc(ring_free, 1)

            def reduce_pieces(n, last_piece):
                dve.wait_ge(ring_free, RING + last_piece + 1)
                nc.vector.tensor_reduce(neg_max[:, 0:HG * KT], piece_max[:, :, :], AX_X, ALU.max, negate=True
                                        ).then_inc(neg_max_done, 1)

            def split_maxima(n, g, bank):
                dve.wait_ge(ring_filled, g + 1)
                dve.wait_ge(neg_stored, 32 * n)
                nc.vector.tensor_copy(neg_hi[:, :], ring_ps[bank][0:HG * KT, 0:P]).then_inc(neg_hi_done, 1)
                dve.wait_ge(neg_hi_done, n + 1)
                nc.vector.tensor_tensor(neg_lo[:, :], ring_ps[bank][0:HG * KT, 0:P], neg_hi[:, :], ALU.subtract
                                        ).then_inc(neg_rows_done, 1)
                dve.wait_ge(neg_rows_done, n + 1)
                dve.sem_inc(ring_free, 1)

            def normalise(n, c, g, bank):
                dve.wait_ge(ring_filled, g + 1)
                tr = ring_ps[bank][:, :].rearrange("p (g v) -> p g v", v=VW)
                nc.vector.reciprocal(inv[:, :], tr[:, :, DH]).then_inc(inv_done, 1)
                dve.wait_ge(inv_done, NC * n + c + 1)
                dve.wait_ge(o_stored[c % 2], 16 * (NC // 2 * n + c // 2))
                nc.vector.tensor_tensor(o_sb[:, c % 2, :, :].rearrange("p t (h d) -> p (t h) d", d=DH), tr[:, :, 0:DH],
                                        inv[:, :].unsqueeze(2).to_broadcast([P, TT * HG, DH]), ALU.mult
                                        ).then_inc(o_done, 1)
                dve.wait_ge(o_done, NC * n + c + 1)
                dve.sem_inc(ring_free, 1)

            def shift_heads(m, u):
                dve.wait_ge(head_scored, m + 1)
                nc.vector.tensor_reduce(head_max[:, :], head_s[:, u, :, :], AX_X, ALU.max).then_inc(head_max_done, 1)
                dve.wait_ge(head_max_done, m + 1)
                nc.vector.tensor_tensor(head_s[:, u, :, :], head_s[:, u, :, :],
                                        head_max[:, :].unsqueeze(2).to_broadcast([P, H, H]), ALU.subtract
                                        ).then_inc(head_shifted, 1)

            for m in range(N_PIECE):
                reduce_piece(m, m, m % RING)
            reduce_pieces(0, N_PIECE - 1)
            split_maxima(0, N_PIECE, N_PIECE % RING)

            def body(n, s, has_next, j):
                item = lambda what, k=0: ring_item(n, has_next, what, k)
                done = 0
                for i in range(N_STEP):
                    if i in SHIFT_AT:
                        u = SHIFT_AT.index(i)
                        shift_heads(2 * n + u, u)
                    upto = PIECES_BY[i] if has_next else 0
                    for m in range(done, upto):
                        reduce_piece(m, *item("piece", m))
                    if done < upto == N_PIECE:
                        reduce_pieces(n + 1, item("piece", N_PIECE - 1)[0])
                    done = upto
                    for c in range(NC - 1):
                        if i == LAST[c] + LAG + 1:
                            normalise(n, c, *item("o", c))
                    if has_next and i == N_STEP - AHEAD + 1:
                        split_maxima(n + 1, *item("maxima"))
                normalise(n, NC - 1, *item("o", NC - 1))
            units(dve, body)

        @block.scalar
        def _(act):
            act.sem_inc(pv_done, LAG + 1)
            act.sem_inc(probs_done, 2)

            def exps(n, s, i, u):
                c, kt = STEPS[i]
                width = CT - max(0, kt - TT * c) * P
                act.wait_ge(st_scored, 2 * (N_STEP * n + i) + u + 1)
                act.wait_ge(pv_done, N_STEP * n + i + 1)
                nc.scalar.activation(probs[:, 2 * turn_of(s, i) + u, :, 0:width], st_ps[u][:, :, 0:width], ACT.Exp
                                     ).then_inc(probs_done, 1)

            def head_probs(m, u):
                act.wait_ge(head_shifted, m + 1)
                act.wait_ge(head_done, m + 1)
                nc.scalar.activation(head_p[:, u, :, :], head_s[:, u, :, :], ACT.Exp).then_inc(head_probs_done, 1)

            def copy_pv(n, c, has_next):
                act.wait_ge(pv_done, LAG + 1 + N_STEP * n + LAST[c] + 1)
                before = ring_item(n, has_next, "o", c - 1)[0] if c else FIRST + len(unit_items) * n - 1
                act.wait_ge(ring_filled, before + 1)
                nc.scalar.copy(pv_sb[:, :], pv_ps[:, :]).then_inc(pv_copied, 1)

            def body(n, s, has_next, j):
                for i in range(N_STEP):
                    if i - 2 in SHIFT_AT:
                        u = SHIFT_AT.index(i - 2)
                        head_probs(2 * n + u, u)
                    exps(n, s, i, 0)
                    exps(n, s, i, 1)
                    for c in range(NC - 1):
                        if i == LAST[c] + LAG:
                            copy_pv(n, c, has_next)
                copy_pv(n, NC - 1, has_next)
            units(act, body)

        @block.tensor
        def _(pe):
            def row_scores(s, m, rnd, g, bank):
                hh, i, pc, width = PIECES[m]
                if m == 0:
                    pe.wait_ge(loaded[s], N_LOAD * (rnd + 1))
                pe.wait_ge(ring_free, g + 1)
                diagonal = pc == i // TT
                out = ring_ps[bank]
                last = nc.tensor.matmul(out[:, 0:width], q6[s][0:SPLIT, hh, i * P:(i + 1) * P],
                                        k6[s][0:SPLIT, hh, pc * CT:pc * CT + width], start=True, stop=not diagonal)
                if diagonal:
                    last = nc.tensor.matmul(out[:, width - P:width], ident_b[:, :], mask_q[:, :], start=False, stop=True)
                last.then_inc(ring_filled, 1)

            def transpose_max(n, g, bank):
                pe.wait_ge(neg_max_done, n + 1)
                pe.wait_ge(ring_free, g + 1)
                nc.tensor.transpose(ring_ps[bank][:, 0:P], neg_max[:, :], ident[:, :]).then_inc(ring_filled, 1)

            def scores(n, s, i, u):
                c, kt = STEPS[i]
                skip = max(0, kt - TT * c) * P
                width = CT - skip
                if i == 0 and u == 0:
                    pe.wait_ge(neg_stored, 32 * (n + 1))
                    pe.wait_ge(consts, 2 + SLOTS)
                pe.wait_ge(probs_done, 2 * (N_STEP * n + i) + u + 1)
                diagonal = kt >= TT * c
                for j in range(2):
                    hh = 2 * u + j
                    last = nc.tensor.matmul(st_ps[u][:, j, 0:width], k6[s][:, hh, kt * P:(kt + 1) * P],
                                            q6[s][:, hh, c * CT + skip:(c + 1) * CT], start=True, stop=not diagonal)
                    if diagonal:
                        last = nc.tensor.matmul(st_ps[u][:, j, 0:P], ident_b[:, :], mask_k[:, :], start=False, stop=True)
                last.then_inc(st_scored, 1)

            def values(n, s, i):
                c, kt = STEPS[i]
                skip = max(0, kt - TT * c) * P
                if kt == 0:
                    pe.wait_ge(pv_copied, NC * n + c)
                pe.wait_ge(probs_done, 2 + 2 * (N_STEP * n + i) + 2)
                for hh in range(HG):
                    last = nc.tensor.matmul(pv_ps[hh * VW:(hh + 1) * VW, skip:CT], vg[s][:, kt, hh * VW:(hh + 1) * VW],
                                            probs[:, 2 * turn_of(s, i) + hh // 2, hh % 2, 0:CT - skip],
                                            start=kt == 0, stop=kt == TT * (c + 1) - 1, skip_group_check=True)
                last.then_inc(pv_done, 1)

            def transpose_o(n, c, g, bank):
                pe.wait_ge(pv_copied, NC * n + c + 1)
                pe.wait_ge(ring_free, g + 1)
                for t in range(TT):
                    last = nc.tensor.transpose(ring_ps[bank][:, t * P:(t + 1) * P], pv_sb[:, t * P:(t + 1) * P], ident[:, :])
                last.then_inc(ring_filled, 1)

            pe.wait_ge(consts, 2)

            for m in range(N_PIECE):
                row_scores(0, m, 0, m, m % RING)
            transpose_max(0, N_PIECE, N_PIECE % RING)

            def body(n, s, has_next, j):
                item = lambda what, k=0: ring_item(n, has_next, what, k)

                def maxima(first, end):
                    for m in range(first, end):
                        row_scores((s + 1) % SLOTS, m, next_round(j, s), *item("piece", m))

                done = 0
                for i in range(N_STEP):
                    upto = PIECES_BY[i] if has_next else 0
                    cut = [done + k * (upto - done) // 4 for k in range(5)]
                    done = upto
                    maxima(cut[0], cut[1])
                    scores(n, s, i, 0)
                    maxima(cut[1], cut[2])
                    scores(n, s, i, 1)
                    maxima(cut[2], cut[3])
                    if i >= LAG:
                        values(n, s, i - LAG)
                    maxima(cut[3], cut[4])
                    for c in range(NC - 1):
                        if i == LAST[c] + LAG + 1:
                            transpose_o(n, c, *item("o", c))
                    if has_next and i == N_STEP - AHEAD + 1:
                        transpose_max(n + 1, *item("maxima"))
                for i in range(N_STEP - LAG, N_STEP):
                    values(n, s, i)
                transpose_o(n, NC - 1, *item("o", NC - 1))
            units(pe, body)


ROW_TILE = 256
CAP = T + ROW_TILE
N_TILE = T * 2 // ROW_TILE + E
SORTED = E * CAP + E * ROW_TILE


def phase3_route(nc, x_v, xn_v, o_v, w, sorted_rows, res_v, pos_v, gates_v, table):
    with ExitStack() as ctx:
        sb = lambda name, shape, dt=F32: ctx.enter_context(nc.sbuf_tensor(name, shape, dt))
        sem = lambda name: ctx.enter_context(nc.semaphore(name))
        bank = lambda name: ctx.enter_context(nc.psum_tensor(name, [P, CT], F32))

        ident = sb("p3_ident", [P, P])
        before = sb("p3_before", [P, P], BF16)
        ones = sb("p3_ones", [P, P], BF16)
        iota_e = sb("p3_iota_e", [P, E])
        iota_tile = sb("p3_iota_tile", [P, N_TILE])
        half = sb("p3_minus_half", [P, TT])
        zeros = sb("p3_zeros", [P, D])
        wo = sb("p3_wo", [P, KD, D])
        gate_w = sb("p3_gate_w", [P, KD, E])
        g2 = sb("p3_g2", [P, D])
        x = sb("p3_x", [P, 2, TT, D])
        xn = sb("p3_xn", [P, 2, TT, D])
        o = sb("p3_o", [P, 2, TT, NG, HG * DH])
        oT = sb("p3_oT", [P, KD, CT])
        x2 = sb("p3_x2", [P, TT, D])
        sq = sb("p3_sq", [P, TT, D])
        ss = sb("p3_ss", [P, TT])
        rrms = sb("p3_rrms", [P, TT])
        res = sb("p3_res", [P, 2, TT, D])
        th = sb("p3_th", [P, 2, TT, D])
        tT = sb("p3_tT", [P, KD, CT])
        logits = sb("p3_logits", [P, TT, E])
        top = sb("p3_top", [P, TT, E])
        top_i = sb("p3_top_i", [P, TT, E], U32)
        top_f = sb("p3_top_f", [P, TT, 2])
        chosen = sb("p3_chosen", [P, TT, 2, E])
        either = sb("p3_either", [P, TT, E], BF16)
        diff = sb("p3_diff", [P, TT])
        ediff = sb("p3_ediff", [P, TT])
        denom = sb("p3_denom", [P, TT])
        gates = sb("p3_gates", [P, 2, TT, 2])
        base = sb("p3_base", [P, E])
        place = sb("p3_place", [P, TT, E])
        picked = sb("p3_picked", [P, TT, 2, E])
        pos_f = sb("p3_pos_f", [P, TT, 2])
        pos_all = sb("p3_pos_all", [P, B * NC * TT * 2])
        pos_sum = sb("p3_pos_sum", [P, B * NC * TT * 2])
        behind = sb("p3_behind", [P, 2, B * NC * TT * 2])
        pos_out = sb("p3_pos_out", [P, B * NC * TT * 2], U32)
        pos = sb("p3_pos", [P, 2, TT, 2], U32)
        region = sb("p3_region", [P, E])
        tail_f = sb("p3_tail_f", [P, E, 2])
        tail = sb("p3_tail", [P, E, 2], U32)
        iota_p = sb("p3_iota_p", [P, 2])
        count = sb("p3_count", [P, E])
        count_i = sb("p3_count_i", [P, E], mybir.dt.int32)
        tiles = sb("p3_tiles", [P, E])
        ends = sb("p3_ends", [P, E])
        ones_e = sb("p3_ones_e", [P, E])
        jump = sb("p3_jump", [P, E])
        past = sb("p3_past", [P, N_TILE, E])
        past_j = sb("p3_past_j", [P, N_TILE, E])
        table_f = sb("p3_table_f", [P, 2, N_TILE])
        table_i = sb("p3_table_i", [P, 2, N_TILE], mybir.dt.int32)

        oT_ps = [bank(f"p3_oT{k}_ps") for k in range(KD)]
        mla_ps = [bank(f"p3_mla{i}_ps") for i in range(2)]
        tT_ps = [bank(f"p3_tT{k}_ps") for k in range(KD)]
        small_ps = bank("p3_small_ps")
        logit_ps = small_ps[:, 0:TT * E].rearrange("p (t e) -> p t e", e=E)
        rank_ps = small_ps[:, TT * E:2 * TT * E].rearrange("p (t e) -> p t e", e=E)
        total_ps = small_ps[:, 2 * TT * E:2 * TT * E + E]

        w_loaded = sem("p3_w_loaded")
        consts = sem("p3_consts")
        zeroed = sem("p3_zeroed")
        loaded = [sem(f"p3_loaded{s}") for s in range(2)]
        oT_done = sem("p3_oT_done")
        oT_copied = sem("p3_oT_copied")
        mla_done = sem("p3_mla_done")
        x2_done = sem("p3_x2_done")
        ss_done = sem("p3_ss_done")
        mean_done = sem("p3_mean_done")
        rrms_done = sem("p3_rrms_done")
        res_done = sem("p3_res_done")
        th_done = sem("p3_th_done")
        tT_done = sem("p3_tT_done")
        tT_copied = sem("p3_tT_copied")
        logit_done = sem("p3_logit_done")
        chain = sem("p3_chain")
        diff_done = sem("p3_diff_done")
        ediff_done = sem("p3_ediff_done")
        either_done = sem("p3_either_done")
        rank_done = sem("p3_rank_done")
        place_done = sem("p3_place_done")
        gates_done = sem("p3_gates_done")
        pos_done = sem("p3_pos_done")
        scattered = [sem(f"p3_scattered{s}") for s in range(2)]
        tail_done = sem("p3_tail_done")
        tail_stored = sem("p3_tail_stored")
        res_stored = [sem(f"p3_res_stored{s}") for s in range(2)]
        place_stored = [sem(f"p3_place_stored{s}") for s in range(2)]
        table_done = sem("p3_table_done")
        table_stored = sem("p3_table_stored")
        apart = sem("p3_apart")
        block = ctx.enter_context(nc.Block())
        ALL = B * NC
        N_LOAD = 16 * (NG + 2)

        def chunks(eng, body):
            with eng.Fori(0, B - 1) as b:
                for c in range(NC):
                    body(b, c, NC * b + c, True)
            for c in range(NC):
                body(B - 1, c, NC * (B - 1) + c, c < NC - 1)

        def uses(b, c):
            return (NC // 2) * b + c // 2

        @block.sync
        def _(sp):
            sp.dma_start(wo[:, :, :], w["ffn_Wo"].rearrange("(k p) n -> p k n", p=P)).then_inc(w_loaded, 16)
            sp.dma_start(gate_w[:, :, :], w["ffn_gate_w"].rearrange("(k p) n -> p k n", p=P)).then_inc(w_loaded, 16)
            sp.dma_start(g2[:, :], w["ffn_g2"].partition_broadcast(P)).then_inc(w_loaded, 16)

            def load(b, c):
                s = c % 2
                for g in range(NG):
                    sp.dma_start(o[:, s, :, g, :], o_v[b, c][:, :, g, :]).then_inc(loaded[s], 16)
                sp.dma_start(xn[:, s, :, :], xn_v[b, c]).then_inc(loaded[s], 16)
                sp.dma_start(x[:, s, :, :], x_v[b, c]).then_inc(loaded[s], 16)

            load(0, 0)
            load(0, 1)
            wait_apart(sp, consts, 1, apart)
            sp.dma_start(sorted_rows[E * CAP:SORTED, :].rearrange("(r p) d -> p r d", p=P),
                         zeros[:, :].unsqueeze(1).to_broadcast([P, E * ROW_TILE // P, D])).then_inc(zeroed, 16)

            def body(b, c, n, follows):
                s = c % 2
                wait_apart(sp, res_done, n + 1, apart)
                if follows and not (isinstance(b, int) and b == B - 1 and c + 2 >= NC):
                    load(b if c + 2 < NC else b + 1, (c + 2) % NC)
                sp.dma_start(res_v[b, c], res[:, s, :, :]).then_inc(res_stored[s], 16)
                wait_apart(sp, gates_done, n + 1, apart)
                sp.dma_start(gates_v[b, c], gates[:, s, :, :]).then_inc(place_stored[s], 16)
            chunks(sp, body)
            wait_apart(sp, table_done, 1, apart)
            sp.dma_start(table.rearrange("(a k) n -> a k n", a=1), table_i[0:1, :, :]).then_inc(table_stored, 16)
            sp.dma_start(pos_v, pos_out[:, :]).then_inc(table_stored, 16)
            wait_apart(sp, zeroed, 16, apart)
            wait_apart(sp, table_stored, 32, apart)
            for s in range(2):
                wait_apart(sp, res_stored[s], 16 * ALL // 2, apart)
                wait_apart(sp, place_stored[s], 16 * ALL // 2, apart)

        @block.gpsimd
        def _(pool):
            nc.gpsimd.memset(zeros[:, :], 0.0).then_inc(consts, 1)
            nc.gpsimd.memset(ident[:, :], 0.0)
            nc.gpsimd.memset(ones[:, :], 1.0)
            nc.gpsimd.memset(half[:, :], -0.5)
            nc.gpsimd.memset(ones_e[:, :], 1.0)
            exact = dict(allow_small_or_imprecise_dtypes=True)
            nc.gpsimd.iota(iota_e[:, :], [[1, E]], base=0, channel_multiplier=0, **exact)
            nc.gpsimd.iota(iota_tile[:, :], [[1, N_TILE]], base=0, channel_multiplier=0, **exact)
            nc.gpsimd.iota(iota_p[:, :], [[P, 2]], base=0, channel_multiplier=1, **exact)
            nc.gpsimd.iota(region[:, :], [[CAP, E]], base=0, channel_multiplier=0, **exact).then_inc(consts, 1)
            wait_apart(pool, consts, 2, apart)
            nc.gpsimd.affine_select(out=ident[:, :], in_=ident[:, :], compare_op=ALU.not_equal, fill=1.0,
                                    base=0, pattern=[[-1, P]], channel_multiplier=1)
            nc.gpsimd.affine_select(out=before[:, :], in_=ones[:, :], compare_op=ALU.is_gt, fill=0.0,
                                    base=0, pattern=[[1, P]], channel_multiplier=-1).then_inc(consts, 1)

            def stage_a(n, s, u):
                wait_apart(pool, ss_done, n + 1, apart)
                nc.gpsimd.tensor_scalar(rrms[:, :], ss[:, :], 1.0 / D, EPS_RMS, ALU.mult, ALU.add).then_inc(mean_done, 1)
                wait_apart(pool, mean_done, n + 1, apart)
                nc.gpsimd.tensor_tensor(rrms[:, :], rrms[:, :], half[:, :], ALU.pow).then_inc(rrms_done, 1)
                wait_apart(pool, res_stored[s], 16 * u, apart)
                nc.gpsimd.tensor_tensor(res[:, s, :, :], x[:, s, :, :], x2[:, :, :], ALU.add).then_inc(res_done, 1)

            stage_a(0, 0, 0)

            def body(b, c, n, follows):
                s = c % 2
                if follows:
                    stage_a(n + 1, (c + 1) % 2, uses(b, c + 1))
                wait_apart(pool, pos_done, n + 1, apart)
                for t in range(TT):
                    for k in range(2):
                        nc.gpsimd.indirect_dma_start(
                            sorted_rows, bass.IndirectOffsetOnAxis(pos[:, s, t, k:k + 1], 0), th[:, s, t, :], None
                        ).then_inc(scattered[s], 16)
            chunks(pool, body)
            wait_apart(pool, tail_done, 1, apart)
            for e in range(E):
                for i in range(2):
                    nc.gpsimd.indirect_dma_start(sorted_rows, bass.IndirectOffsetOnAxis(tail[:, e, i:i + 1], 0),
                                                 zeros[:, :], None).then_inc(tail_stored, 16)
            for s in range(2):
                wait_apart(pool, scattered[s], 16 * 2 * TT * ALL // 2, apart)
            wait_apart(pool, tail_stored, 16 * 2 * E, apart)

        @block.vector
        def _(dve):
            dve.wait_ge(consts, 3)
            nc.vector.tensor_copy(base[:, :], region[:, :]).then_inc(chain, 1)
            dve.wait_ge(chain, 1)
            dve.wait_ge(w_loaded, 48)
            LINKS = 10

            def add_attention(n, s, u):
                dve.wait_ge(loaded[s], N_LOAD * (u + 1))
                dve.wait_ge(res_done, n)
                dve.wait_ge(th_done, n)
                for i in range(2):
                    dve.wait_ge(mla_done, 2 * n + i + 1)
                    nc.vector.tensor_tensor(x2[:, 2 * i:2 * i + 2, :], mla_ps[i][:, :].rearrange("p (t d) -> p t d", d=D),
                                            xn[:, s, 2 * i:2 * i + 2, :], ALU.add).then_inc(x2_done, 1)

            def scale_rms(n, s, u):
                dve.wait_ge(rrms_done, n + 1)
                dve.wait_ge(scattered[s], 16 * 2 * TT * u)
                for t in range(TT):
                    last = nc.vector.scalar_tensor_tensor(th[:, s, t, :], x2[:, t, :], rrms[:, t:t + 1], g2[:, :],
                                                          ALU.mult, ALU.mult)
                last.then_inc(th_done, 1)

            add_attention(0, 0, 0)
            scale_rms(0, 0, 0)

            def body(b, c, n, follows):
                s, s1 = c % 2, (c + 1) % 2
                u1 = uses(b, c + 1)
                links = [0]

                def link(ins):
                    links[0] += 1
                    ins.then_inc(chain, 1)
                    wait_apart(dve, chain, 1 + LINKS * n + links[0], apart)

                if follows:
                    add_attention(n + 1, s1, u1)
                dve.wait_ge(logit_done, n + 1)
                link(nc.vector.tensor_copy(logits[:, :, :], logit_ps))
                for t in range(TT):
                    last = nc.vector.max(top[:, t, :], logits[:, t, :])
                link(last)
                for t in range(TT):
                    last = nc.vector.max_index(top_i[:, t, :], top[:, t, :], logits[:, t, :])
                link(last)
                nc.vector.tensor_tensor(diff[:, :], top[:, :, 1], top[:, :, 0], ALU.subtract).then_inc(diff_done, 1)
                link(nc.vector.tensor_copy(top_f[:, :, :], top_i[:, :, 0:2]))
                link(nc.vector.tensor_tensor(chosen[:, :, :, :].rearrange("p t k e -> p (t k) e"),
                                             iota_e[:, :].unsqueeze(1).to_broadcast([P, TT * 2, E]),
                                             top_f[:, :, :].rearrange("p t k -> p (t k)").unsqueeze(2)
                                             .to_broadcast([P, TT * 2, E]), ALU.is_equal))
                nc.vector.tensor_tensor(either[:, :, :], chosen[:, :, 0, :], chosen[:, :, 1, :], ALU.add
                                        ).then_inc(either_done, 1)
                dve.wait_ge(ediff_done, n + 1)
                link(nc.vector.tensor_scalar(denom[:, :], ediff[:, :], 1.0, None, ALU.add))
                dve.wait_ge(place_stored[s], 16 * uses(b, c))
                link(nc.vector.reciprocal(gates[:, s, :, 0], denom[:, :]))
                nc.vector.tensor_tensor(gates[:, s, :, 1], ediff[:, :], gates[:, s, :, 0], ALU.mult).then_inc(gates_done, 1)
                if follows:
                    scale_rms(n + 1, s1, u1)
                dve.wait_ge(rank_done, n + 1)
                dve.wait_ge(place_done, n)
                link(nc.vector.tensor_tensor(place[:, :, :], rank_ps, base[:, :].unsqueeze(1).to_broadcast([P, TT, E]),
                                             ALU.add))
                nc.vector.tensor_tensor(base[:, :], total_ps, base[:, :], ALU.add).then_inc(place_done, 1)
                for k in range(2):
                    last = nc.vector.tensor_tensor(picked[:, :, k, :], chosen[:, :, k, :], place[:, :, :], ALU.mult)
                link(last)
                link(nc.vector.tensor_reduce(pos_f[:, :, :], picked[:, :, :, :], AX_X, ALU.add))
                nc.vector.tensor_copy(pos_all[:, bass.ds(n * TT * 2, TT * 2)], pos_f[:, :, :].rearrange("p t k -> p (t k)"))
                dve.wait_ge(scattered[s], 16 * 2 * TT * uses(b, c))
                nc.vector.tensor_copy(pos[:, s, :, :], pos_f[:, :, :]).then_inc(pos_done, 1)
                assert links[0] == LINKS
            chunks(dve, body)

            links = [0]

            def link(ins):
                links[0] += 1
                ins.then_inc(chain, 1)
                dve.wait_ge(chain, 1 + LINKS * ALL + links[0])

            dve.wait_ge(place_done, ALL)
            link(nc.vector.tensor_tensor(tail_f[:, :, :], base[:, :].unsqueeze(2).to_broadcast([P, E, 2]),
                                         iota_p[:, :].unsqueeze(1).to_broadcast([P, E, 2]), ALU.add))
            nc.vector.tensor_copy(tail[:, :, :], tail_f[:, :, :]).then_inc(tail_done, 1)
            link(nc.vector.tensor_tensor(count[:, :], base[:, :], region[:, :], ALU.subtract))
            link(nc.vector.tensor_scalar(count_i[:, :], count[:, :], float(ROW_TILE - 1), None, ALU.add))
            link(nc.vector.tensor_scalar(count_i[:, :], count_i[:, :], ROW_TILE.bit_length() - 1, None,
                                         ALU.arith_shift_right))
            link(nc.vector.tensor_copy(tiles[:, :], count_i[:, :]))
            link(nc.vector.tensor_tensor_scan(ends[:, :], ones_e[:, :], tiles[:, :], 0.0, ALU.mult, ALU.add))
            link(nc.vector.tensor_scalar(jump[:, :], tiles[:, :], -float(ROW_TILE), float(CAP), ALU.mult, ALU.add))
            link(nc.vector.tensor_tensor(past[:, :, :], iota_tile[:, :].unsqueeze(2).to_broadcast([P, N_TILE, E]),
                                         ends[:, :].unsqueeze(1).to_broadcast([P, N_TILE, E]), ALU.is_ge))
            link(nc.vector.tensor_reduce(table_f[:, 0, :], past[:, :, :], AX_X, ALU.add))
            link(nc.vector.tensor_tensor(past_j[:, :, :], past[:, :, :],
                                         jump[:, :].unsqueeze(1).to_broadcast([P, N_TILE, E]), ALU.mult))
            link(nc.vector.tensor_reduce(table_f[:, 1, :], past_j[:, :, :], AX_X, ALU.add))
            link(nc.vector.scalar_tensor_tensor(table_f[:, 1, :], iota_tile[:, :], float(ROW_TILE), table_f[:, 1, :],
                                                ALU.mult, ALU.add))
            link(nc.vector.tensor_scalar(table_f[:, 0, :], table_f[:, 0, :], float(E - 1), None, ALU.min))
            nc.vector.tensor_copy(table_i[:, :, :], table_f[:, :, :])
            for e in range(1, E):
                link(nc.vector.tensor_scalar(behind[:, e % 2, :], pos_all[:, :], region[:, e:e + 1], jump[:, e - 1:e],
                                             ALU.is_ge, ALU.mult))
                link(nc.vector.tensor_tensor(pos_sum[:, :], pos_sum[:, :] if e > 1 else pos_all[:, :], behind[:, e % 2, :],
                                             ALU.subtract))
            nc.vector.tensor_copy(pos_out[:, :], pos_sum[:, :]).then_inc(table_done, 1)

        @block.scalar
        def _(act):
            def copy_oT(n):
                for k in range(KD):
                    act.wait_ge(oT_done, KD * n + k + 1)
                    act.wait_ge(mla_done, 2 * n)
                    nc.scalar.copy(oT[:, k, :], oT_ps[k][:, :]).then_inc(oT_copied, 1)

            def squares(n):
                act.wait_ge(mean_done, n)
                act.wait_ge(x2_done, 2 * n + 2)
                for t in range(TT):
                    last = nc.scalar.activation(sq[:, t, :], x2[:, t, :], ACT.Square, accum_out=ss[:, t:t + 1])
                last.then_inc(ss_done, 1)

            copy_oT(0)
            squares(0)

            def body(b, c, n, follows):
                if follows:
                    copy_oT(n + 1)
                for k in range(KD):
                    act.wait_ge(tT_done, KD * n + k + 1)
                    act.wait_ge(logit_done, n)
                    nc.scalar.copy(tT[:, k, :], tT_ps[k][:, :]).then_inc(tT_copied, 1)
                if follows:
                    squares(n + 1)
                act.wait_ge(diff_done, n + 1)
                nc.scalar.activation(ediff[:, :], diff[:, :], ACT.Exp).then_inc(ediff_done, 1)
            chunks(act, body)

        @block.tensor
        def _(pe):
            pe.wait_ge(consts, 3)
            pe.wait_ge(w_loaded, 48)

            def transpose_o(n, s, u):
                pe.wait_ge(loaded[s], N_LOAD * (u + 1))
                pe.wait_ge(oT_copied, KD * n)
                for k in range(KD):
                    for t in range(TT):
                        last = nc.tensor.transpose(oT_ps[k][:, t * P:(t + 1) * P],
                                                   o[:, s, t, 2 * k:2 * k + 2, :].rearrange("p g d -> p (g d)"), ident[:, :])
                    last.then_inc(oT_done, 1)

            def project(n):
                pe.wait_ge(oT_copied, KD * n + KD)
                pe.wait_ge(x2_done, 2 * n)
                for i in range(2):
                    for t in range(2):
                        tok = (2 * i + t) * P
                        for k in range(KD):
                            last = nc.tensor.matmul(mla_ps[i][:, t * D:(t + 1) * D], oT[:, k, tok:tok + P], wo[:, k, :],
                                                    start=k == 0, stop=k == KD - 1)
                    last.then_inc(mla_done, 1)

            transpose_o(0, 0, 0)
            project(0)

            def body(b, c, n, follows):
                s = c % 2
                if follows:
                    transpose_o(n + 1, (c + 1) % 2, uses(b, c + 1))
                pe.wait_ge(th_done, n + 1)
                pe.wait_ge(tT_copied, KD * n)
                for k in range(KD):
                    for t in range(TT):
                        last = nc.tensor.transpose(tT_ps[k][:, t * P:(t + 1) * P], th[:, s, t, k * P:(k + 1) * P], ident[:, :])
                    last.then_inc(tT_done, 1)
                if follows:
                    project(n + 1)
                pe.wait_ge(tT_copied, KD * n + KD)
                pe.wait_ge(place_done, n)
                for t in range(TT):
                    for k in range(KD):
                        last = nc.tensor.matmul(logit_ps[:, t, :], tT[:, k, t * P:(t + 1) * P], gate_w[:, k, :],
                                                start=k == 0, stop=k == KD - 1)
                last.then_inc(logit_done, 1)
                pe.wait_ge(either_done, n + 1)
                for t in range(TT):
                    nc.tensor.matmul(rank_ps[:, t, :], before[:, :], either[:, t, :], start=True, stop=t == 0)
                    for t0 in range(t):
                        nc.tensor.matmul(rank_ps[:, t, :], ones[:, :], either[:, t0, :], start=False, stop=t0 == t - 1)
                for t in range(TT):
                    last = nc.tensor.matmul(total_ps, ones[:, :], either[:, t, :], start=t == 0, stop=t == TT - 1)
                last.then_inc(rank_done, 1)
            chunks(pe, body)


def phase4_experts(nc, head_qkv, w, sorted_rows, expert_rows, attn_rows, table):
    NB = T // P - HEAD_BLOCKS
    QUADS, ALL_QUADS = NB // 2, N_TILE // 4
    RT = ROW_TILE // P
    FB = F // P
    HH = H * H
    with ExitStack() as ctx:
        sb = lambda name, shape, dt=F32: ctx.enter_context(nc.sbuf_tensor(name, shape, dt))
        sem = lambda name: ctx.enter_context(nc.semaphore(name))
        bank = lambda name: ctx.enter_context(nc.psum_tensor(name, [P, CT], F32))

        ident = sb("p4_ident", [P, P])
        table_sb = sb("p4_table", [1, 2, N_TILE], mybir.dt.int32)
        w1 = sb("p4_w1", [P, 2, KD, F])
        w2 = sb("p4_w2", [P, 2, FB, D])
        rows = sb("p4_rows", [P, 2, RT, D])
        rT = sb("p4_rT", [P, KD, ROW_TILE])
        hid = sb("p4_hid", [P, FB, ROW_TILE])
        y = sb("p4_y", [P, 2, RT, D])
        qkv = sb("p4_qkv", [P, 2, 3, D])
        prod = sb("p4_prod", [P, H, H, DH])
        s = sb("p4_s", [P, H, H])
        smax = sb("p4_smax", [P, H])
        sm = sb("p4_sm", [P, H, H])
        pr = sb("p4_pr", [P, 2, H, H])
        psum = sb("p4_psum", [P, H])
        inv = sb("p4_inv", [P, 2, H])
        pv = sb("p4_pv", [P, 2, H, DH, H])
        oh = sb("p4_oh", [P, 2, H, DH])

        rT_ps = bank("p4_rT_ps")
        hid_ps = [bank(f"p4_hid{i}_ps") for i in range(2)]
        y_ps = bank("p4_y_ps")
        q_ps = [bank(f"p4_q{i}_ps") for i in range(2)]

        w_loaded = sem("p4_w_loaded")
        consts = sem("p4_consts")
        w1_loaded = [sem(f"p4_w1_loaded{i}") for i in range(2)]
        rows_loaded = [sem(f"p4_rows_loaded{i}") for i in range(2)]
        rT_done = sem("p4_rT_done")
        rT_copied = sem("p4_rT_copied")
        hid_done = sem("p4_hid_done")
        silu_done = sem("p4_silu_done")
        y_done = sem("p4_y_done")
        y_copied = sem("p4_y_copied")
        y_stored = [sem(f"p4_y_stored{i}") for i in range(2)]
        qkv_loaded = [sem(f"p4_qkv_loaded{i}") for i in range(2)]
        q_copied = sem("p4_q_copied")
        prod_done = sem("p4_prod_done")
        s_done = sem("p4_s_done")
        smax_done = sem("p4_smax_done")
        sm_done = sem("p4_sm_done")
        exp_done = sem("p4_exp_done")
        psum_done = sem("p4_psum_done")
        inv_done = sem("p4_inv_done")
        pv_done = sem("p4_pv_done")
        pv_added = sem("p4_pv_added")
        oh_done = sem("p4_oh_done")
        oh_stored = [sem(f"p4_oh_stored{i}") for i in range(2)]
        apart = sem("p4_apart")
        block = ctx.enter_context(nc.Block())

        def quads(eng, body):
            body(0, True, True, False)
            with eng.Fori(1, QUADS) as g:
                body(g, True, False, False)
            for g in range(QUADS, ALL_QUADS):
                body(g, False, g == QUADS, g == ALL_QUADS - 1)

        @block.sync
        def _(sp):
            sp.dma_start(table_sb[:, :, :], table.unsqueeze(0)).then_inc(w_loaded, 16)

            def load_block(m, u):
                wait_apart(sp, prod_done, m + 1, apart)
                wait_apart(sp, pv_done, m + 1, apart)
                sp.dma_start(qkv[:, u, :, :].rearrange("p i d -> p (i d)"),
                             head_qkv[bass.ds(HEAD_BLOCKS + m, 1), :, :].rearrange("a p d -> p (a d)")).then_inc(qkv_loaded[u], 16)

            load_block(0, 0)
            load_block(1, 1)
            wait_apart(sp, w_loaded, 16, apart)

            def body(g, has_blocks, first, last):
                for i in range(4):
                    n, u = 4 * g + i, i % 2
                    e = sp.value_load(table_sb[0:1, 0, bass.ds(n, 1)], min_val=0, max_val=E - 1)
                    row = sp.value_load(table_sb[0:1, 1, bass.ds(n, 1)], min_val=0, max_val=SORTED - ROW_TILE)
                    wait_apart(sp, rT_done, n + 1, apart)
                    sp.dma_start(rows[:, u, :, :], sorted_rows[bass.ds(row, ROW_TILE), :].rearrange("(t p) d -> p t d", p=P)
                                 ).then_inc(rows_loaded[u], 16)
                    wait_apart(sp, y_done, n + 1, apart)
                    sp.dma_start(w1[:, u, :, :], w["ffn_w1"][bass.ds(e, 1), :, :].rearrange("a (k p) f -> p (a k) f", p=P)
                                 ).then_inc(w1_loaded[u], 16)
                    sp.dma_start(w2[:, u, :, :], w["ffn_w2"][bass.ds(e, 1), :, :].rearrange("a (k p) f -> p (a k) f", p=P)
                                 ).then_inc(w1_loaded[u], 16)
                    if has_blocks and i % 2 and not first:
                        load_block(2 * g + i // 2, i // 2)
            quads(sp, body)

        @block.gpsimd
        def _(pool):
            nc.gpsimd.memset(ident[:, :], 0.0).then_inc(consts, 1)
            wait_apart(pool, consts, 1, apart)
            nc.gpsimd.affine_select(out=ident[:, :], in_=ident[:, :], compare_op=ALU.not_equal, fill=1.0,
                                    base=0, pattern=[[-1, P]], channel_multiplier=1).then_inc(consts, 1)

            def weigh_values(n, u):
                wait_apart(pool, exp_done, n + 1, apart)
                wait_apart(pool, pv_added, n + 1, apart)
                nc.gpsimd.tensor_tensor(
                    pv[:, u, :, :, :],
                    pr[:, u, :, :].unsqueeze(2).to_broadcast([P, H, DH, H]),
                    qkv[:, u, 2, :].rearrange("p (j d) -> p d j", d=DH).unsqueeze(1).to_broadcast([P, H, DH, H]),
                    ALU.mult).then_inc(pv_done, 1)

            def store(n, u):
                wait_apart(pool, oh_done, n + 1, apart)
                nc.gpsimd.dma_start(attn_rows[bass.ds(HEAD_BLOCKS + n, 1), :, :].rearrange("a p d -> p (a d)"),
                                    oh[:, u, :, :].rearrange("p i d -> p (i d)")).then_inc(oh_stored[u], 16)

            weigh_values(0, 0)
            weigh_values(1, 1)
            with pool.Fori(1, NB // 2) as j:
                for u in range(2):
                    store(2 * j + u - 2, u)
                    weigh_values(2 * j + u, u)
            store(NB - 2, 0)
            store(NB - 1, 1)
            for u in range(2):
                wait_apart(pool, oh_stored[u], 16 * NB // 2, apart)

        @block.vector
        def _(dve):
            dve.sem_inc(rT_done, 2)
            dve.sem_inc(y_done, 2)
            dve.sem_inc(pv_added, 2)
            dve.sem_inc(prod_done, 2)
            dve.sem_inc(psum_done, 2)
            dve.sem_inc(pv_done, 2)
            def score(n, u):
                dve.wait_ge(q_copied, n + 1)
                q = q_ps[u][:, 0:D].rearrange("p (i d) -> p i d", d=DH)
                k = qkv[:, u, 1, :].rearrange("p (j d) -> p j d", d=DH)
                nc.vector.tensor_tensor(prod[:, :, :, :], q.unsqueeze(2).to_broadcast([P, H, H, DH]),
                                        k.unsqueeze(1).to_broadcast([P, H, H, DH]), ALU.mult).then_inc(prod_done, 1)
                dve.wait_ge(prod_done, 2 + n + 1)
                nc.vector.tensor_reduce(s[:, :, :], prod[:, :, :, :], AX_X, ALU.add).then_inc(s_done, 1)
                dve.wait_ge(s_done, n + 1)
                nc.vector.tensor_reduce(smax[:, :], s[:, :, :], AX_X, ALU.max).then_inc(smax_done, 1)
                dve.wait_ge(smax_done, n + 1)
                dve.wait_ge(exp_done, n)
                nc.vector.tensor_tensor(sm[:, :, :], s[:, :, :], smax[:, :].unsqueeze(2).to_broadcast([P, H, H]),
                                        ALU.subtract).then_inc(sm_done, 1)

            def row_sums(n, u):
                dve.wait_ge(exp_done, n + 1)
                nc.vector.tensor_reduce(psum[:, :], pr[:, u, :, :], AX_X, ALU.add).then_inc(psum_done, 1)
                dve.wait_ge(psum_done, 2 + n + 1)
                nc.vector.reciprocal(inv[:, u, :], psum[:, :]).then_inc(inv_done, 1)

            def finish(n, u, j):
                dve.wait_ge(pv_done, 2 + n + 1)
                dve.wait_ge(oh_stored[u], 16 * j)
                nc.vector.tensor_reduce(oh[:, u, :, :], pv[:, u, :, :, :], AX_X, ALU.add).then_inc(pv_added, 1)
                dve.wait_ge(pv_added, 2 + n + 1)
                dve.wait_ge(inv_done, n + 1)
                nc.vector.tensor_tensor(oh[:, u, :, :], oh[:, u, :, :],
                                        inv[:, u, :].unsqueeze(2).to_broadcast([P, H, DH]), ALU.mult).then_inc(oh_done, 1)

            score(0, 0)
            score(1, 1)
            row_sums(0, 0)
            with dve.Fori(1, NB // 2) as j:
                for u in range(2):
                    score(2 * j + u, u)
                    row_sums(2 * j + u - 1, 1 - u)
                    finish(2 * j + u - 2, u, j - 1)
            row_sums(NB - 1, 1)
            finish(NB - 2, 0, NB // 2 - 1)
            finish(NB - 1, 1, NB // 2 - 1)

        @block.scalar
        def _(act):
            act.sem_inc(silu_done, 2)

            def copy_rows(n):
                act.wait_ge(rT_done, 2 + n + 1)
                act.wait_ge(hid_done, 2 * n)
                nc.scalar.copy(rT[:, :, :].rearrange("p k t -> p (k t)"), rT_ps[:, :]).then_inc(rT_copied, 1)

            def copy_q(m, u, loads):
                act.wait_ge(qkv_loaded[u], 16 * loads)
                act.wait_ge(prod_done, m + 1)
                nc.scalar.copy(q_ps[u][:, 0:D], qkv[:, u, 0, :]).then_inc(q_copied, 1)

            def probabilities(n, u):
                act.wait_ge(sm_done, n + 1)
                act.wait_ge(psum_done, n + 1)
                act.wait_ge(pv_done, n + 1)
                nc.scalar.activation(pr[:, u, :, :], sm[:, :, :], ACT.Exp).then_inc(exp_done, 1)

            copy_q(0, 0, 1)
            copy_q(1, 1, 1)
            copy_rows(0)

            def body(g, has_blocks, first, last):
                for i in range(4):
                    n, u = 4 * g + i, i % 2
                    for k in range(2):
                        act.wait_ge(hid_done, 2 * n + k + 1)
                        act.wait_ge(y_done, 2 + n)
                        nc.scalar.activation(hid[:, 2 * k:2 * k + 2, :].rearrange("p k t -> p (k t)"), hid_ps[k][:, :],
                                             ACT.Silu).then_inc(silu_done, 1)
                    if not (last and i == 3):
                        copy_rows(n + 1)
                    m = 2 * g + i // 2
                    if i % 2 == 0 and not (first and i == 0) and has_blocks:
                        probabilities(m - 1, 1 - i // 2)
                        if not first:
                            copy_q(m, i // 2, g + 1)
                    if not has_blocks and first and i == 0:
                        probabilities(NB - 1, 1)
                    act.wait_ge(y_done, 2 + n + 1)
                    act.wait_ge(y_stored[u], 16 * (2 * g + i // 2))
                    nc.scalar.copy(y[:, u, :, :].rearrange("p t d -> p (t d)"), y_ps[:, :]).then_inc(y_copied, 1)
                    act.wait_ge(y_copied, n + 1)
                    act.dma_start(expert_rows[bass.ds(n, 1), :, :].rearrange("a (t p) d -> p (a t) d", p=P),
                                  y[:, u, :, :]).then_inc(y_stored[u], 16)
            quads(act, body)
            for u in range(2):
                act.wait_ge(y_stored[u], 16 * N_TILE // 2)

        @block.tensor
        def _(pe):
            pe.wait_ge(consts, 2)

            def transpose_rows(n, u, j):
                pe.wait_ge(rows_loaded[u], 16 * (j + 1))
                pe.wait_ge(rT_copied, n)
                for k in range(KD):
                    for t in range(RT):
                        last = nc.tensor.transpose(rT_ps[:, k * ROW_TILE + t * P:k * ROW_TILE + (t + 1) * P],
                                                   rows[:, u, t, k * P:(k + 1) * P], ident[:, :])
                last.then_inc(rT_done, 1)

            def hidden(n, u, j):
                pe.wait_ge(rT_copied, n + 1)
                pe.wait_ge(w1_loaded[u], 32 * (j + 1))
                for i in range(2):
                    pe.wait_ge(silu_done, 2 * n + i + 1)
                    for f in range(2):
                        for k in range(KD):
                            last = nc.tensor.matmul(hid_ps[i][:, f * ROW_TILE:(f + 1) * ROW_TILE],
                                                    w1[:, u, k, (2 * i + f) * P:(2 * i + f + 1) * P], rT[:, k, :],
                                                    start=k == 0, stop=k == KD - 1)
                    last.then_inc(hid_done, 1)

            def second(n, u):
                pe.wait_ge(silu_done, 2 + 2 * n + 2)
                pe.wait_ge(y_copied, n)
                for t in range(RT):
                    for f in range(FB):
                        last = nc.tensor.matmul(y_ps[:, t * D:(t + 1) * D], hid[:, f, t * P:(t + 1) * P], w2[:, u, f, :],
                                                start=f == 0, stop=f == FB - 1)
                last.then_inc(y_done, 1)

            transpose_rows(0, 0, 0)

            def body(g, has_blocks, first, last):
                for i in range(4):
                    n, u = 4 * g + i, i % 2
                    hidden(n, u, 2 * g + i // 2)
                    if not (last and i == 3):
                        transpose_rows(n + 1, 1 - u, 2 * g + (i + 1) // 2)
                    second(n, u)
            quads(pe, body)


def phase5_combine(nc, res_v, attn_v, pos_v, gates_v, expert_rows, out_v):
    with ExitStack() as ctx:
        sb = lambda name, shape, dt=F32: ctx.enter_context(nc.sbuf_tensor(name, shape, dt))
        sem = lambda name: ctx.enter_context(nc.semaphore(name))
        res = sb("p5_res", [P, 2, TT, D])
        attn = sb("p5_attn", [P, 2, TT, D])
        pos = sb("p5_pos", [P, 2, TT, 2], U32)
        gates = sb("p5_gates", [P, 2, TT, 2])
        ye = sb("p5_ye", [P, 2, TT, 2, D])
        acc = sb("p5_acc", [P, 2, TT, D])
        loaded = [sem(f"p5_loaded{i}") for i in range(2)]
        pos_loaded = [sem(f"p5_pos_loaded{i}") for i in range(2)]
        gathered = [sem(f"p5_gathered{i}") for i in range(2)]
        added = sem("p5_added")
        first_done = sem("p5_first_done")
        out_done = sem("p5_out_done")
        stored = [sem(f"p5_stored{i}") for i in range(2)]
        apart = sem("p5_apart")
        block = ctx.enter_context(nc.Block())

        def chunks(eng, body):
            with eng.Fori(0, B) as b:
                for c in range(NC):
                    body(b, c, NC * b + c, c % 2, NC // 2 * b + c // 2)

        @block.sync
        def _(sp):
            def body(b, c, n, s, u):
                wait_apart(sp, out_done, n + 1, apart)
                sp.dma_start(pos[:, s, :, :], pos_v[b, c]).then_inc(pos_loaded[s], 16)
                sp.dma_start(res[:, s, :, :], res_v[b, c]).then_inc(loaded[s], 16)
                sp.dma_start(attn[:, s, :, :], attn_v[b, c]).then_inc(loaded[s], 16)
                sp.dma_start(gates[:, s, :, :], gates_v[b, c]).then_inc(loaded[s], 16)
            chunks(sp, body)

        @block.gpsimd
        def _(pool):
            def body(b, c, n, s, u):
                wait_apart(pool, pos_loaded[s], 16 * (u + 1), apart)
                wait_apart(pool, out_done, n + 1, apart)
                for t in range(TT):
                    for k in range(2):
                        nc.gpsimd.indirect_dma_start(ye[:, s, t, k, :], None, expert_rows,
                                                     bass.IndirectOffsetOnAxis(pos[:, s, t, k:k + 1], 0)
                                                     ).then_inc(gathered[s], 16)
            chunks(pool, body)

        @block.vector
        def _(dve):
            dve.sem_inc(out_done, 2)

            def body(b, c, n, s, u):
                dve.wait_ge(loaded[s], 48 * (u + 1))
                dve.wait_ge(stored[s], 16 * u)
                nc.vector.tensor_tensor(acc[:, s, :, :], res[:, s, :, :], attn[:, s, :, :], ALU.add).then_inc(added, 1)
                dve.wait_ge(gathered[s], 16 * 2 * TT * (u + 1))
                dve.wait_ge(added, n + 1)
                for t in range(TT):
                    last = nc.vector.scalar_tensor_tensor(acc[:, s, t, :], ye[:, s, t, 0, :], gates[:, s, t, 0:1],
                                                          acc[:, s, t, :], ALU.mult, ALU.add)
                last.then_inc(first_done, 1)
                dve.wait_ge(first_done, n + 1)
                for t in range(TT):
                    last = nc.vector.scalar_tensor_tensor(acc[:, s, t, :], ye[:, s, t, 1, :], gates[:, s, t, 1:2],
                                                          acc[:, s, t, :], ALU.mult, ALU.add)
                last.then_inc(out_done, 1)
            chunks(dve, body)

        @block.scalar
        def _(act):
            def body(b, c, n, s, u):
                act.wait_ge(out_done, 2 + n + 1)
                act.dma_start(out_v[b, c], acc[:, s, :, :]).then_inc(stored[s], 16)
            chunks(act, body)
            for s in range(2):
                act.wait_ge(stored[s], 16 * B * NC // 2)


INPUTS = ["attn_x", "attn_Wq", "attn_bq", "attn_Wk", "attn_bk", "attn_Wv", "attn_bv", "ffn_g1", "ffn_Wq", "ffn_Wdkv",
          "ffn_Wuk", "ffn_Wuv", "ffn_Wo", "ffn_g2", "ffn_gate_w", "ffn_w1", "ffn_w2"]


def build(nc, w, out):
    dram = lambda name, shape, dt=F32: nc.dram_tensor(name, shape, dt, kind="Internal").ap()
    xn = dram("xn", [T, D])
    qk = dram("qk_parts", [2, 3, B, D, S], BF16)
    v = dram("v_padded", [B * NG, S, HG * VW])
    o = dram("o_heads", [B * NG, S, HG * DH])
    res = dram("res", [T, D])
    pos = dram("pos", [P, B * NC * TT * 2], U32)
    gates = dram("gates", [B, NC, P, TT * 2])
    table = dram("tile_table", [2, N_TILE], mybir.dt.int32)
    sorted_rows = dram("sorted_rows", [SORTED, D])
    expert_rows = dram("expert_rows", [N_TILE * ROW_TILE, D])
    attn = dram("attn_rows", [T, D])
    heads = dram("head_qkv", [T, 3 * D])
    by_chunk = lambda a: a.rearrange("(b c t p) d -> b c p t d", b=B, c=NC, p=P)
    by_block = lambda a: a.rearrange("(n p) d -> n p d", p=P)
    x = w["attn_x"].rearrange("b s d -> (b s) d")
    pairs = lambda a: a.rearrange("b c p (t k) -> b c p t k", k=2)

    phase1_project(nc, by_chunk(x), w, by_chunk(xn), qk, v.rearrange("(b g) t v -> b g t v", b=B), by_chunk(heads))
    phase2_attend(nc, qk.rearrange("a p b (h d) t -> a p (b h) d t", d=DH), v, o, by_block(heads), by_block(attn))
    phase3_route(nc, by_chunk(x), by_chunk(xn), o.rearrange("(b g) (c t p) d -> b c p t g d", b=B, c=NC, p=P), w,
                 sorted_rows, by_chunk(res), pos, pairs(gates), table)
    phase4_experts(nc, by_block(heads), w, sorted_rows, expert_rows.rearrange("(n r) d -> n r d", r=ROW_TILE),
                   by_block(attn), table)
    phase5_combine(nc, by_chunk(res), by_chunk(attn),
                   pos.rearrange("p (b c t k) -> b c p t k", b=B, c=NC, k=2), pairs(gates), expert_rows, by_chunk(out))


def kernel(**inputs):
    import numpy as np
    import concourse.bacc as bacc
    from concourse.bass_utils import run_bass_kernel_spmd

    nc = bacc.Bacc("TRN2", target_bir_lowering=False, num_devices=1)
    arrays, w = {}, {}
    for name in INPUTS:
        a = np.ascontiguousarray(inputs[f"L0_{name}"])
        arrays[name] = a
        w[name] = nc.dram_tensor(name, list(a.shape), mybir.dt.from_np(a.dtype), kind="ExternalInput").ap()
    out = nc.dram_tensor("out", [T, D], F32, kind="ExternalOutput").ap()
    build(nc, w, out)
    r = run_bass_kernel_spmd(nc, [arrays], core_ids=[0])
    return r.results[0]["out"].reshape(B, S, D)
```

```python
from contextlib import ExitStack

import concourse.bass as bass
from concourse import mybir

F32 = mybir.dt.float32
BF16 = mybir.dt.bfloat16
U32 = mybir.dt.uint32
ALU = mybir.AluOpType
ACT = mybir.ActivationFunctionType
AX_X = mybir.AxisListType.X

P = 128
B, S, D = 4, 2048, 256
T = B * S
H, DH = 16, 16
L = 128
E, F = 8, 512
KD = D // P
CT = 512
TT = CT // P
NC = S // CT
HG = 4
NG = H // HG
VW = 32
EPS_LN, EPS_RMS = 1e-5, 1e-6
KT = S // P
BIG = 1e30
Q_PART = (0, 0, 1, 1, 0, 2)
K_PART = (0, 1, 0, 1, 2, 0)
SPLIT = DH * len(Q_PART)
ROWS = SPLIT + 2
HEAD_PIECES = [(i, pc, min(CT, (i + 1) * P - pc * CT)) for i in range(KT) for pc in range(i // TT + 1)]
N_LOAD = 16 * (2 * len(Q_PART) + 2)
HEAD_BLOCKS = 2 * B * NG


def wait_apart(eng, sem, value, apart):
    eng.wait_ge(sem, value)
    eng.sem_inc(apart, 1)


def load_unit(sp, qk_heads, v_units, n, q6, k6, vg, loaded):
    for g, (a, k) in enumerate(zip(Q_PART, K_PART)):
        sp.dma_start(q6[g * DH:(g + 1) * DH, :, :],
                     qk_heads[0, a, bass.ds(n * HG, HG), :, :].rearrange("h d t -> d h t")).then_inc(loaded, 16)
        sp.dma_start(k6[g * DH:(g + 1) * DH, :, :],
                     qk_heads[1, k, bass.ds(n * HG, HG), :, :].rearrange("h d t -> d h t")).then_inc(loaded, 16)
    for i in range(2):
        half = slice(i * S // 2, (i + 1) * S // 2)
        sp.dma_start(vg[:, i * KT // 2:(i + 1) * KT // 2, :],
                     v_units[bass.ds(n, 1), half, :].rearrange("a (k p) v -> p (a k) v", p=P)).then_inc(loaded, 16)


def row_piece(nc, out, q6, k6, h, piece, ident_b, mask_q):
    i, pc, width = piece
    diagonal = pc == i // TT
    last = nc.tensor.matmul(out[:, 0:width], q6[0:SPLIT, h, i * P:(i + 1) * P], k6[0:SPLIT, h, pc * CT:pc * CT + width],
                            start=True, stop=not diagonal)
    if diagonal:
        last = nc.tensor.matmul(out[:, width - P:width], ident_b[:, :], mask_q[:, :], start=False, stop=True)
    return last


def phase1_project(nc, apart, x_v, w, xn_v, qk_parts, v_dram, head_qkv, qk_heads, v_units, units):
    q6, k6, _ = units[0]
    with ExitStack() as ctx:
        sb = lambda name, shape, dt=F32: ctx.enter_context(nc.sbuf_tensor(name, shape, dt))
        sem = lambda name: ctx.enter_context(nc.semaphore(name))
        bank = lambda name: ctx.enter_context(nc.psum_tensor(name, [P, CT], F32))

        ident = sb("p1_ident", [P, P])
        wq = sb("p1_wq", [P, KD, D])
        wdkv = sb("p1_wdkv", [P, KD, L])
        wuk = sb("p1_wuk", [P, D])
        wuv = sb("p1_wuv", [P, D])
        g1 = sb("p1_g1", [P, KD])
        half = sb("p1_minus_half", [P, TT])
        plus_half = sb("p1_plus_half", [P, TT])
        wh = sb("p1_wh", [P, KD, 3, D])
        bh = sb("p1_bh", [P, 3, D])
        heads = sb("p1_heads", [P, 2, TT, 3, D])
        meansq = sb("p1_meansq", [P, TT])
        rms = sb("p1_rms", [P, 2, TT])
        x = sb("p1_x", [P, 2, TT, D])
        xn = sb("p1_xn", [P, 2, TT, D])
        h = sb("p1_h", [P, TT, D])
        hT = sb("p1_hT", [P, 2, KD, CT])
        cT = sb("p1_cT", [P, CT])
        stats = sb("p1_stats", [P, TT, 6])
        mv = sb("p1_mv", [P, TT, 2])
        rstd = sb("p1_rstd", [P, TT])
        sq = sb("p1_sq", [P, TT, D])
        ss = sb("p1_ss", [P, TT])
        rrms = sb("p1_rrms", [P, TT])
        parts = sb("p1_parts", [P, 2, 4, 3, CT], BF16)
        rest = sb("p1_rest", [P, 4, CT])
        vx = sb("p1_vx", [P, 2, TT, H, VW])

        ident_b = sb("p1_ident_b", [P, P], BF16)
        mask_q = sb("p1_mask_q", [P, P], BF16)
        piece_max = sb("p1_piece_max", [P, HG * KT, NC])
        neg_max = sb("p1_neg_max", [P, P])
        neg_hi = sb("p1_neg_hi", [HG * KT, P], BF16)
        neg_lo = sb("p1_neg_lo", [HG * KT, P], BF16)

        t_ps = bank("p1_t")
        row_ps = [bank(f"p1_row{i}") for i in range(2)]
        qk_ps = [bank(f"p1_qk{j}") for j in range(2)]
        heads_ps = ctx.enter_context(nc.psum_tensor("p1_heads_ps", [P, 2 * CT], F32))
        cv_ps = bank("p1_cv")

        w_loaded = sem("p1_w_loaded")
        consts = sem("p1_consts")
        w_scaled = sem("p1_w_scaled")
        x_loaded = [sem(f"p1_x_loaded{s}") for s in range(2)]
        stats_done = sem("p1_stats_done")
        mv_done = sem("p1_mv_done")
        rstd_steps = sem("p1_rstd_steps")
        xn_done = sem("p1_xn_done")
        ss_done = sem("p1_ss_done")
        mean_done = sem("p1_mean_done")
        rrms_done = sem("p1_rrms_done")
        rms_done = sem("p1_rms_done")
        h_done = sem("p1_h_done")
        t_done = sem("p1_t_done")
        hT_done = sem("p1_hT_done")
        qk_done = sem("p1_qk_done")
        heads_done = sem("p1_heads_done")
        heads_taken = sem("p1_heads_taken")
        heads_stored = [sem(f"p1_heads_stored{s}") for s in range(2)]
        part0_done = sem("p1_part0_done")
        rest_done = sem("p1_rest_done")
        part1_done = sem("p1_part1_done")
        part2_done = sem("p1_part2_done")
        c_done = sem("p1_c_done")
        cT_done = sem("p1_cT_done")
        v_done = sem("p1_v_done")
        vx_done = sem("p1_vx_done")
        xn_stored = [sem(f"p1_xn_stored{s}") for s in range(2)]
        parts_stored = [sem(f"p1_parts_stored{s}") for s in range(2)]
        vx_stored = [sem(f"p1_vx_stored{s}") for s in range(2)]
        unit_loaded = sem("p1_unit_loaded")
        row_scored = sem("p1_row_scored")
        row_free = sem("p1_row_free")
        ones_set = sem("p1_ones_set")
        maxima_steps = sem("p1_maxima_steps")
        next_loaded = sem("p1_next_loaded")
        maxima_stored = sem("p1_maxima_stored")
        block = ctx.enter_context(nc.Block())

        QUIET = B // 2
        assert HG == 2 * (B - QUIET)

        def chunks(eng, body):
            with eng.Fori(0, QUIET) as b:
                for c in range(NC):
                    body(b, c, NC * b + c, True)
            for b in range(QUIET, B):
                for c in range(NC):
                    body(b, c, NC * b + c, b < B - 1 or c < NC - 1)

        SPOTS = 10

        def pieces_beside(b, c, spot):
            if not isinstance(b, int) or b < QUIET:
                return []
            part = len(HEAD_PIECES) // NC
            beside = [(h, piece) for h in (2 * (b - QUIET), 2 * (b - QUIET) + 1) for piece in HEAD_PIECES[c * part:(c + 1) * part]]
            first = len(beside) * (NC * (b - QUIET) + c)
            here = range(spot * len(beside) // SPOTS, (spot + 1) * len(beside) // SPOTS)
            return [(first + k, *beside[k]) for k in here]

        def uses(b, c):
            return (NC // 2) * b + c // 2

        @block.sync
        def _(sp):
            for c in range(2):
                sp.dma_start(x[:, c, :, :], x_v[0, c]).then_inc(x_loaded[c], 16)
            sp.dma_start(wq[:, :, :], w["ffn_Wq"].rearrange("(k p) n -> p k n", p=P)).then_inc(w_loaded, 16)
            sp.dma_start(wdkv[:, :, :], w["ffn_Wdkv"].rearrange("(k p) n -> p k n", p=P)).then_inc(w_loaded, 16)
            sp.dma_start(wuk[:, :], w["ffn_Wuk"]).then_inc(w_loaded, 16)
            sp.dma_start(wuv[:, :], w["ffn_Wuv"]).then_inc(w_loaded, 16)
            with nc.allow_non_contiguous_dma(reason="256 gains, once"):
                sp.dma_start(g1[:, :], w["ffn_g1"].rearrange("(k p) -> p k", p=P)).then_inc(w_loaded, 16)
            for i, name in enumerate(("q", "k", "v")):
                sp.dma_start(wh[:, :, i, :], w[f"attn_W{name}"].rearrange("(k p) n -> p k n", p=P)).then_inc(w_loaded, 16)
                sp.dma_start(bh[:, i, :], w[f"attn_b{name}"].partition_broadcast(P)).then_inc(w_loaded, 16)

            def store_xn(b, c, n):
                wait_apart(sp, xn_done, n + 1, apart)
                sp.dma_start(xn_v[b, c], xn[:, c % 2, :, :]).then_inc(xn_stored[c % 2], 16)

            def load_x(b, c):
                sp.dma_start(x[:, c % 2, :, :], x_v[b, c]).then_inc(x_loaded[c % 2], 16)

            def store_parts(b, c, n, j):
                wait_apart(sp, part2_done, 4 * n + j + 1, apart)
                sp.dma_start(qk_parts[j // 2, :, b, (j % 2) * P:(j % 2 + 1) * P, c * CT:(c + 1) * CT]
                             .rearrange("a p t -> p a t"), parts[:, c % 2, j, :, :]).then_inc(parts_stored[c % 2], 16)

            store_xn(0, 0, 0)
            load_x(0, 2)

            def body(b, c, n, follows):
                s = c % 2
                store_parts(b, c, n, 0)
                store_parts(b, c, n, 1)
                if follows:
                    store_xn(*((b, c + 1) if c + 1 < NC else (b + 1, 0)), n + 1)
                    if c + 3 < NC:
                        load_x(b, c + 3)
                    elif not isinstance(b, int) or b < B - 1:
                        load_x(b + 1, c + 3 - NC)
                store_parts(b, c, n, 2)
                store_parts(b, c, n, 3)
                wait_apart(sp, heads_taken, TT * n + TT, apart)
                sp.dma_start(head_qkv[b, c], heads[:, s, :, :, :].rearrange("p t i d -> p t (i d)")).then_inc(heads_stored[s], 16)
                wait_apart(sp, vx_done, 2 * n + 2, apart)
                for g in range(NG):
                    sp.dma_start(v_dram[b, g, c * CT:(c + 1) * CT, :].rearrange("(t p) v -> p t v", p=P),
                                 vx[:, s, :, g * HG:(g + 1) * HG, :].rearrange("p t h v -> p t (h v)")
                                 ).then_inc(vx_stored[s], 16)
            for c in range(NC):
                body(0, c, c, True)
            for s in range(2):
                wait_apart(sp, parts_stored[s], 16 * 4 * NC // 2, apart)
                wait_apart(sp, vx_stored[s], 16 * NG * NC // 2, apart)
            load_unit(sp, qk_heads, v_units, 0, *units[0], unit_loaded)
            load_unit(sp, qk_heads, v_units, 1, *units[1], next_loaded)
            with sp.Fori(1, B - 1) as b:
                for c in range(NC):
                    body(b, c, NC * b + c, True)
            for c in range(NC):
                body(B - 1, c, NC * (B - 1) + c, c < NC - 1)
            wait_apart(sp, maxima_steps, 4, apart)
            for k, part in enumerate((neg_hi, neg_lo)):
                sp.dma_start(q6[SPLIT + k:SPLIT + k + 1, :, :].rearrange("a h (i p) -> a (h i) p", p=P),
                             part[:, :]).then_inc(maxima_stored, 16)
            for s in range(2):
                wait_apart(sp, xn_stored[s], 16 * B * NC // 2, apart)
                wait_apart(sp, parts_stored[s], 16 * 4 * B * NC // 2, apart)
                wait_apart(sp, vx_stored[s], 16 * NG * B * NC // 2, apart)
                wait_apart(sp, heads_stored[s], 16 * B * NC // 2, apart)
            wait_apart(sp, unit_loaded, N_LOAD, apart)
            wait_apart(sp, next_loaded, N_LOAD, apart)
            wait_apart(sp, maxima_stored, 32, apart)

        @block.gpsimd
        def _(pool):
            nc.gpsimd.memset(ident_b[:, :], 0.0)
            nc.gpsimd.memset(mask_q[:, :], 0.0)
            nc.gpsimd.memset(neg_max[:, :], 0.0)
            nc.gpsimd.memset(piece_max[:, :, :], -3e38)
            nc.gpsimd.memset(ident[:, :], 0.0).then_inc(consts, 1)
            nc.gpsimd.memset(half[:, :], -0.5)
            nc.gpsimd.memset(plus_half[:, :], 0.5).then_inc(consts, 1)
            nc.gpsimd.memset(vx[:, :, :, :, :], 0.0).then_inc(consts, 1)
            wait_apart(pool, consts, 3, apart)
            nc.gpsimd.affine_select(out=ident_b[:, :], in_=ident_b[:, :], compare_op=ALU.not_equal, fill=1.0,
                                    base=0, pattern=[[-1, P]], channel_multiplier=1)
            nc.gpsimd.affine_select(out=mask_q[:, :], in_=mask_q[:, :], compare_op=ALU.is_ge, fill=-BIG,
                                    base=0, pattern=[[-1, P]], channel_multiplier=1)
            nc.gpsimd.affine_select(out=ident[:, :], in_=ident[:, :], compare_op=ALU.not_equal, fill=1.0,
                                    base=0, pattern=[[-1, P]], channel_multiplier=1).then_inc(consts, 1)
            nc.gpsimd.memset(vx[:, :, :, :, DH:DH + 1], 1.0).then_inc(consts, 1)

            def inverse_std(n):
                wait_apart(pool, mv_done, n + 1, apart)
                nc.gpsimd.tensor_scalar(rstd[:, :], mv[:, :, 1], EPS_LN, None, ALU.add).then_inc(rstd_steps, 1)
                wait_apart(pool, rstd_steps, 2 * n + 1, apart)
                nc.gpsimd.tensor_tensor(rstd[:, :], rstd[:, :], half[:, :], ALU.pow).then_inc(rstd_steps, 1)

            def inverse_rms(n, s):
                wait_apart(pool, ss_done, n + 1, apart)
                nc.gpsimd.tensor_scalar(meansq[:, :], ss[:, :], 1.0 / D, EPS_RMS, ALU.mult, ALU.add).then_inc(mean_done, 1)
                wait_apart(pool, mean_done, n + 1, apart)
                nc.gpsimd.tensor_tensor(rrms[:, :], meansq[:, :], half[:, :], ALU.pow).then_inc(rrms_done, 1)
                nc.gpsimd.tensor_tensor(rms[:, s, :], meansq[:, :], plus_half[:, :], ALU.pow).then_inc(rms_done, 1)

            def lower_parts(n, s, j):
                wait_apart(pool, rest_done, 2 + 4 * n + j + 1, apart)
                nc.gpsimd.tensor_copy(parts[:, s, j, 1, :], rest[:, j, :]).then_inc(part1_done, 1)
                wait_apart(pool, part1_done, 4 * n + j + 1, apart)
                nc.gpsimd.tensor_tensor(parts[:, s, j, 2, :], rest[:, j, :], parts[:, s, j, 1, :],
                                        ALU.subtract).then_inc(part2_done, 1)

            inverse_std(0)
            inverse_rms(0, 0)

            def body(b, c, n, follows):
                if follows:
                    inverse_std(n + 1)
                lower_parts(n, c % 2, 0)
                if follows:
                    inverse_rms(n + 1, (c + 1) % 2)
                lower_parts(n, c % 2, 1)
                lower_parts(n, c % 2, 2)
                lower_parts(n, c % 2, 3)
            chunks(pool, body)
            wait_apart(pool, part2_done, 4 * B * NC, apart)
            nc.gpsimd.memset(k6[SPLIT:ROWS, :, :], 1.0).then_inc(ones_set, 1)
            wait_apart(pool, ones_set, 1, apart)

        @block.vector
        def _(dve):
            dve.sem_inc(rest_done, 2)
            dve.sem_inc(row_free, 2)
            def moments(n, s, u):
                dve.wait_ge(x_loaded[s], 16 * (u + 1))
                for t in range(TT):
                    last = nc.vector.bn_stats(stats[:, t, :], x[:, s, t, :])
                last.then_inc(stats_done, 1)
                wait_apart(dve, stats_done, n + 1, apart)
                for t in range(TT):
                    last = nc.vector.bn_aggr(mv[:, t, :], stats[:, t, :])
                last.then_inc(mv_done, 1)

            def normalise(n, s, u):
                dve.wait_ge(rstd_steps, 2 * n + 2)
                dve.wait_ge(xn_stored[s], 16 * u)
                for t in range(TT):
                    last = nc.vector.tensor_scalar(xn[:, s, t, :], x[:, s, t, :], mv[:, t, 0:1], rstd[:, t:t + 1],
                                                   ALU.subtract, ALU.mult)
                last.then_inc(xn_done, 1)

            def scale_rms(n, s):
                dve.wait_ge(rrms_done, n + 1)
                dve.wait_ge(t_done, KD * n)
                for t in range(TT):
                    last = nc.vector.tensor_scalar(h[:, t, :], xn[:, s, t, :], rrms[:, t:t + 1], None, ALU.mult)
                last.then_inc(h_done, 1)

            def subtract_part0(n, s, j):
                dve.wait_ge(part0_done, 4 * n + j + 1)
                dve.wait_ge(part2_done, 4 * n)
                nc.vector.tensor_tensor(rest[:, j, :], qk_ps[j % 2][:, :], parts[:, s, j, 0, :],
                                        ALU.subtract).then_inc(rest_done, 1)

            def reduce_pieces(b, c, spot):
                for m, h, (i, pc, width) in pieces_beside(b, c, spot):
                    dve.wait_ge(row_scored, m + 1)
                    nc.vector.tensor_reduce(piece_max[:, h * KT + i, pc:pc + 1], row_ps[m % 2][:, 0:width], AX_X,
                                            ALU.max).then_inc(row_free, 1)

            def take_heads(n, s, u, t):
                dve.wait_ge(heads_done, TT * n + t + 1)
                if t == 0:
                    dve.wait_ge(rms_done, n + 1)
                    dve.wait_ge(heads_stored[s], 16 * u)
                nc.vector.scalar_tensor_tensor(heads[:, s, t, :, :].rearrange("p i d -> p (i d)"), heads_ps[:, 0:3 * D],
                                               rms[:, s, t:t + 1], bh[:, :, :].rearrange("p i d -> p (i d)"),
                                               ALU.mult, ALU.add).then_inc(heads_taken, 1)

            moments(0, 0, 0)
            normalise(0, 0, 0)
            dve.wait_ge(w_loaded, 16 * 11)
            nc.vector.tensor_scalar(wh[:, :, 0, :], wh[:, :, 0, :], DH ** -0.5, None, ALU.mult)
            nc.vector.tensor_scalar(bh[:, 0, :], bh[:, 0, :], DH ** -0.5, None, ALU.mult)
            for k in range(KD):
                nc.vector.tensor_scalar(wq[:, k, :], wq[:, k, :], g1[:, k:k + 1], DH ** -0.5, ALU.mult, ALU.mult)
                last = nc.vector.tensor_scalar(wdkv[:, k, :], wdkv[:, k, :], g1[:, k:k + 1], None, ALU.mult)
            last.then_inc(w_scaled, 1)
            scale_rms(0, 0)
            dve.wait_ge(w_scaled, 1)

            def body(b, c, n, follows):
                s, s1 = c % 2, (c + 1) % 2
                u, u1 = uses(b, c), uses(b, c + 1)
                if follows:
                    moments(n + 1, s1, u1)
                reduce_pieces(b, c, 0)
                subtract_part0(n, s, 0)
                reduce_pieces(b, c, 1)
                take_heads(n, s, u, 0)
                reduce_pieces(b, c, 2)
                if follows:
                    normalise(n + 1, s1, u1)
                subtract_part0(n, s, 1)
                reduce_pieces(b, c, 3)
                reduce_pieces(b, c, 4)
                take_heads(n, s, u, 1)
                reduce_pieces(b, c, 5)
                if follows:
                    scale_rms(n + 1, s1)
                take_heads(n, s, u, 2)
                reduce_pieces(b, c, 6)
                subtract_part0(n, s, 2)
                reduce_pieces(b, c, 7)
                subtract_part0(n, s, 3)
                take_heads(n, s, u, 3)
                reduce_pieces(b, c, 8)
                reduce_pieces(b, c, 9)
            chunks(dve, body)
            dve.wait_ge(row_free, 2 + HG * len(HEAD_PIECES))
            nc.vector.tensor_reduce(neg_max[:, 0:HG * KT], piece_max[:, :, :], AX_X, ALU.max, negate=True
                                    ).then_inc(maxima_steps, 1)
            dve.wait_ge(maxima_steps, 2)
            nc.vector.tensor_copy(neg_hi[:, :], t_ps[0:HG * KT, 0:P]).then_inc(maxima_steps, 1)
            dve.wait_ge(maxima_steps, 3)
            nc.vector.tensor_tensor(neg_lo[:, :], t_ps[0:HG * KT, 0:P], neg_hi[:, :], ALU.subtract).then_inc(maxima_steps, 1)

        @block.scalar
        def _(act):
            def squares(n, s):
                act.wait_ge(xn_done, n + 1)
                act.wait_ge(mean_done, n)
                for t in range(TT):
                    last = nc.scalar.activation(sq[:, t, :], xn[:, s, t, :], ACT.Square, accum_out=ss[:, t:t + 1])
                last.then_inc(ss_done, 1)

            def part0(b, c, n, s, j):
                act.wait_ge(qk_done, 4 * n + j + 1)
                act.wait_ge(parts_stored[s], 64 * uses(b, c))
                nc.scalar.copy(parts[:, s, j, 0, :], qk_ps[j % 2][:, :]).then_inc(part0_done, 1)

            def copy_hT(n, s, k):
                act.wait_ge(t_done, KD * n + k + 1)
                nc.scalar.copy(hT[:, s, k, :], t_ps[:, :]).then_inc(hT_done, 1)

            act.wait_ge(consts, 5)
            squares(0, 0)
            for k in range(KD):
                copy_hT(0, 0, k)

            def body(b, c, n, follows):
                s = c % 2
                part0(b, c, n, s, 0)
                part0(b, c, n, s, 1)
                if follows:
                    squares(n + 1, (c + 1) % 2)
                act.wait_ge(c_done, n + 1)
                act.wait_ge(v_done, 2 * n)
                nc.scalar.copy(cT[:, :], cv_ps[:, :]).then_inc(cT_done, 1)
                part0(b, c, n, s, 2)
                part0(b, c, n, s, 3)
                act.wait_ge(vx_stored[s], 16 * NG * uses(b, c))
                for i in range(2):
                    if follows:
                        act.wait_ge(heads_done, TT * n)
                        copy_hT(n + 1, (c + 1) % 2, i)
                    act.wait_ge(v_done, 2 * n + i + 1)
                    nc.scalar.copy(vx[:, s, 2 * i:2 * i + 2, :, 0:DH],
                                   cv_ps[:, :].rearrange("p (t h d) -> p t h d", t=2, h=H)).then_inc(vx_done, 1)
            chunks(act, body)

        @block.tensor
        def _(pe):
            def transpose_h(n, k):
                pe.wait_ge(h_done, n + 1)
                pe.wait_ge(hT_done, KD * n + k)
                for t in range(TT):
                    last = nc.tensor.transpose(t_ps[:, t * P:(t + 1) * P], h[:, t, k * P:(k + 1) * P], ident[:, :])
                last.then_inc(t_done, 1)

            def score_pieces(b, c, spot):
                for m, head, piece in pieces_beside(b, c, spot):
                    if m == 0:
                        pe.wait_ge(unit_loaded, N_LOAD)
                    pe.wait_ge(row_free, m + 1)
                    row_piece(nc, row_ps[m % 2], q6, k6, head, piece, ident_b, mask_q).then_inc(row_scored, 1)

            def values(n, i):
                pe.wait_ge(vx_done, 2 * n + i)
                for t in range(2):
                    tok = (2 * i + t) * P
                    last = nc.tensor.matmul(cv_ps[:, t * D:(t + 1) * D], cT[:, tok:tok + P], wuv[:, :], start=True, stop=True)
                last.then_inc(v_done, 1)

            def queries(n, s, m):
                pe.wait_ge(rest_done, 4 * n + m + 1)
                for k in range(KD):
                    last = nc.tensor.matmul(qk_ps[m][:, :], wq[:, k, m * P:(m + 1) * P], hT[:, s, k, :],
                                            start=k == 0, stop=k == KD - 1)
                last.then_inc(qk_done, 1)

            def keys(n, m):
                pe.wait_ge(cT_done, n + 1)
                pe.wait_ge(rest_done, 4 * n + 2 + m + 1)
                nc.tensor.matmul(qk_ps[m][:, :], wuk[:, m * P:(m + 1) * P], cT[:, :],
                                 start=True, stop=True).then_inc(qk_done, 1)

            def head_rows(n, s, t):
                pe.wait_ge(heads_taken, TT * n + t)
                for k in range(KD):
                    nc.tensor.matmul(heads_ps[:, 0:2 * D], hT[:, s, k, t * P:(t + 1) * P],
                                     wh[:, k, 0:2, :].rearrange("p i d -> p (i d)"), start=k == 0, stop=k == KD - 1)
                for k in range(KD):
                    last = nc.tensor.matmul(heads_ps[:, 2 * D:3 * D], hT[:, s, k, t * P:(t + 1) * P], wh[:, k, 2, :],
                                            start=k == 0, stop=k == KD - 1)
                last.then_inc(heads_done, 1)

            pe.wait_ge(consts, 5)
            for k in range(KD):
                transpose_h(0, k)
            pe.wait_ge(w_scaled, 1)

            def body(b, c, n, follows):
                s = c % 2
                pe.wait_ge(hT_done, KD * n + KD)
                queries(n, s, 0)
                score_pieces(b, c, 0)
                head_rows(n, s, 0)
                score_pieces(b, c, 1)
                queries(n, s, 1)
                score_pieces(b, c, 2)
                pe.wait_ge(vx_done, 2 * n)
                for k in range(KD):
                    last = nc.tensor.matmul(cv_ps[:, :], wdkv[:, k, :], hT[:, s, k, :], start=k == 0, stop=k == KD - 1)
                last.then_inc(c_done, 1)
                score_pieces(b, c, 3)
                head_rows(n, s, 1)
                score_pieces(b, c, 4)
                keys(n, 0)
                score_pieces(b, c, 5)
                head_rows(n, s, 2)
                score_pieces(b, c, 6)
                keys(n, 1)
                if follows:
                    transpose_h(n + 1, 0)
                values(n, 0)
                score_pieces(b, c, 7)
                head_rows(n, s, 3)
                score_pieces(b, c, 8)
                if follows:
                    transpose_h(n + 1, 1)
                score_pieces(b, c, 9)
                values(n, 1)
            chunks(pe, body)
            pe.wait_ge(hT_done, KD * B * NC)
            pe.wait_ge(maxima_steps, 1)
            nc.tensor.transpose(t_ps[:, 0:P], neg_max[:, :], ident[:, :]).then_inc(maxima_steps, 1)


def phase2_attend(nc, apart, qk_heads, v_units, o_dram, head_qkv, attn_rows, first_units):
    UNITS = HEAD_BLOCKS // 2
    assert UNITS == B * NG
    STEPS = [(c, kt) for c in range(NC) for kt in range(TT * (c + 1))]
    N_STEP = len(STEPS)
    LAST = [max(i for i, (c, _) in enumerate(STEPS) if c == cc) for cc in range(NC)]
    PIECES = [(h, CT // width if CT % width == 0 else 1, (i, pc, width)) for i, pc, width in HEAD_PIECES
              for h in range(0, HG, CT // width if CT % width == 0 else 1)]
    N_PIECE = len(PIECES)
    SLOTS = 3
    RING = 3
    LAG = 2
    AHEAD = 3
    skipped = lambda c, kt: max(0, kt - TT * c) * P
    step_cost = [CT + CT - skipped(c, kt) for c, kt in STEPS[:N_STEP - AHEAD]]
    piece_cost = [P // 2 + heads * width for _, heads, (_, _, width) in PIECES]
    PIECES_BY = [sum(sum(piece_cost[:m + 1]) * sum(step_cost) <= sum(step_cost[:i + 1]) * sum(piece_cost)
                     for m in range(N_PIECE)) for i in range(N_STEP)]
    assert PIECES_BY[N_STEP - AHEAD - 1] == N_PIECE

    with ExitStack() as ctx:
        sb = lambda name, shape, dt=F32: ctx.enter_context(nc.sbuf_tensor(name, shape, dt))
        sem = lambda name: ctx.enter_context(nc.semaphore(name))

        ident = sb("p2_ident", [P, P])
        ident_b = sb("p2_ident_b", [P, P], BF16)
        mask_q = sb("p2_mask_q", [P, P], BF16)
        mask_k = sb("p2_mask_k", [P, P], BF16)
        slots = [*first_units, (sb("p2_q6", [ROWS, HG, S], BF16), sb("p2_k6", [ROWS, HG, S], BF16),
                                sb("p2_vg", [P, KT, HG * VW]))]
        assert len(slots) == SLOTS
        q6, k6, vg = zip(*slots)
        probs = sb("p2_probs", [P, 2 * (LAG + 1), 2, CT])
        piece_max = sb("p2_piece_max", [P, HG, KT, NC])
        neg_max = sb("p2_neg_max", [P, P])
        neg_hi = sb("p2_neg_hi", [HG * KT, P], BF16)
        neg_lo = sb("p2_neg_lo", [HG * KT, P], BF16)
        pv_sb = sb("p2_pv_sb", [P, 2, CT])
        pv_t = sb("p2_pv_t", [P, CT // VW, VW])
        inv = sb("p2_inv", [P, CT // VW])
        o_sb = sb("p2_o", [P, 2, CT])

        head_in = sb("p2_head_in", [P, 2, 3, H, DH])
        terms = sb("p2_terms", [P, H, H, DH])
        head_s = sb("p2_head_s", [P, 2, H, H])
        head_max = sb("p2_head_max", [P, H])
        head_p = sb("p2_head_p", [P, 2, H, H])
        head_sum = sb("p2_head_sum", [P, H, H // 2])
        head_inv = sb("p2_head_inv", [P, H])
        minus_one = sb("p2_minus_one", [P, H])
        head_o = sb("p2_head_o", [P, 2, H, DH])

        ring_ps = [ctx.enter_context(nc.psum_tensor(f"p2_ring{i}", [P, CT], F32)) for i in range(RING)]
        st_ps = [ctx.enter_context(nc.psum_tensor(f"p2_st{i}", [P, 2, CT], F32)) for i in range(2)]
        pv_ps = ctx.enter_context(nc.psum_tensor("p2_pv", [P, CT], F32))

        consts = sem("p2_consts")
        loaded = [sem(f"p2_loaded{s}") for s in range(SLOTS)]
        ring_filled = sem("p2_ring_filled")
        ring_free = sem("p2_ring_free")
        neg_max_done = sem("p2_neg_max_done")
        neg_hi_done = sem("p2_neg_hi_done")
        neg_rows_done = sem("p2_neg_rows_done")
        neg_stored = sem("p2_neg_stored")
        st_scored = sem("p2_st_scored")
        probs_done = sem("p2_probs_done")
        pv_done = sem("p2_pv_done")
        pv_copied = sem("p2_pv_copied")
        pv_turned = sem("p2_pv_turned")
        inv_done = sem("p2_inv_done")
        scaled = sem("p2_scaled")
        o_done = sem("p2_o_done")
        ones_set = sem("p2_ones_set")
        head_loaded = [sem(f"p2_head_loaded{s}") for s in range(2)]
        head_steps = sem("p2_head_steps")
        head_scored = sem("p2_head_scored")
        head_max_done = sem("p2_head_max_done")
        head_shifted = sem("p2_head_shifted")
        head_probs_done = sem("p2_head_probs_done")
        head_done = sem("p2_head_done")
        head_stored = [sem(f"p2_head_stored{s}") for s in range(2)]
        o_stored = [sem(f"p2_o_stored{s}") for s in range(2)]
        block = ctx.enter_context(nc.Block())

        SHIFT_AT = (12, 20)

        def turn_of(s, i):
            return (N_STEP * s + i) % (LAG + 1)
        assert SLOTS * N_STEP % (LAG + 1) == 0

        N_ITEM = N_PIECE + 1
        assert SLOTS * N_ITEM % RING == 0

        def ring_item(n, s, r):
            return N_ITEM * n + r, (N_ITEM * s + r) % RING

        def units(eng, body):
            with eng.Fori(0, (UNITS - 1) // SLOTS) as j:
                for s in range(SLOTS):
                    body(SLOTS * j + s, s, True, j)
            body(UNITS - 1, (UNITS - 1) % SLOTS, False, (UNITS - 1) // SLOTS)

        def next_round(j, s):
            return j + (s + 1) // SLOTS

        def load(sp, n, s):
            load_unit(sp, qk_heads, v_units, n, q6[s], k6[s], vg[s], loaded[s])

        @block.sync
        def _(sp):
            def store_neg_rows(n, s):
                wait_apart(sp, neg_rows_done, n + 1, apart)
                for r, part in enumerate((neg_hi, neg_lo)):
                    sp.dma_start(q6[s][SPLIT + r:SPLIT + r + 1, :, :].rearrange("a h (i p) -> a (h i) p", p=P),
                                 part[:, :]).then_inc(neg_stored, 16)

            def store_o(n, c):
                wait_apart(sp, o_done, NC * n + c + 1, apart)
                for h in range(HG):
                    sp.dma_start(o_dram[bass.ds(n, 1), h * DH:(h + 1) * DH, c * CT:(c + 1) * CT].rearrange("a d t -> d (a t)"),
                                 o_sb[h * VW:h * VW + DH, c % 2, :]).then_inc(o_stored[c % 2], 16)

            sp.sem_inc(loaded[0], N_LOAD)
            sp.sem_inc(loaded[1], N_LOAD)
            sp.sem_inc(neg_stored, 32)

            def body(n, s, loads, has_next):
                if loads:
                    wait_apart(sp, pv_done, LAG + 1 + N_STEP * n, apart)
                    load(sp, n + 2, (s + 2) % SLOTS)
                for c in range(NC - 1):
                    store_o(n, c)
                if has_next:
                    store_neg_rows(n + 1, (s + 1) % SLOTS)
                store_o(n, NC - 1)
            rounds = (UNITS - 2) // SLOTS
            with sp.Fori(0, rounds) as j:
                for s in range(SLOTS):
                    body(SLOTS * j + s, s, True, True)
            for n in range(SLOTS * rounds, UNITS):
                body(n, n % SLOTS, n + 2 < UNITS, n + 1 < UNITS)
            for s in range(2):
                wait_apart(sp, o_stored[s], 16 * HG * UNITS * NC // 2, apart)

        @block.gpsimd
        def _(pool):
            nc.gpsimd.memset(ident[:, :], 0.0)
            nc.gpsimd.memset(ident_b[:, :], 0.0)
            nc.gpsimd.memset(mask_q[:, :], 0.0)
            nc.gpsimd.memset(mask_k[:, :], 0.0)
            nc.gpsimd.memset(neg_max[:, :], 0.0)
            nc.gpsimd.memset(piece_max[:, :, :, :], -3e38).then_inc(consts, 1)
            wait_apart(pool, consts, 1, apart)
            for m in (ident, ident_b):
                nc.gpsimd.affine_select(out=m[:, :], in_=m[:, :], compare_op=ALU.not_equal, fill=1.0,
                                        base=0, pattern=[[-1, P]], channel_multiplier=1)
            nc.gpsimd.affine_select(out=mask_q[:, :], in_=mask_q[:, :], compare_op=ALU.is_ge, fill=-BIG,
                                    base=0, pattern=[[-1, P]], channel_multiplier=1)
            nc.gpsimd.affine_select(out=mask_k[:, :], in_=mask_k[:, :], compare_op=ALU.is_ge, fill=-BIG,
                                    base=0, pattern=[[1, P]], channel_multiplier=-1).then_inc(consts, 1)
            wait_apart(pool, consts, 2, apart)
            nc.gpsimd.memset(minus_one[:, :], -1.0).then_inc(head_steps, 1)
            STEPS_A, STEPS_B = 4, 10

            def steps(scored, weighed):
                return 1 + STEPS_A * scored + STEPS_B * weighed

            def load_heads(m, u):
                pool.dma_start(head_in[:, u, :, :, :].rearrange("p i h d -> p (i h d)"),
                               head_qkv[bass.ds(m, 1), :, :].rearrange("a p d -> p (a d)")).then_inc(head_loaded[u], 16)

            def step(ins, count):
                ins.then_inc(head_steps, 1)
                wait_apart(pool, head_steps, count, apart)

            def score_heads(m, u, loads, before):
                wait_apart(pool, head_loaded[u], 16 * loads, apart)
                step(nc.gpsimd.tensor_tensor(
                    terms[:, :, :, :], head_in[:, u, 0, :, :].unsqueeze(2).to_broadcast([P, H, H, DH]),
                    head_in[:, u, 1, :, :].unsqueeze(1).to_broadcast([P, H, H, DH]), ALU.mult), before + 1)
                width = DH // 2
                for k in range(STEPS_A - 1):
                    step(nc.gpsimd.tensor_tensor(terms[:, :, :, 0:width], terms[:, :, :, 0:width],
                                                 terms[:, :, :, width:2 * width], ALU.add), before + 2 + k)
                    width //= 2
                nc.gpsimd.tensor_tensor(head_s[:, u, :, :], terms[:, :, :, 0], terms[:, :, :, 1], ALU.add
                                        ).then_inc(head_scored, 1)
                wait_apart(pool, head_scored, m + 1, apart)

            def weigh_heads(m, u, stores, before):
                wait_apart(pool, head_probs_done, m + 1, apart)
                step(nc.gpsimd.tensor_tensor(
                    terms[:, :, :, :], head_p[:, u, :, :].unsqueeze(2).to_broadcast([P, H, DH, H]),
                    head_in[:, u, 2, :, :].rearrange("p j d -> p d j").unsqueeze(1).to_broadcast([P, H, DH, H]),
                    ALU.mult), before + 1)
                width = H // 2
                for k in range(3):
                    step(nc.gpsimd.tensor_tensor(terms[:, :, :, 0:width], terms[:, :, :, 0:width],
                                                 terms[:, :, :, width:2 * width], ALU.add), before + 2 + k)
                    width //= 2
                src, width = head_p[:, u, :, :], H // 2
                for k in range(4):
                    step(nc.gpsimd.tensor_tensor(head_sum[:, :, 0:width], src[:, :, 0:width],
                                                 src[:, :, width:2 * width], ALU.add), before + 5 + k)
                    src, width = head_sum[:, :, :], width // 2
                step(nc.gpsimd.tensor_tensor(head_inv[:, :], head_sum[:, :, 0], minus_one[:, :], ALU.pow), before + 9)
                wait_apart(pool, head_stored[u], 16 * stores, apart)
                step(nc.gpsimd.tensor_tensor(head_o[:, u, :, :], terms[:, :, :, 0], terms[:, :, :, 1], ALU.add), before + 10)
                nc.gpsimd.tensor_tensor(head_o[:, u, :, :], head_o[:, u, :, :],
                                        head_inv[:, :].unsqueeze(2).to_broadcast([P, H, DH]), ALU.mult).then_inc(head_done, 1)
                wait_apart(pool, head_done, 2 + m + 1, apart)
                pool.dma_start(attn_rows[bass.ds(m, 1), :, :].rearrange("a p d -> p (a d)"),
                               head_o[:, u, :, :].rearrange("p h d -> p (h d)")).then_inc(head_stored[u], 16)

            wait_apart(pool, head_steps, 1, apart)
            load_heads(0, 0)
            load_heads(1, 1)
            for u in range(2):
                score_heads(u, u, 1, steps(u, 0))
                nc.gpsimd.memset(k6[1 + u][SPLIT:ROWS, :, :], 1.0).then_inc(ones_set, 1)
                wait_apart(pool, ones_set, 1 + u, apart)
            with pool.Fori(0, UNITS - 1) as n:
                for u in range(2):
                    weigh_heads(2 * n + u, u, n, steps(2 * n + 2, 2 * n + u))
                    load_heads(2 * n + 2 + u, u)
                for u in range(2):
                    score_heads(2 * n + 2 + u, u, n + 2, steps(2 * n + 2 + u, 2 * n + 2))
            for u in range(2):
                weigh_heads(2 * (UNITS - 1) + u, u, UNITS - 1, steps(2 * UNITS, 2 * (UNITS - 1) + u))
            for u in range(2):
                wait_apart(pool, head_stored[u], 16 * UNITS, apart)

        @block.vector
        def _(dve):
            dve.sem_inc(ring_free, RING)
            for done in (neg_max_done, neg_hi_done, neg_rows_done):
                dve.sem_inc(done, 1)
            dve.sem_inc(head_done, 2)
            dve.sem_inc(pv_turned, 2)
            dve.wait_ge(consts, 2)

            def reduce_piece(m, g, bank):
                h, heads, (i, pc, width) = PIECES[m]
                dve.wait_ge(ring_filled, g + 1)
                nc.vector.tensor_reduce(piece_max[:, h:h + heads, i, pc],
                                        ring_ps[bank][:, 0:heads * width].rearrange("p (h k) -> p h k", h=heads), AX_X,
                                        ALU.max).then_inc(ring_free, 1)

            def reduce_pieces(n, last_piece):
                dve.wait_ge(ring_free, RING + last_piece + 1)
                nc.vector.tensor_reduce(neg_max[:, 0:HG * KT], piece_max[:, :, :, :].rearrange("p h i c -> p (h i) c"), AX_X, ALU.max, negate=True
                                        ).then_inc(neg_max_done, 1)

            def split_maxima(n, g, bank):
                dve.wait_ge(ring_filled, g + 1)
                dve.wait_ge(neg_stored, 32 * n)
                nc.vector.tensor_copy(neg_hi[:, :], ring_ps[bank][0:HG * KT, 0:P]).then_inc(neg_hi_done, 1)
                dve.wait_ge(neg_hi_done, n + 1)
                nc.vector.tensor_tensor(neg_lo[:, :], ring_ps[bank][0:HG * KT, 0:P], neg_hi[:, :], ALU.subtract
                                        ).then_inc(neg_rows_done, 1)
                dve.wait_ge(neg_rows_done, n + 1)
                dve.sem_inc(ring_free, 1)

            def turn(n, c):
                dve.wait_ge(pv_copied, NC * n + c + 1)
                dve.wait_ge(o_done, NC * n + c)
                nc.vector.transpose(pv_t[:, :, :].rearrange("p j v -> p (j v)"), pv_sb[:, c % 2, :]).then_inc(pv_turned, 1)

            def invert_sums(n, c):
                dve.wait_ge(pv_turned, 2 + NC * n + c + 1)
                nc.vector.reciprocal(inv[:, :], pv_t[:, :, DH]).then_inc(inv_done, 1)

            def normalise(n, c):
                dve.wait_ge(inv_done, NC * n + c + 1)
                nc.vector.tensor_tensor(pv_t[:, :, 0:DH], pv_t[:, :, 0:DH],
                                        inv[:, :].unsqueeze(2).to_broadcast([P, CT // VW, DH]), ALU.mult).then_inc(scaled, 1)

            def turn_back(n, c):
                dve.wait_ge(scaled, NC * n + c + 1)
                dve.wait_ge(o_stored[c % 2], 16 * HG * (NC // 2 * n + c // 2))
                nc.vector.transpose(o_sb[:, c % 2, :], pv_t[:, :, :].rearrange("p j v -> p (j v)")).then_inc(o_done, 1)

            def shift_heads(m, u):
                dve.wait_ge(head_scored, m + 1)
                nc.vector.tensor_reduce(head_max[:, :], head_s[:, u, :, :], AX_X, ALU.max).then_inc(head_max_done, 1)
                dve.wait_ge(head_max_done, m + 1)
                nc.vector.tensor_tensor(head_s[:, u, :, :], head_s[:, u, :, :],
                                        head_max[:, :].unsqueeze(2).to_broadcast([P, H, H]), ALU.subtract
                                        ).then_inc(head_shifted, 1)

            def body(n, s, has_next, j):
                done = 0
                for i in range(N_STEP):
                    if i in SHIFT_AT:
                        u = SHIFT_AT.index(i)
                        shift_heads(2 * n + u, u)
                    upto = PIECES_BY[i] if has_next else 0
                    for c in range(NC - 1):
                        for k, finish in enumerate((turn, invert_sums, normalise, turn_back)):
                            if i == LAST[c] + LAG + 2 + k:
                                finish(n, c)
                    for m in range(done, upto):
                        reduce_piece(m, *ring_item(n, s, m))
                    if done < upto == N_PIECE:
                        reduce_pieces(n + 1, ring_item(n, s, N_PIECE - 1)[0])
                    done = upto
                    if has_next and i == N_STEP - AHEAD + 1:
                        split_maxima(n + 1, *ring_item(n, s, N_PIECE))
                for finish in (turn, invert_sums, normalise, turn_back):
                    finish(n, NC - 1)
            units(dve, body)

        @block.scalar
        def _(act):
            act.sem_inc(pv_done, LAG + 1)
            act.sem_inc(probs_done, 2)

            def exps(n, s, i, u):
                c, kt = STEPS[i]
                width = CT - max(0, kt - TT * c) * P
                act.wait_ge(st_scored, 2 * (N_STEP * n + i) + u + 1)
                act.wait_ge(pv_done, N_STEP * n + i + 1)
                nc.scalar.activation(probs[:, 2 * turn_of(s, i) + u, :, 0:width], st_ps[u][:, :, 0:width], ACT.Exp
                                     ).then_inc(probs_done, 1)

            def head_probs(m, u):
                act.wait_ge(head_shifted, m + 1)
                act.wait_ge(head_done, m + 1)
                nc.scalar.activation(head_p[:, u, :, :], head_s[:, u, :, :], ACT.Exp).then_inc(head_probs_done, 1)

            def copy_pv(n, c):
                act.wait_ge(pv_done, LAG + 1 + N_STEP * n + LAST[c] + 1)
                act.wait_ge(pv_turned, NC * n + c + 1)
                nc.scalar.copy(pv_sb[:, c % 2, :], pv_ps[:, :]).then_inc(pv_copied, 1)

            def body(n, s, has_next, j):
                for i in range(N_STEP):
                    if i - 2 in SHIFT_AT:
                        u = SHIFT_AT.index(i - 2)
                        head_probs(2 * n + u, u)
                    exps(n, s, i, 0)
                    exps(n, s, i, 1)
                    for c in range(NC - 1):
                        if i == LAST[c] + LAG:
                            copy_pv(n, c)
                copy_pv(n, NC - 1)
            units(act, body)

        @block.tensor
        def _(pe):
            def row_scores(s, m, rnd, g, bank):
                h, heads, piece = PIECES[m]
                if m == 0:
                    pe.wait_ge(loaded[s], N_LOAD * (rnd + 1))
                pe.wait_ge(ring_free, g + 1)
                for k in range(heads):
                    last = row_piece(nc, ring_ps[bank][:, k * piece[2]:(k + 1) * piece[2]], q6[s], k6[s], h + k, piece,
                                     ident_b, mask_q)
                last.then_inc(ring_filled, 1)

            def transpose_max(n, g, bank):
                pe.wait_ge(neg_max_done, n + 1)
                pe.wait_ge(ring_free, g + 1)
                nc.tensor.transpose(ring_ps[bank][:, 0:P], neg_max[:, :], ident[:, :]).then_inc(ring_filled, 1)

            def scores(n, s, i, u):
                c, kt = STEPS[i]
                skip = max(0, kt - TT * c) * P
                width = CT - skip
                if i == 0 and u == 0:
                    pe.wait_ge(neg_stored, 32 * (n + 1))
                    if s:
                        pe.wait_ge(ones_set, s)
                pe.wait_ge(probs_done, 2 * (N_STEP * n + i) + u + 1)
                diagonal = kt >= TT * c
                for j in range(2):
                    hh = 2 * u + j
                    last = nc.tensor.matmul(st_ps[u][:, j, 0:width], k6[s][:, hh, kt * P:(kt + 1) * P],
                                            q6[s][:, hh, c * CT + skip:(c + 1) * CT], start=True, stop=not diagonal)
                    if diagonal:
                        last = nc.tensor.matmul(st_ps[u][:, j, 0:P], ident_b[:, :], mask_k[:, :], start=False, stop=True)
                last.then_inc(st_scored, 1)

            def values(n, s, i):
                c, kt = STEPS[i]
                skip = max(0, kt - TT * c) * P
                if kt == 0:
                    pe.wait_ge(pv_copied, NC * n + c)
                pe.wait_ge(probs_done, 2 + 2 * (N_STEP * n + i) + 2)
                for hh in range(HG):
                    last = nc.tensor.matmul(pv_ps[hh * VW:(hh + 1) * VW, skip:CT], vg[s][:, kt, hh * VW:(hh + 1) * VW],
                                            probs[:, 2 * turn_of(s, i) + hh // 2, hh % 2, 0:CT - skip],
                                            start=kt == 0, stop=kt == TT * (c + 1) - 1, skip_group_check=True)
                last.then_inc(pv_done, 1)

            pe.wait_ge(consts, 2)

            def body(n, s, has_next, j):
                def maxima(first, end):
                    for m in range(first, end):
                        row_scores((s + 1) % SLOTS, m, next_round(j, s), *ring_item(n, s, m))

                done = 0
                for i in range(N_STEP):
                    upto = PIECES_BY[i] if has_next else 0
                    cut = [done + k * (upto - done) // 4 for k in range(5)]
                    done = upto
                    maxima(cut[0], cut[1])
                    scores(n, s, i, 0)
                    maxima(cut[1], cut[2])
                    scores(n, s, i, 1)
                    maxima(cut[2], cut[3])
                    if i >= LAG:
                        values(n, s, i - LAG)
                    maxima(cut[3], cut[4])
                    if has_next and i == N_STEP - AHEAD + 1:
                        transpose_max(n + 1, *ring_item(n, s, N_PIECE))
                for i in range(N_STEP - LAG, N_STEP):
                    values(n, s, i)
            units(pe, body)


ROW_TILE = 256
CAP = T + ROW_TILE
N_TILE = T * 2 // ROW_TILE + E
SORTED = E * CAP + E * ROW_TILE


def phase3_route(nc, apart, x_v, xn_v, o_v, w, sorted_rows, res_v, pos_v, gates_v, table):
    with ExitStack() as ctx:
        sb = lambda name, shape, dt=F32: ctx.enter_context(nc.sbuf_tensor(name, shape, dt))
        sem = lambda name: ctx.enter_context(nc.semaphore(name))
        bank = lambda name: ctx.enter_context(nc.psum_tensor(name, [P, CT], F32))

        ident = sb("p3_ident", [P, P])
        before = sb("p3_before", [P, P], BF16)
        ones = sb("p3_ones", [P, P], BF16)
        iota_e = sb("p3_iota_e", [P, E])
        iota_tile = sb("p3_iota_tile", [P, N_TILE])
        half = sb("p3_minus_half", [P, TT])
        zeros = sb("p3_zeros", [P, D])
        wo = sb("p3_wo", [P, KD, D])
        gate_w = sb("p3_gate_w", [P, KD, E])
        g2 = sb("p3_g2", [P, D])
        x = sb("p3_x", [P, NC, TT, D])
        xn = sb("p3_xn", [P, NC, TT, D])
        oT = sb("p3_oT", [P, NC, KD, CT])
        x2 = sb("p3_x2", [P, TT, D])
        sq = sb("p3_sq", [P, TT, D])
        ss = sb("p3_ss", [P, TT])
        rrms = sb("p3_rrms", [P, TT])
        res = sb("p3_res", [P, 2, TT, D])
        th = sb("p3_th", [P, NC, TT, D])
        tT = sb("p3_tT", [P, KD, CT])
        logits = sb("p3_logits", [P, TT, E])
        top = sb("p3_top", [P, TT, E])
        top_i = sb("p3_top_i", [P, TT, E], U32)
        top_f = sb("p3_top_f", [P, TT, 2])
        chosen = sb("p3_chosen", [P, TT, 2, E])
        either = sb("p3_either", [P, TT, E], BF16)
        diff = sb("p3_diff", [P, TT])
        ediff = sb("p3_ediff", [P, TT])
        denom = sb("p3_denom", [P, TT])
        gates = sb("p3_gates", [P, 2, TT, 2])
        base = sb("p3_base", [P, E])
        place = sb("p3_place", [P, TT, E])
        picked = sb("p3_picked", [P, TT, 2, E])
        pos_f = sb("p3_pos_f", [P, TT, 2])
        pos_all = sb("p3_pos_all", [P, B * NC * TT * 2])
        pos_sum = sb("p3_pos_sum", [P, B * NC * TT * 2])
        behind = sb("p3_behind", [P, 2, B * NC * TT * 2])
        pos_out = sb("p3_pos_out", [P, B * NC * TT * 2], U32)
        pos = sb("p3_pos", [P, NC, TT, 2], U32)
        region = sb("p3_region", [P, E])
        tail = sb("p3_tail", [P, E], mybir.dt.int32)
        count = sb("p3_count", [P, E])
        count_i = sb("p3_count_i", [P, E], mybir.dt.int32)
        tiles = sb("p3_tiles", [P, E])
        ends = sb("p3_ends", [P, E])
        ones_e = sb("p3_ones_e", [P, E])
        jump = sb("p3_jump", [P, E])
        past = sb("p3_past", [P, N_TILE, E])
        past_j = sb("p3_past_j", [P, N_TILE, E])
        table_f = sb("p3_table_f", [P, 2, N_TILE])
        table_i = sb("p3_table_i", [P, 2, N_TILE], mybir.dt.int32)

        mla_ps = [bank(f"p3_mla{i}_ps") for i in range(2)]
        tT_ps = [bank(f"p3_tT{k}_ps") for k in range(KD)]
        small_ps = bank("p3_small_ps")
        logit_bank = bank("p3_logit_ps")
        logit_ps = logit_bank[:, 0:TT * E].rearrange("p (t e) -> p t e", e=E)
        rank_ps = small_ps[:, 0:TT * E].rearrange("p (t e) -> p t e", e=E)
        total_ps = small_ps[:, TT * E:TT * E + E]

        w_loaded = sem("p3_w_loaded")
        small_loaded = sem("p3_small_loaded")
        consts = sem("p3_consts")
        loaded = [sem(f"p3_loaded{c}") for c in range(NC)]
        mla_done = sem("p3_mla_done")
        x2_done = sem("p3_x2_done")
        ss_done = sem("p3_ss_done")
        rms_steps = sem("p3_rms_steps")
        res_done = sem("p3_res_done")
        th_done = sem("p3_th_done")
        tT_done = sem("p3_tT_done")
        tT_copied = sem("p3_tT_copied")
        logit_done = sem("p3_logit_done")
        chain = sem("p3_chain")
        diff_done = sem("p3_diff_done")
        ediff_done = sem("p3_ediff_done")
        either_done = sem("p3_either_done")
        rank_done = sem("p3_rank_done")
        place_done = sem("p3_place_done")
        gates_done = sem("p3_gates_done")
        pos_done = sem("p3_pos_done")
        scattered = [sem(f"p3_scattered{c}") for c in range(NC)]
        tail_done = sem("p3_tail_done")
        tail_stored = sem("p3_tail_stored")
        res_stored = [sem(f"p3_res_stored{s}") for s in range(2)]
        place_stored = [sem(f"p3_place_stored{s}") for s in range(2)]
        table_done = sem("p3_table_done")
        table_stored = sem("p3_table_stored")
        block = ctx.enter_context(nc.Block())
        ALL = B * NC
        N_LOADED = 16 * 3

        def chunks(eng, body):
            with eng.Fori(0, B - 1) as b:
                for c in range(NC):
                    body(b, c, NC * b + c, NC)
            for c in range(NC):
                body(B - 1, c, NC * (B - 1) + c, NC - 1 - c)

        def after(b, c):
            return (b, c) if c < NC else (b + 1, c - NC)

        def uses(b, c):
            return (NC // 2) * b + c // 2

        @block.sync
        def _(sp):
            def load(b, c):
                sp.dma_start(oT[:, c, :, :], o_v[b, c]).then_inc(loaded[c], 16)
                sp.dma_start(xn[:, c, :, :], xn_v[b, c]).then_inc(loaded[c], 16)
                sp.dma_start(x[:, c, :, :], x_v[b, c]).then_inc(loaded[c], 16)

            sp.dma_start(wo[:, :, :], w["ffn_Wo"].rearrange("(k p) n -> p k n", p=P)).then_inc(w_loaded, 16)
            load(0, 0)
            sp.dma_start(g2[:, :], w["ffn_g2"].partition_broadcast(P)).then_inc(small_loaded, 16)
            sp.dma_start(gate_w[:, :, :], w["ffn_gate_w"].rearrange("(k p) n -> p k n", p=P)).then_inc(small_loaded, 16)
            for c in range(1, NC):
                load(0, c)

            def store_res(b, c):
                sp.dma_start(res_v[b, c], res[:, c % 2, :, :]).then_inc(res_stored[c % 2], 16)

            wait_apart(sp, res_done, 1, apart)
            store_res(0, 0)

            def body(b, c, n, ahead):
                if ahead >= NC:
                    wait_apart(sp, res_done, n + 1, apart)
                    load(b + 1, c)
                if ahead >= 1:
                    wait_apart(sp, res_done, n + 2, apart)
                    store_res(*after(b, c + 1))
                wait_apart(sp, gates_done, n + 1, apart)
                sp.dma_start(gates_v[b, c], gates[:, c % 2, :, :]).then_inc(place_stored[c % 2], 16)
            chunks(sp, body)
            wait_apart(sp, consts, 1, apart)
            sp.dma_start(sorted_rows[E * CAP:SORTED, :].rearrange("(r p) d -> p r d", p=P),
                         zeros[:, :].unsqueeze(1).to_broadcast([P, E * ROW_TILE // P, D])).then_inc(tail_stored, 16)
            wait_apart(sp, tail_done, 1, apart)
            for e in range(E):
                row = sp.value_load(tail[0:1, e:e + 1], min_val=e * CAP, max_val=e * CAP + T)
                sp.dma_start(sorted_rows[bass.ds(row, ROW_TILE), :].rearrange("(r p) d -> p r d", p=P),
                             zeros[:, :].unsqueeze(1).to_broadcast([P, ROW_TILE // P, D])).then_inc(tail_stored, 16)
            wait_apart(sp, table_done, 1, apart)
            sp.dma_start(table.rearrange("(a k) n -> a k n", a=1), table_i[0:1, :, :]).then_inc(table_stored, 16)
            sp.dma_start(pos_v, pos_out[:, :]).then_inc(table_stored, 16)
            wait_apart(sp, table_stored, 32, apart)
            wait_apart(sp, tail_stored, 16 * (E + 1), apart)
            for s in range(2):
                wait_apart(sp, res_stored[s], 16 * ALL // 2, apart)
                wait_apart(sp, place_stored[s], 16 * ALL // 2, apart)

        @block.gpsimd
        def _(pool):
            nc.gpsimd.memset(zeros[:, :], 0.0).then_inc(consts, 1)
            nc.gpsimd.memset(ident[:, :], 0.0)
            nc.gpsimd.memset(ones[:, :], 1.0)
            nc.gpsimd.memset(half[:, :], -0.5)
            nc.gpsimd.memset(ones_e[:, :], 1.0)
            exact = dict(allow_small_or_imprecise_dtypes=True)
            nc.gpsimd.iota(iota_e[:, :], [[1, E]], base=0, channel_multiplier=0, **exact)
            nc.gpsimd.iota(iota_tile[:, :], [[1, N_TILE]], base=0, channel_multiplier=0, **exact)
            nc.gpsimd.iota(region[:, :], [[CAP, E]], base=0, channel_multiplier=0, **exact).then_inc(consts, 1)
            wait_apart(pool, consts, 2, apart)
            nc.gpsimd.affine_select(out=ident[:, :], in_=ident[:, :], compare_op=ALU.not_equal, fill=1.0,
                                    base=0, pattern=[[-1, P]], channel_multiplier=1)
            nc.gpsimd.affine_select(out=before[:, :], in_=ones[:, :], compare_op=ALU.is_gt, fill=0.0,
                                    base=0, pattern=[[1, P]], channel_multiplier=-1).then_inc(consts, 1)

            def inverse_rms(n):
                wait_apart(pool, ss_done, n + 1, apart)
                nc.gpsimd.tensor_scalar(rrms[:, :], ss[:, :], 1.0 / D, EPS_RMS, ALU.mult, ALU.add).then_inc(rms_steps, 1)
                wait_apart(pool, rms_steps, 2 * n + 1, apart)
                nc.gpsimd.tensor_tensor(rrms[:, :], rrms[:, :], half[:, :], ALU.pow).then_inc(rms_steps, 1)

            inverse_rms(0)
            inverse_rms(1)

            def body(b, c, n, ahead):
                if ahead >= 2:
                    inverse_rms(n + 2)
                wait_apart(pool, pos_done, n + 1, apart)
                for t in range(TT):
                    for k in range(2):
                        nc.gpsimd.indirect_dma_start(
                            sorted_rows, bass.IndirectOffsetOnAxis(pos[:, c, t, k:k + 1], 0), th[:, c, t, :], None
                        ).then_inc(scattered[c], 16)
            chunks(pool, body)
            for c in range(NC):
                wait_apart(pool, scattered[c], 16 * 2 * TT * B, apart)

        @block.vector
        def _(dve):
            dve.wait_ge(consts, 3)
            nc.vector.tensor_copy(base[:, :], region[:, :]).then_inc(chain, 1)
            dve.wait_ge(chain, 1)
            dve.wait_ge(small_loaded, 32)
            LINKS = 10

            def add_attention(b, c, n):
                dve.wait_ge(loaded[c], N_LOADED * (b + 1))
                dve.wait_ge(res_done, n)
                dve.wait_ge(th_done, n)
                for i in range(2):
                    dve.wait_ge(mla_done, 2 * n + i + 1)
                    nc.vector.tensor_tensor(x2[:, 2 * i:2 * i + 2, :], mla_ps[i][:, :].rearrange("p (t d) -> p t d", d=D),
                                            xn[:, c, 2 * i:2 * i + 2, :], ALU.add).then_inc(x2_done, 1)

            def scale_rms(b, c, n):
                dve.wait_ge(rms_steps, 2 * n + 2)
                dve.wait_ge(scattered[c], 16 * 2 * TT * b)
                for t in range(TT):
                    last = nc.vector.scalar_tensor_tensor(th[:, c, t, :], x2[:, t, :], rrms[:, t:t + 1], g2[:, :],
                                                          ALU.mult, ALU.mult)
                last.then_inc(th_done, 1)

            def add_x(b, c, n):
                s = c % 2
                dve.wait_ge(res_stored[s], 16 * uses(b, c))
                dve.wait_ge(x2_done, 2 * n + 2)
                nc.vector.tensor_tensor(res[:, s, :, :], x[:, c, :, :], x2[:, :, :], ALU.add).then_inc(res_done, 1)

            for c in range(2):
                add_attention(0, c, c)
                add_x(0, c, c)
                scale_rms(0, c, c)

            def body(b, c, n, ahead):
                s = c % 2
                links = [0]

                def link(ins):
                    links[0] += 1
                    ins.then_inc(chain, 1)
                    wait_apart(dve, chain, 1 + LINKS * n + links[0], apart)

                dve.wait_ge(logit_done, n + 1)
                link(nc.vector.tensor_copy(logits[:, :, :], logit_ps))
                for t in range(TT):
                    last = nc.vector.max(top[:, t, :], logits[:, t, :])
                link(last)
                for t in range(TT):
                    last = nc.vector.max_index(top_i[:, t, :], top[:, t, :], logits[:, t, :])
                link(last)
                nc.vector.tensor_tensor(diff[:, :], top[:, :, 1], top[:, :, 0], ALU.subtract).then_inc(diff_done, 1)
                link(nc.vector.tensor_copy(top_f[:, :, :], top_i[:, :, 0:2]))
                link(nc.vector.tensor_tensor(chosen[:, :, :, :].rearrange("p t k e -> p (t k) e"),
                                             iota_e[:, :].unsqueeze(1).to_broadcast([P, TT * 2, E]),
                                             top_f[:, :, :].rearrange("p t k -> p (t k)").unsqueeze(2)
                                             .to_broadcast([P, TT * 2, E]), ALU.is_equal))
                nc.vector.tensor_tensor(either[:, :, :], chosen[:, :, 0, :], chosen[:, :, 1, :], ALU.add
                                        ).then_inc(either_done, 1)
                if ahead >= 2:
                    add_attention(*after(b, c + 2), n + 2)
                dve.wait_ge(ediff_done, n + 1)
                link(nc.vector.tensor_scalar(denom[:, :], ediff[:, :], 1.0, None, ALU.add))
                dve.wait_ge(place_stored[s], 16 * uses(b, c))
                link(nc.vector.reciprocal(gates[:, s, :, 0], denom[:, :]))
                nc.vector.tensor_tensor(gates[:, s, :, 1], ediff[:, :], gates[:, s, :, 0], ALU.mult).then_inc(gates_done, 1)
                dve.wait_ge(rank_done, n + 1)
                dve.wait_ge(place_done, n)
                link(nc.vector.tensor_tensor(place[:, :, :], rank_ps, base[:, :].unsqueeze(1).to_broadcast([P, TT, E]),
                                             ALU.add))
                nc.vector.tensor_tensor(base[:, :], total_ps, base[:, :], ALU.add).then_inc(place_done, 1)
                for k in range(2):
                    last = nc.vector.tensor_tensor(picked[:, :, k, :], chosen[:, :, k, :], place[:, :, :], ALU.mult)
                link(last)
                link(nc.vector.tensor_reduce(pos_f[:, :, :], picked[:, :, :, :], AX_X, ALU.add))
                nc.vector.tensor_copy(pos_all[:, bass.ds(n * TT * 2, TT * 2)], pos_f[:, :, :].rearrange("p t k -> p (t k)"))
                dve.wait_ge(scattered[c], 16 * 2 * TT * b)
                nc.vector.tensor_copy(pos[:, c, :, :], pos_f[:, :, :]).then_inc(pos_done, 1)
                assert links[0] == LINKS
                if ahead >= 2:
                    add_x(*after(b, c + 2), n + 2)
                    scale_rms(*after(b, c + 2), n + 2)
            chunks(dve, body)

            links = [0]

            def link(ins):
                links[0] += 1
                ins.then_inc(chain, 1)
                dve.wait_ge(chain, 1 + LINKS * ALL + links[0])

            dve.wait_ge(place_done, ALL)
            nc.vector.tensor_copy(tail[:, :], base[:, :]).then_inc(tail_done, 1)
            link(nc.vector.tensor_tensor(count[:, :], base[:, :], region[:, :], ALU.subtract))
            link(nc.vector.tensor_scalar(count_i[:, :], count[:, :], float(ROW_TILE - 1), None, ALU.add))
            link(nc.vector.tensor_scalar(count_i[:, :], count_i[:, :], ROW_TILE.bit_length() - 1, None,
                                         ALU.arith_shift_right))
            link(nc.vector.tensor_copy(tiles[:, :], count_i[:, :]))
            link(nc.vector.tensor_tensor_scan(ends[:, :], ones_e[:, :], tiles[:, :], 0.0, ALU.mult, ALU.add))
            link(nc.vector.tensor_scalar(jump[:, :], tiles[:, :], -float(ROW_TILE), float(CAP), ALU.mult, ALU.add))
            link(nc.vector.tensor_tensor(past[:, :, :], iota_tile[:, :].unsqueeze(2).to_broadcast([P, N_TILE, E]),
                                         ends[:, :].unsqueeze(1).to_broadcast([P, N_TILE, E]), ALU.is_ge))
            link(nc.vector.tensor_reduce(table_f[:, 0, :], past[:, :, :], AX_X, ALU.add))
            link(nc.vector.tensor_tensor(past_j[:, :, :], past[:, :, :],
                                         jump[:, :].unsqueeze(1).to_broadcast([P, N_TILE, E]), ALU.mult))
            link(nc.vector.tensor_reduce(table_f[:, 1, :], past_j[:, :, :], AX_X, ALU.add))
            link(nc.vector.scalar_tensor_tensor(table_f[:, 1, :], iota_tile[:, :], float(ROW_TILE), table_f[:, 1, :],
                                                ALU.mult, ALU.add))
            link(nc.vector.tensor_scalar(table_f[:, 0, :], table_f[:, 0, :], float(E - 1), None, ALU.min))
            nc.vector.tensor_copy(table_i[:, :, :], table_f[:, :, :])
            for e in range(1, E):
                link(nc.vector.tensor_scalar(behind[:, e % 2, :], pos_all[:, :], region[:, e:e + 1], jump[:, e - 1:e],
                                             ALU.is_ge, ALU.mult))
                link(nc.vector.tensor_tensor(pos_sum[:, :], pos_sum[:, :] if e > 1 else pos_all[:, :], behind[:, e % 2, :],
                                             ALU.subtract))
            nc.vector.tensor_copy(pos_out[:, :], pos_sum[:, :]).then_inc(table_done, 1)

        @block.scalar
        def _(act):
            def squares(n):
                act.wait_ge(rms_steps, 2 * n)
                act.wait_ge(x2_done, 2 * n + 2)
                for t in range(TT):
                    last = nc.scalar.activation(sq[:, t, :], x2[:, t, :], ACT.Square, accum_out=ss[:, t:t + 1])
                last.then_inc(ss_done, 1)

            def copy_tT(n):
                for k in range(KD):
                    act.wait_ge(tT_done, KD * n + k + 1)
                    act.wait_ge(logit_done, n)
                    nc.scalar.copy(tT[:, k, :], tT_ps[k][:, :]).then_inc(tT_copied, 1)

            squares(0)
            copy_tT(0)
            squares(1)

            def body(b, c, n, ahead):
                act.wait_ge(diff_done, n + 1)
                nc.scalar.activation(ediff[:, :], diff[:, :], ACT.Exp).then_inc(ediff_done, 1)
                if ahead >= 1:
                    copy_tT(n + 1)
                if ahead >= 2:
                    squares(n + 2)
            chunks(act, body)

        @block.tensor
        def _(pe):
            pe.wait_ge(consts, 3)

            def project(b, c, n):
                pe.wait_ge(loaded[c], N_LOADED * (b + 1))
                pe.wait_ge(x2_done, 2 * n)
                for i in range(2):
                    for t in range(2):
                        tok = (2 * i + t) * P
                        for k in range(KD):
                            last = nc.tensor.matmul(mla_ps[i][:, t * D:(t + 1) * D], oT[:, c, k, tok:tok + P], wo[:, k, :],
                                                    start=k == 0, stop=k == KD - 1)
                    last.then_inc(mla_done, 1)

            def transpose_th(c, n):
                pe.wait_ge(th_done, n + 1)
                pe.wait_ge(tT_copied, KD * n)
                for k in range(KD):
                    for t in range(TT):
                        last = nc.tensor.transpose(tT_ps[k][:, t * P:(t + 1) * P], th[:, c, t, k * P:(k + 1) * P], ident[:, :])
                    last.then_inc(tT_done, 1)

            def logits_of(n):
                pe.wait_ge(tT_copied, KD * n + KD)
                pe.wait_ge(either_done, n)
                for t in range(TT):
                    for k in range(KD):
                        last = nc.tensor.matmul(logit_ps[:, t, :], tT[:, k, t * P:(t + 1) * P], gate_w[:, k, :],
                                                start=k == 0, stop=k == KD - 1)
                last.then_inc(logit_done, 1)

            def ranks(n):
                pe.wait_ge(either_done, n + 1)
                pe.wait_ge(place_done, n)
                for t in range(TT):
                    nc.tensor.matmul(rank_ps[:, t, :], before[:, :], either[:, t, :], start=True, stop=t == 0)
                    for t0 in range(t):
                        nc.tensor.matmul(rank_ps[:, t, :], ones[:, :], either[:, t0, :], start=False, stop=t0 == t - 1)
                for t in range(TT):
                    last = nc.tensor.matmul(total_ps, ones[:, :], either[:, t, :], start=t == 0, stop=t == TT - 1)
                last.then_inc(rank_done, 1)

            pe.wait_ge(w_loaded, 16)
            for n in range(2):
                project(0, n, n)
            pe.wait_ge(small_loaded, 32)
            transpose_th(0, 0)

            def body(b, c, n, ahead):
                logits_of(n)
                if ahead >= 2:
                    project(*after(b, c + 2), n + 2)
                if ahead >= 1:
                    transpose_th((c + 1) % NC, n + 1)
                ranks(n)
            chunks(pe, body)


def phase4_experts(nc, apart, head_qkv, w, sorted_rows, expert_rows, attn_rows, table):
    NB = T // P - HEAD_BLOCKS
    QUADS, ALL_QUADS = NB // 2, N_TILE // 4
    RT = ROW_TILE // P
    FB = F // P
    HH = H * H
    with ExitStack() as ctx:
        sb = lambda name, shape, dt=F32: ctx.enter_context(nc.sbuf_tensor(name, shape, dt))
        sem = lambda name: ctx.enter_context(nc.semaphore(name))
        bank = lambda name: ctx.enter_context(nc.psum_tensor(name, [P, CT], F32))

        ident = sb("p4_ident", [P, P])
        table_sb = sb("p4_table", [1, 2, N_TILE], mybir.dt.int32)
        w1 = sb("p4_w1", [P, 2, KD, F])
        w2 = sb("p4_w2", [P, 2, FB, D])
        rows = sb("p4_rows", [P, 2, RT, D])
        rT = sb("p4_rT", [P, KD, ROW_TILE])
        hid = sb("p4_hid", [P, FB, ROW_TILE])
        y = sb("p4_y", [P, 2, RT, D])
        qkv = sb("p4_qkv", [P, 2, 3, D])
        prod = sb("p4_prod", [P, H, H, DH])
        s = sb("p4_s", [P, H, H])
        smax = sb("p4_smax", [P, H])
        sm = sb("p4_sm", [P, H, H])
        pr = sb("p4_pr", [P, 2, H, H])
        psum = sb("p4_psum", [P, H])
        inv = sb("p4_inv", [P, 2, H])
        pv = sb("p4_pv", [P, 2, H, DH, H])
        oh = sb("p4_oh", [P, 2, H, DH])

        rT_ps = bank("p4_rT_ps")
        hid_ps = [bank(f"p4_hid{i}_ps") for i in range(2)]
        y_ps = [bank(f"p4_y{t}_ps") for t in range(RT)]
        q_ps = [bank(f"p4_q{i}_ps") for i in range(2)]

        w_loaded = sem("p4_w_loaded")
        consts = sem("p4_consts")
        w1_loaded = [sem(f"p4_w1_loaded{i}") for i in range(2)]
        rows_loaded = [sem(f"p4_rows_loaded{i}") for i in range(2)]
        rT_done = sem("p4_rT_done")
        rT_copied = sem("p4_rT_copied")
        hid_done = sem("p4_hid_done")
        silu_done = sem("p4_silu_done")
        y_done = sem("p4_y_done")
        y_copied = sem("p4_y_copied")
        y_stored = [sem(f"p4_y_stored{i}") for i in range(2)]
        qkv_loaded = [sem(f"p4_qkv_loaded{i}") for i in range(2)]
        q_copied = sem("p4_q_copied")
        prod_done = sem("p4_prod_done")
        s_done = sem("p4_s_done")
        smax_done = sem("p4_smax_done")
        sm_done = sem("p4_sm_done")
        exp_done = sem("p4_exp_done")
        psum_done = sem("p4_psum_done")
        inv_done = sem("p4_inv_done")
        pv_done = sem("p4_pv_done")
        pv_added = sem("p4_pv_added")
        oh_done = sem("p4_oh_done")
        oh_stored = [sem(f"p4_oh_stored{i}") for i in range(2)]
        block = ctx.enter_context(nc.Block())

        def quads(eng, body):
            body(0, True, True, False)
            with eng.Fori(1, QUADS) as g:
                body(g, True, False, False)
            for g in range(QUADS, ALL_QUADS):
                body(g, False, g == QUADS, g == ALL_QUADS - 1)

        @block.sync
        def _(sp):
            sp.dma_start(table_sb[:, :, :], table.unsqueeze(0)).then_inc(w_loaded, 16)

            def load_block(m, u):
                wait_apart(sp, prod_done, m + 1, apart)
                wait_apart(sp, pv_done, m + 1, apart)
                sp.dma_start(qkv[:, u, :, :].rearrange("p i d -> p (i d)"),
                             head_qkv[bass.ds(HEAD_BLOCKS + m, 1), :, :].rearrange("a p d -> p (a d)")).then_inc(qkv_loaded[u], 16)

            load_block(0, 0)
            load_block(1, 1)
            wait_apart(sp, w_loaded, 16, apart)

            def body(g, has_blocks, first, last):
                for i in range(4):
                    n, u = 4 * g + i, i % 2
                    e = sp.value_load(table_sb[0:1, 0, bass.ds(n, 1)], min_val=0, max_val=E - 1)
                    row = sp.value_load(table_sb[0:1, 1, bass.ds(n, 1)], min_val=0, max_val=SORTED - ROW_TILE)
                    wait_apart(sp, rT_done, n + 1, apart)
                    sp.dma_start(rows[:, u, :, :], sorted_rows[bass.ds(row, ROW_TILE), :].rearrange("(t p) d -> p t d", p=P)
                                 ).then_inc(rows_loaded[u], 16)
                    wait_apart(sp, y_done, n + 1, apart)
                    sp.dma_start(w1[:, u, :, :], w["ffn_w1"][bass.ds(e, 1), :, :].rearrange("a (k p) f -> p (a k) f", p=P)
                                 ).then_inc(w1_loaded[u], 16)
                    sp.dma_start(w2[:, u, :, :], w["ffn_w2"][bass.ds(e, 1), :, :].rearrange("a (k p) f -> p (a k) f", p=P)
                                 ).then_inc(w1_loaded[u], 16)
                    if has_blocks and i % 2 and not first:
                        load_block(2 * g + i // 2, i // 2)
            quads(sp, body)

        @block.gpsimd
        def _(pool):
            nc.gpsimd.memset(ident[:, :], 0.0).then_inc(consts, 1)
            wait_apart(pool, consts, 1, apart)
            nc.gpsimd.affine_select(out=ident[:, :], in_=ident[:, :], compare_op=ALU.not_equal, fill=1.0,
                                    base=0, pattern=[[-1, P]], channel_multiplier=1).then_inc(consts, 1)

            def weigh_values(n, u):
                wait_apart(pool, exp_done, n + 1, apart)
                wait_apart(pool, pv_added, n + 1, apart)
                nc.gpsimd.tensor_tensor(
                    pv[:, u, :, :, :],
                    pr[:, u, :, :].unsqueeze(2).to_broadcast([P, H, DH, H]),
                    qkv[:, u, 2, :].rearrange("p (j d) -> p d j", d=DH).unsqueeze(1).to_broadcast([P, H, DH, H]),
                    ALU.mult).then_inc(pv_done, 1)

            def store(n, u):
                wait_apart(pool, oh_done, n + 1, apart)
                nc.gpsimd.dma_start(attn_rows[bass.ds(HEAD_BLOCKS + n, 1), :, :].rearrange("a p d -> p (a d)"),
                                    oh[:, u, :, :].rearrange("p i d -> p (i d)")).then_inc(oh_stored[u], 16)

            weigh_values(0, 0)
            weigh_values(1, 1)
            with pool.Fori(1, NB // 2) as j:
                for u in range(2):
                    store(2 * j + u - 2, u)
                    weigh_values(2 * j + u, u)
            store(NB - 2, 0)
            store(NB - 1, 1)
            for u in range(2):
                wait_apart(pool, oh_stored[u], 16 * NB // 2, apart)

        @block.vector
        def _(dve):
            dve.sem_inc(rT_done, 2)
            dve.sem_inc(y_done, 2)
            dve.sem_inc(pv_added, 2)
            dve.sem_inc(prod_done, 2)
            dve.sem_inc(psum_done, 2)
            dve.sem_inc(pv_done, 2)
            def score(n, u):
                dve.wait_ge(q_copied, n + 1)
                q = q_ps[u][:, 0:D].rearrange("p (i d) -> p i d", d=DH)
                k = qkv[:, u, 1, :].rearrange("p (j d) -> p j d", d=DH)
                nc.vector.tensor_tensor(prod[:, :, :, :], q.unsqueeze(2).to_broadcast([P, H, H, DH]),
                                        k.unsqueeze(1).to_broadcast([P, H, H, DH]), ALU.mult).then_inc(prod_done, 1)
                dve.wait_ge(prod_done, 2 + n + 1)
                nc.vector.tensor_reduce(s[:, :, :], prod[:, :, :, :], AX_X, ALU.add).then_inc(s_done, 1)
                dve.wait_ge(s_done, n + 1)
                nc.vector.tensor_reduce(smax[:, :], s[:, :, :], AX_X, ALU.max).then_inc(smax_done, 1)
                dve.wait_ge(smax_done, n + 1)
                dve.wait_ge(exp_done, n)
                nc.vector.tensor_tensor(sm[:, :, :], s[:, :, :], smax[:, :].unsqueeze(2).to_broadcast([P, H, H]),
                                        ALU.subtract).then_inc(sm_done, 1)

            def row_sums(n, u):
                dve.wait_ge(exp_done, n + 1)
                nc.vector.tensor_reduce(psum[:, :], pr[:, u, :, :], AX_X, ALU.add).then_inc(psum_done, 1)
                dve.wait_ge(psum_done, 2 + n + 1)
                nc.vector.reciprocal(inv[:, u, :], psum[:, :]).then_inc(inv_done, 1)

            def finish(n, u, j):
                dve.wait_ge(pv_done, 2 + n + 1)
                dve.wait_ge(oh_stored[u], 16 * j)
                nc.vector.tensor_reduce(oh[:, u, :, :], pv[:, u, :, :, :], AX_X, ALU.add).then_inc(pv_added, 1)
                dve.wait_ge(pv_added, 2 + n + 1)
                dve.wait_ge(inv_done, n + 1)
                nc.vector.tensor_tensor(oh[:, u, :, :], oh[:, u, :, :],
                                        inv[:, u, :].unsqueeze(2).to_broadcast([P, H, DH]), ALU.mult).then_inc(oh_done, 1)

            score(0, 0)
            score(1, 1)
            row_sums(0, 0)
            with dve.Fori(1, NB // 2) as j:
                for u in range(2):
                    score(2 * j + u, u)
                    row_sums(2 * j + u - 1, 1 - u)
                    finish(2 * j + u - 2, u, j - 1)
            row_sums(NB - 1, 1)
            finish(NB - 2, 0, NB // 2 - 1)
            finish(NB - 1, 1, NB // 2 - 1)

        @block.scalar
        def _(act):
            act.sem_inc(silu_done, 2)

            def copy_rows(n):
                act.wait_ge(rT_done, 2 + n + 1)
                act.wait_ge(hid_done, 2 * n)
                nc.scalar.copy(rT[:, :, :].rearrange("p k t -> p (k t)"), rT_ps[:, :]).then_inc(rT_copied, 1)

            def copy_q(m, u, loads):
                act.wait_ge(qkv_loaded[u], 16 * loads)
                act.wait_ge(prod_done, m + 1)
                nc.scalar.copy(q_ps[u][:, 0:D], qkv[:, u, 0, :]).then_inc(q_copied, 1)

            def probabilities(n, u):
                act.wait_ge(sm_done, n + 1)
                act.wait_ge(psum_done, n + 1)
                act.wait_ge(pv_done, n + 1)
                nc.scalar.activation(pr[:, u, :, :], sm[:, :, :], ACT.Exp).then_inc(exp_done, 1)

            copy_q(0, 0, 1)
            copy_q(1, 1, 1)
            copy_rows(0)

            def body(g, has_blocks, first, last):
                for i in range(4):
                    n, u = 4 * g + i, i % 2
                    for k in range(2):
                        act.wait_ge(hid_done, 2 * n + k + 1)
                        act.wait_ge(y_done, 2 + n)
                        nc.scalar.activation(hid[:, 2 * k:2 * k + 2, :].rearrange("p k t -> p (k t)"), hid_ps[k][:, :],
                                             ACT.Silu).then_inc(silu_done, 1)
                    if not (last and i == 3):
                        copy_rows(n + 1)
                    m = 2 * g + i // 2
                    if i % 2 == 0 and not (first and i == 0) and has_blocks:
                        probabilities(m - 1, 1 - i // 2)
                        if not first:
                            copy_q(m, i // 2, g + 1)
                    if not has_blocks and first and i == 0:
                        probabilities(NB - 1, 1)
                    act.wait_ge(y_done, 2 + n + 1)
                    act.wait_ge(y_stored[u], 16 * (2 * g + i // 2))
                    for t in range(RT):
                        last_copy = nc.scalar.copy(y[:, u, t, :], y_ps[t][:, 0:D])
                    last_copy.then_inc(y_copied, 1)
                    act.wait_ge(y_copied, n + 1)
                    act.dma_start(expert_rows[bass.ds(n, 1), :, :].rearrange("a (t p) d -> p (a t) d", p=P),
                                  y[:, u, :, :]).then_inc(y_stored[u], 16)
            quads(act, body)
            for u in range(2):
                act.wait_ge(y_stored[u], 16 * N_TILE // 2)

        @block.tensor
        def _(pe):
            pe.wait_ge(consts, 2)

            def transpose_rows(n, u, j):
                pe.wait_ge(rows_loaded[u], 16 * (j + 1))
                pe.wait_ge(rT_copied, n)
                for k in range(KD):
                    for t in range(RT):
                        last = nc.tensor.transpose(rT_ps[:, k * ROW_TILE + t * P:k * ROW_TILE + (t + 1) * P],
                                                   rows[:, u, t, k * P:(k + 1) * P], ident[:, :])
                last.then_inc(rT_done, 1)

            def hidden(n, u, j):
                pe.wait_ge(rT_copied, n + 1)
                pe.wait_ge(w1_loaded[u], 32 * (j + 1))
                for i in range(2):
                    pe.wait_ge(silu_done, 2 * n + i + 1)
                    for f in range(2):
                        for k in range(KD):
                            last = nc.tensor.matmul(hid_ps[i][:, f * ROW_TILE:(f + 1) * ROW_TILE],
                                                    w1[:, u, k, (2 * i + f) * P:(2 * i + f + 1) * P], rT[:, k, :],
                                                    start=k == 0, stop=k == KD - 1)
                    last.then_inc(hid_done, 1)

            def second(n, u):
                pe.wait_ge(y_copied, n)
                for k in range(2):
                    pe.wait_ge(silu_done, 2 + 2 * n + k + 1)
                    for t in range(RT):
                        for f in range(k * FB // 2, (k + 1) * FB // 2):
                            last = nc.tensor.matmul(y_ps[t][:, 0:D], hid[:, f, t * P:(t + 1) * P], w2[:, u, f, :],
                                                    start=f == 0, stop=f == FB - 1)
                last.then_inc(y_done, 1)

            transpose_rows(0, 0, 0)

            def body(g, has_blocks, first, last):
                for i in range(4):
                    n, u = 4 * g + i, i % 2
                    hidden(n, u, 2 * g + i // 2)
                    if not (last and i == 3):
                        transpose_rows(n + 1, 1 - u, 2 * g + (i + 1) // 2)
                    second(n, u)
            quads(pe, body)


def phase5_combine(nc, apart, res_v, attn_v, pos_v, gates_v, expert_rows, out_v):
    with ExitStack() as ctx:
        sb = lambda name, shape, dt=F32: ctx.enter_context(nc.sbuf_tensor(name, shape, dt))
        sem = lambda name: ctx.enter_context(nc.semaphore(name))
        res = sb("p5_res", [P, NC, TT, D])
        attn = sb("p5_attn", [P, NC, TT, D])
        pos = sb("p5_pos", [P, NC, TT, 2], U32)
        gates = sb("p5_gates", [P, NC, TT, 2])
        ye = sb("p5_ye", [P, NC, TT, 2, D])
        acc = sb("p5_acc", [P, NC, TT, D])
        loaded = [sem(f"p5_loaded{i}") for i in range(NC)]
        pos_loaded = [sem(f"p5_pos_loaded{i}") for i in range(NC)]
        gathered = [sem(f"p5_gathered{i}") for i in range(NC)]
        steps = sem("p5_steps")
        out_done = sem("p5_out_done")
        stored = [sem(f"p5_stored{i}") for i in range(NC)]
        block = ctx.enter_context(nc.Block())

        def chunks(eng, body):
            with eng.Fori(0, B) as b:
                for c in range(NC):
                    body(b, c, NC * b + c)

        @block.sync
        def _(sp):
            def body(b, c, n):
                wait_apart(sp, out_done, n + 1, apart)
                sp.dma_start(pos[:, c, :, :], pos_v[b, c]).then_inc(pos_loaded[c], 16)
                sp.dma_start(res[:, c, :, :], res_v[b, c]).then_inc(loaded[c], 16)
                sp.dma_start(attn[:, c, :, :], attn_v[b, c]).then_inc(loaded[c], 16)
                sp.dma_start(gates[:, c, :, :], gates_v[b, c]).then_inc(loaded[c], 16)
            chunks(sp, body)

        @block.gpsimd
        def _(pool):
            def body(b, c, n):
                wait_apart(pool, pos_loaded[c], 16 * (b + 1), apart)
                wait_apart(pool, out_done, n + 1, apart)
                for t in range(TT):
                    for k in range(2):
                        nc.gpsimd.indirect_dma_start(ye[:, c, t, k, :], None, expert_rows,
                                                     bass.IndirectOffsetOnAxis(pos[:, c, t, k:k + 1], 0)
                                                     ).then_inc(gathered[c], 16)
            chunks(pool, body)

        @block.vector
        def _(dve):
            dve.sem_inc(out_done, NC)

            def body(b, c, n):
                dve.wait_ge(loaded[c], 48 * (b + 1))
                dve.wait_ge(stored[c], 16 * b)
                nc.vector.tensor_tensor(acc[:, c, :, :], res[:, c, :, :], attn[:, c, :, :], ALU.add).then_inc(steps, 1)
                dve.wait_ge(gathered[c], 16 * 2 * TT * (b + 1))
                dve.wait_ge(steps, 2 * n + 1)
                for t in range(TT):
                    last = nc.vector.scalar_tensor_tensor(acc[:, c, t, :], ye[:, c, t, 0, :], gates[:, c, t, 0:1],
                                                          acc[:, c, t, :], ALU.mult, ALU.add)
                last.then_inc(steps, 1)
                dve.wait_ge(steps, 2 * n + 2)
                for t in range(TT):
                    last = nc.vector.scalar_tensor_tensor(acc[:, c, t, :], ye[:, c, t, 1, :], gates[:, c, t, 1:2],
                                                          acc[:, c, t, :], ALU.mult, ALU.add)
                last.then_inc(out_done, 1)
            chunks(dve, body)

        @block.scalar
        def _(act):
            def body(b, c, n):
                act.wait_ge(out_done, NC + n + 1)
                act.dma_start(out_v[b, c], acc[:, c, :, :]).then_inc(stored[c], 16)
            chunks(act, body)
            for c in range(NC):
                act.wait_ge(stored[c], 16 * B)


INPUTS = ["attn_x", "attn_Wq", "attn_bq", "attn_Wk", "attn_bk", "attn_Wv", "attn_bv", "ffn_g1", "ffn_Wq", "ffn_Wdkv",
          "ffn_Wuk", "ffn_Wuv", "ffn_Wo", "ffn_g2", "ffn_gate_w", "ffn_w1", "ffn_w2"]


def build(nc, w, out):
    dram = lambda name, shape, dt=F32: nc.dram_tensor(name, shape, dt, kind="Internal").ap()
    xn = dram("xn", [T, D])
    qk = dram("qk_parts", [2, 3, B, D, S], BF16)
    v = dram("v_padded", [B * NG, S, HG * VW])
    o = dram("o_heads", [B * NG, HG * DH, S])
    res = dram("res", [T, D])
    pos = dram("pos", [P, B * NC * TT * 2], U32)
    gates = dram("gates", [B, NC, P, TT * 2])
    table = dram("tile_table", [2, N_TILE], mybir.dt.int32)
    sorted_rows = dram("sorted_rows", [SORTED, D])
    expert_rows = dram("expert_rows", [N_TILE * ROW_TILE, D])
    attn = dram("attn_rows", [T, D])
    heads = dram("head_qkv", [T, 3 * D])
    by_chunk = lambda a: a.rearrange("(b c t p) d -> b c p t d", b=B, c=NC, p=P)
    by_block = lambda a: a.rearrange("(n p) d -> n p d", p=P)
    x = w["attn_x"].rearrange("b s d -> (b s) d")
    pairs = lambda a: a.rearrange("b c p (t k) -> b c p t k", k=2)

    o_v = o.rearrange("(b k g) d (c t) -> b c (g d) k t", b=B, k=KD, c=NC)
    qk_heads = qk.rearrange("a p b (h d) t -> a p (b h) d t", d=DH)
    with ExitStack() as all_phases:
        apart = all_phases.enter_context(nc.semaphore("apart"))
        with ExitStack() as ctx:
            units = [tuple(ctx.enter_context(nc.sbuf_tensor(f"unit{u}_{name}", shape, dt)) for name, shape, dt in
                           (("q6", [ROWS, HG, S], BF16), ("k6", [ROWS, HG, S], BF16), ("vg", [P, KT, HG * VW], F32)))
                     for u in range(2)]
            phase1_project(nc, apart, by_chunk(x), w, by_chunk(xn), qk, v.rearrange("(b g) t v -> b g t v", b=B), by_chunk(heads),
                           qk_heads, v, units)
            phase2_attend(nc, apart, qk_heads, v, o, by_block(heads), by_block(attn), units)
        phase3_route(nc, apart, by_chunk(x), by_chunk(xn), o_v, w,
                     sorted_rows, by_chunk(res), pos, pairs(gates), table)
        phase4_experts(nc, apart, by_block(heads), w, sorted_rows, expert_rows.rearrange("(n r) d -> n r d", r=ROW_TILE),
                       by_block(attn), table)
        phase5_combine(nc, apart, by_chunk(res), by_chunk(attn),
                       pos.rearrange("p (b c t k) -> b c p t k", b=B, c=NC, k=2), pairs(gates), expert_rows, by_chunk(out))


def kernel(**inputs):
    import numpy as np
    import concourse.bacc as bacc
    from concourse.bass_utils import run_bass_kernel_spmd

    nc = bacc.Bacc("TRN2", target_bir_lowering=False, num_devices=1)
    arrays, w = {}, {}
    for name in INPUTS:
        a = np.ascontiguousarray(inputs[f"L0_{name}"])
        arrays[name] = a
        w[name] = nc.dram_tensor(name, list(a.shape), mybir.dt.from_np(a.dtype), kind="ExternalInput").ap()
    out = nc.dram_tensor("out", [T, D], F32, kind="ExternalOutput").ap()
    build(nc, w, out)
    r = run_bass_kernel_spmd(nc, [arrays], core_ids=[0])
    return r.results[0]["out"].reshape(B, S, D)
```
